# Optimizing a Trainium2 kernel written in Bass

```python
import numpy as np
import jax
import jax.numpy as jnp

def _softmax(x, axis=-1):
    return jax.nn.softmax(x, axis=axis)

def _gelu(x):
    return jax.nn.gelu(x, approximate=True)

def _silu(x):
    return jax.nn.silu(x)

def _sigmoid(x):
    return jax.nn.sigmoid(x)

def _layernorm(x, axis=-1, eps=1e-05):
    m = jnp.mean(x, axis=axis, keepdims=True)
    v = jnp.var(x, axis=axis, keepdims=True)
    return (x - m) / jnp.sqrt(v + eps)

def _scatter_add(tgt, idx, src, axis=0):
    return tgt.at[idx].add(src)

def _segment_sum(src, seg, n):
    return jax.ops.segment_sum(src, seg, n)
kernel_name = 'mk_xattn_ffn_d4_seqx_r8_750850'

def setup_inputs(seed: int=0):
    np.random.seed(seed)
    _w = jnp.asarray

    def _rec_inputs():
        import jax
        import jax.numpy as jnp
        _rk = jax.random.key(seed)
        x = -0.0002928 + 1 * jax.random.normal(jax.random.fold_in(_rk, 1), (16, 256, 128), jnp.float32)
        _lenS = 256 - jax.random.randint(jax.random.fold_in(_rk, 7), (16,), 0, max(1, 256 // 4) + 1, jnp.int32)
        _lenS2 = 64 - jax.random.randint(jax.random.fold_in(_rk, 8), (16,), 0, max(1, 64 // 4) + 1, jnp.int32)
        _ctx_1024P = jax.random.normal(jax.random.fold_in(_rk, 11), (16, 16, 128), jnp.float32)
        _ctx_1024c = jax.random.dirichlet(jax.random.fold_in(_rk, 511), 0.3 * jnp.ones((16,), jnp.float32), (16, 64))
        _ctx_1024t = jnp.einsum('bsk,bkd->bsd', _ctx_1024c, _ctx_1024P)
        _ctx_1024t = _ctx_1024t * jax.lax.rsqrt(jnp.mean(jnp.square(_ctx_1024t)) + 1e-12) * 0.953939
        ctx_1024 = -1.39393e-06 + 0.999914 * (_ctx_1024t + 0.3 * jax.random.normal(jax.random.fold_in(_rk, 611), (16, 64, 128), jnp.float32))
        _validS = jnp.arange(256)[None, :] < _lenS[:, None]
        _validS2 = jnp.arange(64)[None, :] < _lenS2[:, None]
        _causal = jnp.tril(jnp.ones((256, 256), dtype=bool))
        mask_BxSxS2_bf1 = jnp.ones((16, 256, 64), dtype=bool)
        mask_BxS2_bf1 = jnp.ones((16, 64), dtype=bool)
        return (x, ctx_1024, mask_BxSxS2_bf1, mask_BxS2_bf1)
    x, ctx_1024, mask_BxSxS2_bf1, mask_BxS2_bf1 = _rec_inputs()

    def _L0_xattn_setup():
        import jax, jax.numpy as jnp
        import numpy as np
        DIM = 128
        HEAD_DIM = 64
        NUM_HEADS = DIM // HEAD_DIM
        SCALE = HEAD_DIM ** (-0.5)
        key = jax.random.key(seed)
        k_x, k_ctx, k_wq, k_wkv, k_wo = jax.random.split(key, 5)
        B, N, M = (2, 256, 256)
        x = jax.random.normal(k_x, (B, N, DIM), dtype=jnp.float32)
        context = jax.random.normal(k_ctx, (B, M, DIM), dtype=jnp.float32)
        mask = jnp.ones((B, N, M), dtype=bool)
        s = DIM ** (-0.5)
        Wq = jax.random.normal(k_wq, (DIM, DIM), dtype=jnp.float32) * s
        Wkv = jax.random.normal(k_wkv, (DIM, 2 * DIM), dtype=jnp.float32) * s
        Wo = jax.random.normal(k_wo, (DIM, DIM), dtype=jnp.float32) * s
        return {'x': x, 'context': context, 'mask': mask, 'Wq': Wq, 'Wkv': Wkv, 'Wo': Wo}
    _L0_xattn_all = _L0_xattn_setup()
    _L0_xattn_in = {k: v for k, v in _L0_xattn_all.items() if k in ('Wq', 'Wkv', 'Wo')}
    del _L0_xattn_all

    def _L0_ffn_setup():
        import jax, jax.numpy as jnp
        import numpy as np
        BLOCK = 32
        W_BITS = 4
        ACT_BITS = 16

        def act_qdq(x):
            qmax = 2.0 ** (ACT_BITS - 1) - 1.0
            scale = jnp.maximum(jnp.max(jnp.abs(x)) / qmax, 1e-12)
            return jnp.clip(jnp.round(x / scale), -qmax - 1.0, qmax) * scale

        def fixed_qdq_u16(x):
            scale = 1.0 / 65536.0
            return jnp.clip(jnp.round(x / scale), 0.0, 65535.0) * scale

        def lpbq_dequant(w):
            O, I = w.shape
            qmax = 2.0 ** (W_BITS - 1) - 1.0
            wb = w.reshape(O, I // BLOCK, BLOCK)
            s = jnp.maximum(jnp.max(jnp.abs(wb), axis=-1, keepdims=True) / qmax, 1e-12)
            wq = jnp.clip(jnp.round(wb / s), -qmax - 1.0, qmax) * s
            return wq.reshape(O, I)
        key = jax.random.key(seed)
        k1, k2, k3, k4 = jax.random.split(key, 4)
        B, S, H, I = (2, 512, 128, 384)
        x = jax.random.normal(k1, (B, S, H), jnp.float32)
        w_gate = jax.random.normal(k2, (I, H), jnp.float32) * 0.02
        w_up = jax.random.normal(k3, (I, H), jnp.float32) * 0.02
        w_down = jax.random.normal(k4, (H, I), jnp.float32) * 0.02
        return {'x': x, 'w_gate': w_gate, 'w_up': w_up, 'w_down': w_down}
    _L0_ffn_all = _L0_ffn_setup()
    _L0_ffn_in = {k: v for k, v in _L0_ffn_all.items() if k in ('w_gate', 'w_up', 'w_down')}
    del _L0_ffn_all

    def _L1_xattn_setup():
        import jax, jax.numpy as jnp
        import numpy as np
        D_MODEL = 128
        NUM_HEADS = 16
        HEAD_DIM = D_MODEL // NUM_HEADS
        key = jax.random.key(seed)
        ks = jax.random.split(key, 10)
        B, SQ, SK = (2, 256, 256)
        scale = 1.0 / np.sqrt(D_MODEL)
        inp = {'x1': jax.random.normal(ks[0], (B, SQ, D_MODEL), jnp.float32), 'x2': jax.random.normal(ks[1], (B, SK, D_MODEL), jnp.float32), 'Wq': jax.random.normal(ks[2], (D_MODEL, D_MODEL), jnp.float32) * scale, 'bq': jnp.zeros((D_MODEL,), jnp.float32), 'Wk': jax.random.normal(ks[3], (D_MODEL, D_MODEL), jnp.float32) * scale, 'bk': jnp.zeros((D_MODEL,), jnp.float32), 'Wv': jax.random.normal(ks[4], (D_MODEL, D_MODEL), jnp.float32) * scale, 'bv': jnp.zeros((D_MODEL,), jnp.float32), 'Wo': jax.random.normal(ks[5], (D_MODEL, D_MODEL), jnp.float32) * scale, 'bo': jnp.zeros((D_MODEL,), jnp.float32)}
        return inp
    _L1_xattn_all = _L1_xattn_setup()
    _L1_xattn_in = {k: v for k, v in _L1_xattn_all.items() if k in ('Wq', 'bq', 'Wk', 'bk', 'Wv', 'bv', 'Wo', 'bo')}
    del _L1_xattn_all

    def _L1_ffn_setup():
        import jax, jax.numpy as jnp
        import numpy as np
        DMODEL = 128
        N_EXPERTS = 16
        EXPERT_SIZE = 32
        K = 4
        key = jax.random.key(seed)
        k1, k2, k3, k4 = jax.random.split(key, 4)
        std_sel = 1.0 / np.sqrt(DMODEL)
        std_val = 1.0 / np.sqrt(N_EXPERTS * EXPERT_SIZE)
        return {'x': jax.random.normal(k1, (4, 256, DMODEL), dtype=jnp.float32), 'expert_sel': jax.random.normal(k2, (N_EXPERTS, DMODEL), dtype=jnp.float32) * std_sel, 'keys': jax.random.normal(k3, (N_EXPERTS, DMODEL, EXPERT_SIZE), dtype=jnp.float32) * std_sel, 'values': jax.random.normal(k4, (N_EXPERTS, EXPERT_SIZE, DMODEL), dtype=jnp.float32) * std_val, 'route_scale': jnp.ones((1,), dtype=jnp.float32)}
    _L1_ffn_all = _L1_ffn_setup()
    _L1_ffn_in = {k: v for k, v in _L1_ffn_all.items() if k in ('expert_sel', 'keys', 'values', 'route_scale')}
    del _L1_ffn_all

    def _L2_xattn_setup():
        import jax, jax.numpy as jnp
        import numpy as np
        GAMMA = 10.0
        BASE = 10000.0
        SCALE = 64 ** (-0.5)
        NUM_HEADS = 16

        def _larope(t, seq_len):
            B, H, L, D = t.shape
            inv_freq = 1.0 / BASE ** (jnp.arange(0, D, 2, dtype=jnp.float32) / D)
            pos = GAMMA * (jnp.arange(L, dtype=jnp.float32) / float(seq_len))
            ang = pos[:, None] * inv_freq
            cos = jnp.cos(ang)
            sin = jnp.sin(ang)
            te, to = (t[..., 0::2], t[..., 1::2])
            re = te * cos - to * sin
            ro = te * sin + to * cos
            return jnp.stack([re, ro], axis=-1).reshape(t.shape)
        key = jax.random.key(seed)
        ks = jax.random.split(key, 8)
        B, Lq, Lk, D = (8, 256, 64, 128)
        s = D ** (-0.5)
        return {'x': jax.random.normal(ks[0], (B, Lq, D), jnp.float32), 'context': jax.random.normal(ks[1], (B, Lk, D), jnp.float32), 'context_mask': jnp.ones((B, Lk), dtype=bool), 'Wq': jax.random.normal(ks[2], (D, D), jnp.float32) * s, 'bq': jnp.zeros((D,), jnp.float32), 'Wkv': jax.random.normal(ks[3], (D, 2 * D), jnp.float32) * s, 'bkv': jnp.zeros((2 * D,), jnp.float32), 'Wo': jax.random.normal(ks[4], (D, D), jnp.float32) * s, 'bo': jnp.zeros((D,), jnp.float32)}
    _L2_xattn_all = _L2_xattn_setup()
    _L2_xattn_in = {k: v for k, v in _L2_xattn_all.items() if k in ('Wq', 'bq', 'Wkv', 'bkv', 'Wo', 'bo')}
    del _L2_xattn_all

    def _L2_ffn_setup():
        import jax, jax.numpy as jnp
        import numpy as np
        B, T, D = (2, 256, 128)
        DCD = 512
        RET = 128
        NEXP = 512
        NKEYS = 64
        H = 4
        KPH = 8
        key = jax.random.key(seed)
        ks = jax.random.split(key, 10)
        s = lambda k, shape, scale: jax.random.normal(k, shape, jnp.float32) * scale
        return {'hidden_states': jax.random.normal(ks[0], (B, T, D), jnp.float32), 'Wg': s(ks[1], (D, DCD), 0.02), 'bg': jnp.zeros((DCD,), jnp.float32), 'Wu': s(ks[2], (D, DCD), 0.02), 'bu': jnp.zeros((DCD,), jnp.float32), 'Wd': s(ks[3], (DCD, D), 0.02), 'bd': jnp.zeros((D,), jnp.float32), 'Wq': s(ks[4], (D, RET * H), 0.02), 'keys': s(ks[5], (H, NKEYS, 2, RET // 2), 0.02), 'down_embed': s(ks[6], (NEXP, D), 0.02), 'up_embed': s(ks[7], (NEXP, D), 0.02)}
    _L2_ffn_all = _L2_ffn_setup()
    _L2_ffn_in = {k: v for k, v in _L2_ffn_all.items() if k in ('Wg', 'bg', 'Wu', 'bu', 'Wd', 'bd', 'Wq', 'keys', 'down_embed', 'up_embed')}
    del _L2_ffn_all

    def _L3_xattn_setup():
        import jax, jax.numpy as jnp
        import numpy as np
        D_MODEL = 128
        NUM_HEADS = 16
        DEPTH = D_MODEL // NUM_HEADS
        B, LQ, LKV = (4, 128, 256)

        def _xavier(key, shape):
            fan_in, fan_out = (shape[1], shape[0])
            limit = float(np.sqrt(6.0 / (fan_in + fan_out)))
            return jax.random.uniform(key, shape, jnp.float32, -limit, limit)

        def _split_heads(x, b):
            return x.reshape(b, -1, NUM_HEADS, DEPTH).transpose(0, 2, 1, 3)
        key = jax.random.key(seed)
        ks = jax.random.split(key, 6)
        return {'query': jax.random.normal(ks[0], (B, LQ, D_MODEL), jnp.float32), 'value': jax.random.normal(ks[1], (B, LKV, D_MODEL), jnp.float32), 'wq_w': _xavier(ks[2], (D_MODEL, D_MODEL)), 'wk_w': _xavier(ks[3], (D_MODEL, D_MODEL)), 'wv_w': _xavier(ks[4], (D_MODEL, D_MODEL)), 'dense_w': _xavier(ks[5], (D_MODEL, D_MODEL)), 'wq_b': jnp.zeros((D_MODEL,), jnp.float32), 'wk_b': jnp.zeros((D_MODEL,), jnp.float32), 'wv_b': jnp.zeros((D_MODEL,), jnp.float32), 'dense_b': jnp.zeros((D_MODEL,), jnp.float32)}
    _L3_xattn_all = _L3_xattn_setup()
    _L3_xattn_in = {k: v for k, v in _L3_xattn_all.items() if k in ('wq_w', 'wk_w', 'wv_w', 'dense_w', 'wq_b', 'wk_b', 'wv_b', 'dense_b')}
    del _L3_xattn_all

    def _L3_ffn_setup():
        import jax, jax.numpy as jnp
        import numpy as np
        DIM = 128
        INTER = 128
        N_EXPERTS = 8
        TOPK = 2
        N_SHARED = 2
        key = jax.random.key(seed)
        ks = jax.random.split(key, 10)
        s = 0.02
        return {'x': jax.random.normal(ks[0], (4, 256, DIM), dtype=jnp.float32), 'gate_w': jax.random.normal(ks[1], (N_EXPERTS, DIM), dtype=jnp.float32) * s, 'gate_bias': jax.random.normal(ks[2], (N_EXPERTS,), dtype=jnp.float32) * s, 'w1': jax.random.normal(ks[3], (N_EXPERTS, INTER, DIM), dtype=jnp.float32) * s, 'w3': jax.random.normal(ks[4], (N_EXPERTS, INTER, DIM), dtype=jnp.float32) * s, 'w2': jax.random.normal(ks[5], (N_EXPERTS, DIM, INTER), dtype=jnp.float32) * s, 'sw1': jax.random.normal(ks[6], (N_SHARED * INTER, DIM), dtype=jnp.float32) * s, 'sw3': jax.random.normal(ks[7], (N_SHARED * INTER, DIM), dtype=jnp.float32) * s, 'sw2': jax.random.normal(ks[8], (DIM, N_SHARED * INTER), dtype=jnp.float32) * s}
    _L3_ffn_all = _L3_ffn_setup()
    _L3_ffn_in = {k: v for k, v in _L3_ffn_all.items() if k in ('gate_w', 'gate_bias', 'w1', 'w3', 'w2', 'sw1', 'sw3', 'sw2')}
    del _L3_ffn_all
    return {'x': x, 'ctx_1024': ctx_1024, 'mask_BxSxS2_bf1': mask_BxSxS2_bf1, 'mask_BxS2_bf1': mask_BxS2_bf1, 'L0_xattn_Wq': _L0_xattn_in['Wq'], 'L0_xattn_Wkv': _L0_xattn_in['Wkv'], 'L0_xattn_Wo': _L0_xattn_in['Wo'], 'L0_ffn_w_gate': _L0_ffn_in['w_gate'], 'L0_ffn_w_up': _L0_ffn_in['w_up'], 'L0_ffn_w_down': _L0_ffn_in['w_down'], 'L1_xattn_Wq': _L1_xattn_in['Wq'], 'L1_xattn_bq': _L1_xattn_in['bq'], 'L1_xattn_Wk': _L1_xattn_in['Wk'], 'L1_xattn_bk': _L1_xattn_in['bk'], 'L1_xattn_Wv': _L1_xattn_in['Wv'], 'L1_xattn_bv': _L1_xattn_in['bv'], 'L1_xattn_Wo': _L1_xattn_in['Wo'], 'L1_xattn_bo': _L1_xattn_in['bo'], 'L1_ffn_expert_sel': _L1_ffn_in['expert_sel'], 'L1_ffn_keys': _L1_ffn_in['keys'], 'L1_ffn_values': _L1_ffn_in['values'], 'L1_ffn_route_scale': _L1_ffn_in['route_scale'], 'L2_xattn_Wq': _L2_xattn_in['Wq'], 'L2_xattn_bq': _L2_xattn_in['bq'], 'L2_xattn_Wkv': _L2_xattn_in['Wkv'], 'L2_xattn_bkv': _L2_xattn_in['bkv'], 'L2_xattn_Wo': _L2_xattn_in['Wo'], 'L2_xattn_bo': _L2_xattn_in['bo'], 'L2_ffn_Wg': _L2_ffn_in['Wg'], 'L2_ffn_bg': _L2_ffn_in['bg'], 'L2_ffn_Wu': _L2_ffn_in['Wu'], 'L2_ffn_bu': _L2_ffn_in['bu'], 'L2_ffn_Wd': _L2_ffn_in['Wd'], 'L2_ffn_bd': _L2_ffn_in['bd'], 'L2_ffn_Wq': _L2_ffn_in['Wq'], 'L2_ffn_keys': _L2_ffn_in['keys'], 'L2_ffn_down_embed': _L2_ffn_in['down_embed'], 'L2_ffn_up_embed': _L2_ffn_in['up_embed'], 'L3_xattn_wq_w': _L3_xattn_in['wq_w'], 'L3_xattn_wk_w': _L3_xattn_in['wk_w'], 'L3_xattn_wv_w': _L3_xattn_in['wv_w'], 'L3_xattn_dense_w': _L3_xattn_in['dense_w'], 'L3_xattn_wq_b': _L3_xattn_in['wq_b'], 'L3_xattn_wk_b': _L3_xattn_in['wk_b'], 'L3_xattn_wv_b': _L3_xattn_in['wv_b'], 'L3_xattn_dense_b': _L3_xattn_in['dense_b'], 'L3_ffn_gate_w': _L3_ffn_in['gate_w'], 'L3_ffn_gate_bias': _L3_ffn_in['gate_bias'], 'L3_ffn_w1': _L3_ffn_in['w1'], 'L3_ffn_w3': _L3_ffn_in['w3'], 'L3_ffn_w2': _L3_ffn_in['w2'], 'L3_ffn_sw1': _L3_ffn_in['sw1'], 'L3_ffn_sw3': _L3_ffn_in['sw3'], 'L3_ffn_sw2': _L3_ffn_in['sw2']}

def reference(x, ctx_1024, mask_BxSxS2_bf1, mask_BxS2_bf1, L0_xattn_Wq, L0_xattn_Wkv, L0_xattn_Wo, L0_ffn_w_gate, L0_ffn_w_up, L0_ffn_w_down, L1_xattn_Wq, L1_xattn_bq, L1_xattn_Wk, L1_xattn_bk, L1_xattn_Wv, L1_xattn_bv, L1_xattn_Wo, L1_xattn_bo, L1_ffn_expert_sel, L1_ffn_keys, L1_ffn_values, L1_ffn_route_scale, L2_xattn_Wq, L2_xattn_bq, L2_xattn_Wkv, L2_xattn_bkv, L2_xattn_Wo, L2_xattn_bo, L2_ffn_Wg, L2_ffn_bg, L2_ffn_Wu, L2_ffn_bu, L2_ffn_Wd, L2_ffn_bd, L2_ffn_Wq, L2_ffn_keys, L2_ffn_down_embed, L2_ffn_up_embed, L3_xattn_wq_w, L3_xattn_wk_w, L3_xattn_wv_w, L3_xattn_dense_w, L3_xattn_wq_b, L3_xattn_wk_b, L3_xattn_wv_b, L3_xattn_dense_b, L3_ffn_gate_w, L3_ffn_gate_bias, L3_ffn_w1, L3_ffn_w3, L3_ffn_w2, L3_ffn_sw1, L3_ffn_sw3, L3_ffn_sw2):
    import jax
    import jax.numpy as jnp

    def _L0_xattn_ref(x, context, mask, Wq, Wkv, Wo):
        import jax, jax.numpy as jnp
        import numpy as np
        DIM = 128
        HEAD_DIM = 64
        NUM_HEADS = DIM // HEAD_DIM
        SCALE = HEAD_DIM ** (-0.5)
        B, N, C = x.shape
        M = context.shape[1]
        H, D = (NUM_HEADS, HEAD_DIM)
        q = (x @ Wq).reshape(B, N, H, D).transpose(0, 2, 1, 3)
        kv = (context @ Wkv).reshape(B, M, 2, H, D).transpose(2, 0, 3, 1, 4)
        k, v = (kv[0], kv[1])
        attn = jnp.einsum('bhnd,bhmd->bhnm', q, k) * SCALE
        attn = jnp.where(mask[:, None, :, :], attn, -jnp.inf)
        attn = jax.nn.softmax(attn, axis=-1)
        out = jnp.einsum('bhnm,bhmd->bhnd', attn, v)
        out = out.transpose(0, 2, 1, 3).reshape(B, N, C)
        return out @ Wo

    def _L0_ffn_ref(x, w_gate, w_up, w_down):
        import jax, jax.numpy as jnp
        import numpy as np
        BLOCK = 32
        W_BITS = 4
        ACT_BITS = 16

        def act_qdq(x):
            qmax = 2.0 ** (ACT_BITS - 1) - 1.0
            scale = jnp.maximum(jnp.max(jnp.abs(x)) / qmax, 1e-12)
            return jnp.clip(jnp.round(x / scale), -qmax - 1.0, qmax) * scale

        def fixed_qdq_u16(x):
            scale = 1.0 / 65536.0
            return jnp.clip(jnp.round(x / scale), 0.0, 65535.0) * scale

        def lpbq_dequant(w):
            O, I = w.shape
            qmax = 2.0 ** (W_BITS - 1) - 1.0
            wb = w.reshape(O, I // BLOCK, BLOCK)
            s = jnp.maximum(jnp.max(jnp.abs(wb), axis=-1, keepdims=True) / qmax, 1e-12)
            wq = jnp.clip(jnp.round(wb / s), -qmax - 1.0, qmax) * s
            return wq.reshape(O, I)
        x = act_qdq(x)
        up = act_qdq(x @ lpbq_dequant(w_up).T)
        gate = act_qdq(x @ lpbq_dequant(w_gate).T)
        sig = fixed_qdq_u16(jax.nn.sigmoid(gate))
        gate = act_qdq(gate * sig)
        o = act_qdq(gate * up)
        return o @ lpbq_dequant(w_down).T

    def _L1_xattn_ref(x1, x2, Wq, bq, Wk, bk, Wv, bv, Wo, bo):
        import jax, jax.numpy as jnp
        import numpy as np
        D_MODEL = 128
        NUM_HEADS = 16
        HEAD_DIM = D_MODEL // NUM_HEADS
        B, SQ, _ = x1.shape
        SK = x2.shape[1]

        def split_heads(t, S):
            return t.reshape(B, S, NUM_HEADS, HEAD_DIM).transpose(0, 2, 1, 3)
        Q = split_heads(x1 @ Wq + bq, SQ)
        K = split_heads(x2 @ Wk + bk, SK)
        V = split_heads(x2 @ Wv + bv, SK)
        scores = jnp.einsum('bhqd,bhkd->bhqk', Q, K) / jnp.sqrt(jnp.asarray(HEAD_DIM, Q.dtype))
        attn = jax.nn.softmax(scores, axis=-1)
        ctx = jnp.einsum('bhqk,bhkd->bhqd', attn, V)
        ctx = ctx.transpose(0, 2, 1, 3).reshape(B, SQ, D_MODEL)
        return ctx @ Wo + bo

    def _L1_ffn_ref(x, expert_sel, keys, values, route_scale):
        import jax, jax.numpy as jnp
        import numpy as np
        DMODEL = 128
        N_EXPERTS = 16
        EXPERT_SIZE = 32
        K = 4
        sel_logits = jnp.einsum('btd,ed->bte', x, expert_sel)
        sel_probs = jax.nn.sigmoid(sel_logits)
        _, sel_index = jax.lax.top_k(sel_probs, K)
        sel_val = jnp.take_along_axis(sel_probs, sel_index, axis=-1)
        sel_val = sel_val / jnp.clip(sel_val.sum(-1, keepdims=True), 1e-09)
        sel_val = sel_val * route_scale
        scores_all = jax.nn.relu(jnp.einsum('btd,edh->bteh', x, keys))
        values_all = jnp.einsum('bteh,ehv->btev', scores_all, values)
        sel_idx_exp = sel_index[..., None]
        selected = jnp.take_along_axis(values_all, sel_idx_exp, axis=2)
        out = (selected * sel_val[..., None]).sum(axis=2)
        return out

    def _L2_xattn_ref(x, context, context_mask, Wq, bq, Wkv, bkv, Wo, bo):
        import jax, jax.numpy as jnp
        import numpy as np
        GAMMA = 10.0
        BASE = 10000.0
        SCALE = 64 ** (-0.5)
        NUM_HEADS = 16

        def _larope(t, seq_len):
            B, H, L, D = t.shape
            inv_freq = 1.0 / BASE ** (jnp.arange(0, D, 2, dtype=jnp.float32) / D)
            pos = GAMMA * (jnp.arange(L, dtype=jnp.float32) / float(seq_len))
            ang = pos[:, None] * inv_freq
            cos = jnp.cos(ang)
            sin = jnp.sin(ang)
            te, to = (t[..., 0::2], t[..., 1::2])
            re = te * cos - to * sin
            ro = te * sin + to * cos
            return jnp.stack([re, ro], axis=-1).reshape(t.shape)
        B, Lq, D = x.shape
        Lk = context.shape[1]
        H = NUM_HEADS
        hd = D // H
        q = x @ Wq + bq
        kv = context @ Wkv + bkv
        k, v = jnp.split(kv, 2, axis=-1)
        q = q.reshape(B, Lq, H, hd).transpose(0, 2, 1, 3)
        k = k.reshape(B, Lk, H, hd).transpose(0, 2, 1, 3)
        v = v.reshape(B, Lk, H, hd).transpose(0, 2, 1, 3)
        q = _larope(q, Lq)
        k = _larope(k, Lk)
        scores = jnp.einsum('bhqd,bhkd->bhqk', q, k) * SCALE
        scores = jnp.where(context_mask[:, None, None, :], scores, -jnp.inf)
        attn = jax.nn.softmax(scores, axis=-1)
        out = jnp.einsum('bhqk,bhkd->bhqd', attn, v)
        out = out.transpose(0, 2, 1, 3).reshape(B, Lq, H * hd)
        return out @ Wo + bo

    def _L2_ffn_ref(hidden_states, Wg, bg, Wu, bu, Wd, bd, Wq, keys, down_embed, up_embed):
        import jax, jax.numpy as jnp
        import numpy as np
        B, T, D = (2, 256, 128)
        DCD = 512
        RET = 128
        NEXP = 512
        NKEYS = 64
        H = 4
        KPH = 8
        b, t, d = hidden_states.shape
        q = (hidden_states @ Wq).reshape(b, t, 2, H, RET // 2)
        sim = jnp.einsum('btphn,hkpn->pbthk', q, keys)
        sc, ix = jax.lax.top_k(sim, KPH)
        sx, sy = (sc[0], sc[1])
        ixx, ixy = (ix[0], ix[1])
        all_sc = (sx[..., :, None] + sy[..., None, :]).reshape(b, t, H, KPH * KPH)
        all_ix = (ixx[..., :, None] * NKEYS + ixy[..., None, :]).reshape(b, t, H, KPH * KPH)
        scores, pk = jax.lax.top_k(all_sc, KPH)
        idx = jnp.take_along_axis(all_ix, pk, axis=-1)
        de = down_embed[idx]
        ue = up_embed[idx]
        w = jnp.einsum('btd,bthkd->bthk', hidden_states, de)
        w = jax.nn.silu(w) * jax.nn.softmax(scores, axis=-1)
        experts_states = jnp.einsum('bthk,bthkd->btd', w, ue)
        mlp = jax.nn.silu(hidden_states @ Wg + bg) * (hidden_states @ Wu + bu) @ Wd + bd
        return mlp + experts_states

    def _L3_xattn_ref(query, value, wq_w, wk_w, wv_w, dense_w, wq_b, wk_b, wv_b, dense_b):
        import jax, jax.numpy as jnp
        import numpy as np
        D_MODEL = 128
        NUM_HEADS = 16
        DEPTH = D_MODEL // NUM_HEADS
        B, LQ, LKV = (4, 128, 256)

        def _xavier(key, shape):
            fan_in, fan_out = (shape[1], shape[0])
            limit = float(np.sqrt(6.0 / (fan_in + fan_out)))
            return jax.random.uniform(key, shape, jnp.float32, -limit, limit)

        def _split_heads(x, b):
            return x.reshape(b, -1, NUM_HEADS, DEPTH).transpose(0, 2, 1, 3)
        b = query.shape[0]
        q = query @ wq_w.T + wq_b
        k = value @ wk_w.T + wk_b
        v = value @ wv_w.T + wv_b
        q = _split_heads(q, b)
        k = _split_heads(k, b)
        v = _split_heads(v, b)
        scale = jnp.sqrt(jnp.asarray(DEPTH, q.dtype))
        scores = jnp.einsum('bhqd,bhkd->bhqk', q, k) / scale
        attn = jax.nn.softmax(scores, axis=-1)
        ctx = jnp.einsum('bhqk,bhkd->bhqd', attn, v)
        ctx = ctx.transpose(0, 2, 1, 3).reshape(b, -1, D_MODEL)
        return ctx @ dense_w.T + dense_b

    def _L3_ffn_ref(x, gate_w, gate_bias, w1, w3, w2, sw1, sw3, sw2):
        import jax, jax.numpy as jnp
        import numpy as np
        DIM = 128
        INTER = 128
        N_EXPERTS = 8
        TOPK = 2
        N_SHARED = 2
        shape = x.shape
        xt = x.reshape(-1, shape[-1])
        scores = jax.nn.softmax((xt @ gate_w.T).astype(jnp.float32), axis=-1)
        _, idx = jax.lax.top_k(scores + gate_bias, TOPK)
        weights = jnp.take_along_axis(scores, idx, axis=1).astype(x.dtype)
        y = jnp.zeros_like(xt)
        for e in range(N_EXPERTS):
            gate_e = jnp.sum(jnp.where(idx == e, weights, 0.0), axis=1)
            h = jax.nn.silu(xt @ w1[e].T) * (xt @ w3[e].T)
            y = y + gate_e[:, None] * (h @ w2[e].T)
        z = jax.nn.silu(xt @ sw1.T) * (xt @ sw3.T) @ sw2.T
        return (y + z).reshape(shape)
    x = x + _L0_xattn_ref(_layernorm(x, axis=-1), ctx_1024, mask_BxSxS2_bf1, L0_xattn_Wq, L0_xattn_Wkv, L0_xattn_Wo)
    x = x + _L0_ffn_ref(_layernorm(x, axis=-1), L0_ffn_w_gate, L0_ffn_w_up, L0_ffn_w_down)
    x = x + _L1_xattn_ref(_layernorm(x, axis=-1), ctx_1024, L1_xattn_Wq, L1_xattn_bq, L1_xattn_Wk, L1_xattn_bk, L1_xattn_Wv, L1_xattn_bv, L1_xattn_Wo, L1_xattn_bo)
    x = x + _L1_ffn_ref(_layernorm(x, axis=-1), L1_ffn_expert_sel, L1_ffn_keys, L1_ffn_values, L1_ffn_route_scale)
    x = x + _L2_xattn_ref(_layernorm(x, axis=-1), ctx_1024, mask_BxS2_bf1, L2_xattn_Wq, L2_xattn_bq, L2_xattn_Wkv, L2_xattn_bkv, L2_xattn_Wo, L2_xattn_bo)
    x = x + _L2_ffn_ref(_layernorm(x, axis=-1), L2_ffn_Wg, L2_ffn_bg, L2_ffn_Wu, L2_ffn_bu, L2_ffn_Wd, L2_ffn_bd, L2_ffn_Wq, L2_ffn_keys, L2_ffn_down_embed, L2_ffn_up_embed)
    x = x + _L3_xattn_ref(_layernorm(x, axis=-1), ctx_1024, L3_xattn_wq_w, L3_xattn_wk_w, L3_xattn_wv_w, L3_xattn_dense_w, L3_xattn_wq_b, L3_xattn_wk_b, L3_xattn_wv_b, L3_xattn_dense_b)
    x = x + _L3_ffn_ref(_layernorm(x, axis=-1), L3_ffn_gate_w, L3_ffn_gate_bias, L3_ffn_w1, L3_ffn_w3, L3_ffn_w2, L3_ffn_sw1, L3_ffn_sw3, L3_ffn_sw2)
    return x

_drawn_inputs = setup_inputs


def setup_inputs(seed=0):
    import zlib

    import numpy as np

    out = dict(_drawn_inputs(seed))
    spreads = {'L1_xattn_bq': (0.0, 0.528),
     'L1_xattn_bk': (0.0, 2.0),
     'L1_xattn_bv': (0.0, 0.1),
     'L1_xattn_bo': (0.0, 0.277),
     'L2_xattn_bq': (0.0, 2.0),
     'L2_xattn_bkv': (0.0, 0.1),
     'L2_xattn_bo': (0.0, 0.1),
     'L2_ffn_bg': (0.0, 0.8),
     'L2_ffn_bu': (0.0, 0.8),
     'L2_ffn_bd': (0.0, 0.421),
     'L3_xattn_wq_b': (0.0, 1.734),
     'L3_xattn_wk_b': (0.0, 2.0),
     'L3_xattn_wv_b': (0.0, 0.46),
     'L3_xattn_dense_b': (0.0, 0.47)}
    factors = {'L0_ffn_w_gate': 7.535,
     'L0_ffn_w_up': 7.347,
     'L0_ffn_w_down': 7.27,
     'L2_ffn_Wg': 7.408,
     'L2_ffn_Wu': 7.304,
     'L2_ffn_Wd': 6.755,
     'L2_ffn_Wq': 25.764,
     'L2_ffn_keys': 24.016,
     'L2_ffn_down_embed': 8.0,
     'L2_ffn_up_embed': 8.0,
     'L3_ffn_gate_w': 8.0,
     'L3_ffn_gate_bias': 8.0,
     'L3_ffn_w1': 8.0,
     'L3_ffn_w3': 8.0,
     'L3_ffn_w2': 8.0,
     'L3_ffn_sw1': 8.0,
     'L3_ffn_sw3': 8.0,
     'L3_ffn_sw2': 8.0}
    for name, (base, spread) in spreads.items():
        noise = np.random.default_rng([zlib.crc32(name.encode()), seed]).standard_normal(out[name].shape)
        drawn = base * np.exp(spread * noise) if base else spread * noise
        out[name] = jnp.asarray(drawn.astype(out[name].dtype))
    for name, factor in factors.items():
        out[name] = (out[name] * factor).astype(out[name].dtype)
    return out
```

```python
from contextlib import ExitStack

import concourse.bass as bass
import numpy as np
from concourse import mybir

F32 = mybir.dt.float32
BF16 = mybir.dt.bfloat16
U8 = mybir.dt.uint8
ALU = mybir.AluOpType
ACT = mybir.ActivationFunctionType
AX = mybir.AxisListType
ds = bass.ds

P = 128
B, SQ, SK, D = 16, 256, 64, 128
N_TILES = B * SQ // P
N_GROUPS = N_TILES // 4
GT = 4
GN = GT * P
LN_EPS = 1e-5
MASKED = 1e30
ROUND = 1.5 * 2.0 ** 23
QMAX16 = 2.0 ** 15 - 1.0
QMAX4 = 2.0 ** 3 - 1.0
QBLOCK = 32
TINY = 1e-12
I0 = 384
NC0 = I0 // P
MOE1_E, MOE1_H, MOE1_K = 16, 32, 4
NH2, NK2 = 4, 64
NEXP2 = 512
ROWS2 = NEXP2 // NK2
E3 = 8
TOPK3 = 2
CH3 = E3 + 2

PACKS = {
    "const": [("ident", P), ("kmask8", 16), ("kmask64", 2), ("vmask8", 64), ("vmask64", P),
              ("cosq", SQ), ("sinq", SQ), ("cosk", SK), ("sink", SK),
              ("cols", 24)],
    "once": [("hsel8", 8 * P), ("hsel64", P), ("row0", P), ("f2_wqT", 8 * P), ("f2_keysT", 8 * NK2)],
    "a0": [("a0_wq", P), ("a0_wk", P), ("a0_wv", P), ("a0_wo", P)],
    "f0": [("f0_gate", NC0 * P), ("f0_up", NC0 * P), ("f0_down", I0)],
    "a1": [("a1_wq", P), ("a1_wk", P), ("a1_wv", P), ("a1_wo", P)],
    "f1": [("f1_sel", MOE1_E), ("f1_keys", 512), ("f1_values", 512)],
    "a2": [("a2_wq", P), ("a2_wk", P), ("a2_wv", P), ("a2_wo", P), ("a2_wqs", P), ("a2_wks", P)],
    "f2": [("f2_wg", 512), ("f2_wu", 512), ("f2_wd", 512), ("f2_downT", 512), ("f2_upE", 512)],
    "a3": [("a3_wq", P), ("a3_wk", P), ("a3_wv", P), ("a3_wo", P)],
    "f3": [("f3_gate", E3), ("f3_w1", CH3 * P), ("f3_w3", CH3 * P), ("f3_w2", CH3 * P)],
}
COLS = ["a1_bq", "a1_bk", "a1_bv", "a2_bq", "a2_bk", "a2_bv", "a2_bqs", "a2_bks", "a3_bq", "a3_bk", "a3_bv",
        "f2_bg0", "f2_bg1", "f2_bg2", "f2_bg3", "f2_bu0", "f2_bu1", "f2_bu2", "f2_bu3"]
ROWS = ["a1_bo", "a2_bo", "a3_bo", "f2_bd"]
WIDTH = {k: sum(n for _, n in v) for k, v in PACKS.items()}


def build(nc, dram):
    with ExitStack() as ctx:
        def sb(name, shape, dt=F32):
            return ctx.enter_context(nc.sbuf_tensor(name, shape, dt))

        sems = {}

        def S(name):
            if name not in sems:
                sems[name] = ctx.enter_context(nc.semaphore(name))
            return sems[name]

        X = sb("X", [P, N_TILES, D])
        stats = sb("stats", [P, N_TILES, 6])
        W = {}
        pack_sb = {}
        big = sb("big", [P, 2 * N_GROUPS * NC0 * GN])
        HALF = N_GROUPS * NC0 * GN
        F0N = NC0 * GN
        tmp_all = sb("tmp", [P, 4 * F0N])
        tmp = tmp_all[:, :].rearrange("p (j i n) -> p j i n", j=2, i=2)
        shared = {"once": big[:, HALF:HALF + WIDTH["once"]], "f3": tmp_all[:, 0:WIDTH["f3"]]}
        for k, parts in PACKS.items():
            pack_sb[k] = shared[k] if k in shared else sb("w_" + k, [P, WIDTH[k]])
            at = 0
            for name, n in parts:
                W[name] = pack_sb[k][:, at:at + n]
                at += n

        def col(name):
            i = COLS.index(name)
            return W["cols"][:, i:i + 1]

        ident = W["ident"]
        ident16 = sb("ident16", [P, P], BF16)
        hsel16 = {8: sb("hsel16_8", [P, 8 * P], BF16), 64: sb("hsel16_64", [P, P], BF16)}
        row0_16 = sb("row0_16", [P, P], BF16)
        rows_bc = sb("rows_bc", [P, 4 * P])
        addrow = sb("addrow", [P, 4, P])
        bvmat = sb("bvmat", [P, 3, P])
        simw = sb("simw", [P, 512])
        gbias3 = sb("gbias3", [P, E3])
        rscale = sb("rscale", [P, 1])
        lnw = sb("lnw", [P, 10, N_TILES])
        hrow = sb("hrow", [P, 2, GN])
        hT = sb("hT", [P, 2, GN])
        qs = sb("qs", [P, 32])
        UP = big[:, 0:HALF].rearrange("p (g n) -> p g n", g=N_GROUPS)
        GATE = big[:, HALF:2 * HALF].rearrange("p (g n) -> p g n", g=N_GROUPS)
        H0 = big[:, 2 * HALF - N_GROUPS * GN:2 * HALF].rearrange("p (g n) -> p g n", g=N_GROUPS)

        class Carve:

            def __init__(self, limit=2 * HALF):
                self.at, self.limit = 0, limit

            def take(self, n, dt=F32):
                words = n if dt == F32 else (n + 1) // 2
                piece = big[:, self.at:self.at + words]
                self.at += words
                assert self.at <= self.limit
                return piece if dt == F32 else piece.bitcast(dt)[:, 0:n]

        psum = ctx.enter_context(nc.psum_tensor("psum", [P, 8, 512], F32))

        def bank(i):
            return psum[:, i, :]

        def tile_of(A, t):
            return A[:, ds(t, 1), :].rearrange("p a b -> p (a b)")

        def per_group(eng, body, first=0):
            with eng.Fori(0, N_GROUPS // 2 - 1) as k:
                for j in range(2):
                    body(2 * k + j, j, False)
            for g in (N_GROUPS - 2, N_GROUPS - 1):
                body(g, g % 2, g == N_GROUPS - 1)

        SUB = ("a0", "f0", "a1", "f1", "a2", "f2", "a3", "f3")
        HAS_ROW = {"a1": 0, "a2": 1, "a3": 2, "f2": 3}
        ALL = dict(stats=1, ln=10, var=1, std=1, normed=N_GROUPS, turned=N_GROUPS, hT=N_GROUPS, biased=N_GROUPS,
                   res=N_GROUPS, bn=N_TILES)
        ATT = dict(go=1, k_ps=1, v_ps=4, k=2, v=4, zero=2, kv=3 * B, q_ps=B, qT=B, q16=B, mx_ps=4 * B, mx=4 * B,
                   nm_ps=B, nmT=B, st_ps=4 * B, pt=4 * B, pv=4 * B, rz=B, oT=B, o_ps=B, mask=0, r=0, prep=0)
        ATT_A0 = dict(ATT, go=0, mx_ps=2 * B, mx=2 * B, st_ps=B, pt=B, pv=B, mask=2)

        def count(s, name):
            if name in ALL:
                return 0 if name == "biased" and s not in HAS_ROW else ALL[name]
            if s[0] == "f":
                return 0
            return (ATT_A0 if s == "a0" else ATT)[name]

        def sem(s, name):
            return S("all_" + name if name in ALL else "att_" + name if s[0] == "a" else s + "_" + name)

        def at(s, name):
            if name not in ALL and s[0] == "f":
                return 0
            return sum(count(x, name) for x in SUB[:SUB.index(s)])


        def settle(eng):
            eng.sem_inc(S("settled"), 1)

        def link(eng, chain, counter):
            def step(ins):
                counter[0] += 1
                ins.then_inc(chain, 1)
                eng.wait_ge(chain, counter[0])
            return step

        mean, rstd = lnw[:, 0, :], lnw[:, 1, :]

        def ln_finish_dve(dve, s):
            me, mo, ve, vo = (stats[:, :, i] for i in (1, 4, 2, 5))
            diff, sq, var, std, y, e = (lnw[:, i, :] for i in range(2, 8))
            c = [at(s, "ln")]
            step = link(dve, sem(s, "ln"), c)
            dve.wait_ge(sem(s, "stats"), at(s, "stats") + 1)
            step(dve.tensor_tensor(mean, me, mo, ALU.add))
            step(dve.tensor_scalar(mean, mean, 0.5, None, ALU.mult))
            step(dve.tensor_tensor(diff, me, mo, ALU.subtract))
            step(dve.scalar_tensor_tensor(out=sq, in0=diff, scalar=0.25, in1=diff, op0=ALU.mult, op1=ALU.mult))
            step(dve.tensor_tensor(var, ve, vo, ALU.add))
            step(dve.scalar_tensor_tensor(out=var, in0=var, scalar=1.0 / D, in1=sq, op0=ALU.mult, op1=ALU.add))
            dve.tensor_scalar(var, var, LN_EPS, None, ALU.add).then_inc(sem(s, "var"), 1)
            dve.wait_ge(sem(s, "std"), at(s, "std") + 1)
            step(dve.reciprocal(y, std))
            step(dve.tensor_tensor(e, y, y, ALU.mult))
            step(dve.scalar_tensor_tensor(out=e, in0=e, scalar=-0.5, in1=var, op0=ALU.mult, op1=ALU.mult))
            step(dve.scalar_tensor_tensor(out=rstd, in0=e, scalar=1.5, in1=y, op0=ALU.add, op1=ALU.mult))

        def ln_finish_act(act, s):
            act.wait_ge(sem(s, "var"), at(s, "var") + 1)
            act.activation(lnw[:, 5, :], lnw[:, 4, :], ACT.Sqrt).then_inc(sem(s, "std"), 1)

        def normalise(dve, s, g, j):
            dve.wait_ge(sem(s, "turned"), at(s, "turned") + g + 1)
            for t in range(GT):
                ins = dve.tensor_scalar(hrow[:, j, t * P:(t + 1) * P], tile_of(X, 4 * g + t),
                                        mean[:, ds(4 * g + t, 1)], rstd[:, ds(4 * g + t, 1)],
                                        ALU.subtract, ALU.mult)
            ins.then_inc(sem(s, "normed"), 1)

        def turn(pe, s, g, j, bank_free=None):
            pe.wait_ge(sem(s, "normed"), at(s, "normed") + g + 1)
            if bank_free is not None:
                pe.wait_ge(*bank_free)
            for t in range(GT):
                ins = pe.transpose(bank(0)[:, t * P:(t + 1) * P], hrow[:, j, t * P:(t + 1) * P], ident)
            ins.then_inc(sem(s, "turned"), 1)

        def take_turned(act, s, g, j):
            act.wait_ge(sem(s, "turned"), at(s, "turned") + g + 1 + 2)
            act.activation(hT[:, j, :], bank(0), ACT.Copy).then_inc(sem(s, "hT"), 1)

        def residual(dve, s, g, src, last_sub, ready):
            dve.wait_ge(*ready)
            if s in HAS_ROW:
                dve.wait_ge(sem(s, "biased"), at(s, "biased") + g + 1)
            xg = X[:, ds(4 * g, 4), :]
            dve.tensor_tensor(xg, xg, src.rearrange("p (t n) -> p t n", t=GT), ALU.add).then_inc(sem(s, "res"), 1)
            tail_stats(dve, s, g, last_sub)

        def tail_stats(dve, s, g, last_sub):
            if not last_sub:
                dve.wait_ge(sem(s, "res"), at(s, "res") + g + 1 + 1)
                for t in range(GT):
                    dve.bn_stats(tile_of(stats, 4 * g + t), tile_of(X, 4 * g + t)).then_inc(sem(s, "bn"), 1)

        def stats_done(dve, s, nxt):
            dve.wait_ge(sem(s, "bn"), at(s, "bn") + N_TILES)
            dve.sem_inc(sem(nxt, "stats"), 1)

        def bias_rows(pool, s):
            row = addrow[:, HAS_ROW[s], :]
            pool.wait_ge(S("rows"), 1)
            with pool.Fori(0, N_GROUPS) as g:
                pool.wait_ge(sem(s, "normed"), at(s, "normed") + g + 1)
                xg = X[:, ds(4 * g, 4), :]
                pool.tensor_tensor(xg, xg, row.unsqueeze(1).to_broadcast([P, GT, P]), ALU.add)\
                    .then_inc(sem(s, "biased"), 1)

        class Attn:
            def __init__(self, s, hd, scale, bias, rope, mask):
                self.s, self.hd, self.scale, self.bias, self.rope, self.mask = s, hd, scale, bias, rope, mask
                self.first = s == "a0"
                self.H = D // hd
                self.C = self.H // 2
                self.NP = max(1, self.C // 2)
                self.PC = min(2, self.C)
                self.MW = min(512, self.H * SK)
                self.MH = self.MW // SK
                self.U = 2 * self.H * SK // self.MW
                self.NPT = 4 if self.NP == 4 else 2
                a = Carve(HALF if s == "a0" else 2 * HALF)
                self.kT = a.take(B * SK)
                self.V2 = a.take(B * P).rearrange("p (b n) -> p b n", b=B)
                self.kbd = [a.take(self.C * P) for _ in range(2)]
                self.kbd16 = [a.take(self.C * P, BF16) for _ in range(2)]
                self.vw = [a.take(256) for _ in range(2)]
                self.pt = [a.take(512) for _ in range(self.NPT)]
                self.qT = [a.take(256) for _ in range(2)]
                self.q16 = [a.take(256, BF16) for _ in range(2)]
                self.nm = [a.take(2 * self.H) for _ in range(2)]
                self.nmT = [a.take(256, BF16) for _ in range(2)]
                self.oT = [a.take(256) for _ in range(2)]
                self.rz = a.take(256)
                self.t1, self.t2 = a.take(512), a.take(512)
                self.m16 = a.take(N_TILES * 2 * SK, BF16).rearrange("p (t n) -> p t n", t=N_TILES)
                self.km16 = a.take(B * SK, BF16)
                self.kmT = a.take(B)
                self.end = a.at
                self.kmask = W["kmask%d" % hd]
                self.vmask = W["vmask%d" % hd]
                self.hsel = hsel16[hd]

        atts = {
            "a0": Attn("a0", 64, 64 ** -0.5, False, False, "full"),
            "a1": Attn("a1", 8, 8 ** -0.5, True, False, None),
            "a2": Attn("a2", 8, 64 ** -0.5, True, True, "keys"),
            "a3": Attn("a3", 8, 8 ** -0.5, True, False, None),
        }
        mask_u8 = sb("mask_u8", [P, N_TILES * SK], U8)
        kmrow_u8 = sb("kmrow_u8", [1, B * SK], U8)
        kmT_u8 = sb("kmT_u8", [P, B], U8)
        ctxd = sb("ctxd", [P, B, 2, SK])

        def att_prep_pe(pe, L):
            s = L.s
            pe.wait_ge(S("ld_" + s), 16)
            pe.wait_ge(S("ld_ctx"), 16)
            if s != "a0":
                pe.wait_ge(sem(s, "go"), at(s, "go") + 1)
            for i in range(2):
                ins = pe.matmul(bank(1 + i), W[s + "_wk"], ctxd[:, 8 * i:8 * i + 8, 0, :], start=True, stop=True)
                if L.rope:
                    ins = pe.matmul(bank(3 + i), W[s + "_wks"], ctxd[:, 8 * i:8 * i + 8, 0, :], start=True, stop=True)
            ins.then_inc(sem(L.s, "k_ps"), 1)
            for i in range(4):
                if i > 1:
                    pe.wait_ge(sem(L.s, "v"), at(L.s, "v") + i - 1)
                for m in range(4):
                    b = 4 * i + m
                    ins = pe.matmul(bank(5 + i % 2)[:, m * P:(m + 1) * P], ctxd[:, b].rearrange("p a k -> p (a k)"),
                                    W[s + "_wv"], start=True, stop=True)
                ins.then_inc(sem(L.s, "v_ps"), 1)

        def att_prep_act(act, L):
            act.wait_ge(sem(L.s, "k_ps"), at(L.s, "k_ps") + 1)
            if not L.rope:
                for i in range(2):
                    act.activation(L.kT[:, 512 * i:512 * i + 512], bank(1 + i), ACT.Identity,
                                   bias=col(L.s + "_bk") if L.bias else 0.0).then_inc(sem(L.s, "k"), 1)
            for i in range(4):
                act.wait_ge(sem(L.s, "v_ps"), at(L.s, "v_ps") + i + 1)
                act.activation(L.V2[:, 4 * i:4 * i + 4, :].rearrange("p b n -> p (b n)"), bank(5 + i % 2), ACT.Copy)\
                    .then_inc(sem(L.s, "v"), 1)

        def att_prep_dve(dve, L):
            c = [0]
            step = link(dve, sem(L.s, "prep"), c)
            if L.rope:
                dve.wait_ge(sem(L.s, "k_ps"), at(L.s, "k_ps") + 1)
                for i in range(2):
                    v = lambda a: a.rearrange("p (b k) -> p b k", k=SK)
                    step(dve.scalar_tensor_tensor(
                        out=v(L.t1), in0=v(bank(1 + i)), scalar=col(L.s + "_bk"),
                        in1=W["cosk"].unsqueeze(1).to_broadcast([P, 8, SK]), op0=ALU.add, op1=ALU.mult))
                    step(dve.scalar_tensor_tensor(
                        out=v(L.t2), in0=v(bank(3 + i)), scalar=col(L.s + "_bks"),
                        in1=W["sink"].unsqueeze(1).to_broadcast([P, 8, SK]), op0=ALU.add, op1=ALU.mult))
                    ins = dve.tensor_tensor(L.kT[:, 512 * i:512 * i + 512], L.t1, L.t2, ALU.add)
                    ins.then_inc(sem(L.s, "k"), 1)
                    dve.wait_ge(sem(L.s, "k"), at(L.s, "k") + i + 1)
            dve.memset(L.nmT[0], 0.0).then_inc(sem(L.s, "zero"), 1)
            dve.memset(L.nmT[1], 0.0).then_inc(sem(L.s, "zero"), 1)
            if L.mask == "full":
                dve.wait_ge(S("ld_mask"), 48)
                m = mask_u8[:, :].rearrange("p (t k) -> p t k", t=N_TILES)
                for h in range(2):
                    dve.tensor_scalar(L.m16[:, :, h * SK:(h + 1) * SK], m, 1.0, MASKED, ALU.subtract, ALU.mult)\
                        .then_inc(sem(L.s, "mask"), 1)
            if L.mask == "keys":
                dve.wait_ge(S("ld_mask"), 48)
                dve.memset(L.km16, 0.0).then_inc(sem(L.s, "mask"), 1)
                dve.wait_ge(sem(L.s, "mask"), at(L.s, "mask") + 1)
                dve.tensor_scalar(L.km16[0:1, :], kmrow_u8[:, :], 1.0, MASKED, ALU.subtract, ALU.mult)\
                    .then_inc(sem(L.s, "mask"), 1)
                dve.tensor_scalar(L.kmT, kmT_u8[:, :], 1.0, MASKED, ALU.subtract, ALU.mult)\
                    .then_inc(sem(L.s, "mask"), 1)

        def att_pool(pool, L):
            pool.wait_ge(sem(L.s, "k"), at(L.s, "k") + 2)
            pool.wait_ge(sem(L.s, "v"), at(L.s, "v") + 4)
            row = L.s in HAS_ROW
            if row:
                pool.wait_ge(S("rows"), 1)

            def batch(b, j):
                pool.wait_ge(sem(L.s, "o_ps"), at(L.s, "o_ps") + b + 1)
                k = L.kT[:, ds(b * SK, SK)].unsqueeze(1).to_broadcast([P, L.H, SK])
                m = L.kmask.unsqueeze(2).to_broadcast([P, L.H, SK])
                pool.tensor_tensor(L.kbd16[j].rearrange("p (h k) -> p h k", h=L.H), k, m, ALU.mult)\
                    .then_inc(sem(L.s, "kv"), 1)
                pool.tensor_tensor(L.kbd[j].rearrange("p (h k) -> p h k", h=L.H), k, m, ALU.mult)\
                    .then_inc(sem(L.s, "kv"), 1)
                v = tile_of(L.V2, b)
                if L.hd == 64:
                    pool.tensor_tensor(L.vw[j][:, 0:P], v, L.vmask, ALU.mult).then_inc(sem(L.s, "kv"), 1)
                else:
                    pool.tensor_tensor(
                        L.vw[j].rearrange("p (q e n) -> p q e n", q=4, e=2),
                        v.rearrange("p (q n) -> p q n", q=4).unsqueeze(2).to_broadcast([P, 4, 2, 32]),
                        L.vmask.rearrange("p (e n) -> p e n", e=2).unsqueeze(1).to_broadcast([P, 4, 2, 32]),
                        ALU.mult).then_inc(sem(L.s, "kv"), 1)

            def bias(g):
                pool.wait_ge(sem(L.s, "normed"), at(L.s, "normed") + g + 1)
                xg = X[:, ds(4 * g, 4), :]
                r = addrow[:, HAS_ROW[L.s], :]
                pool.tensor_tensor(xg, xg, r.unsqueeze(1).to_broadcast([P, GT, P]), ALU.add)\
                    .then_inc(sem(L.s, "biased"), 1)

            with pool.Fori(0, N_GROUPS) as g:
                batch(2 * g, 0)
                batch(2 * g + 1, 1)
                if row:
                    bias(g)

        def att_pe(pe, L):
            s = L.s
            if L.first:
                pe.sem_inc(sem(L.s, "turned"), 2)
            if L.first:
                pe.sem_inc(sem(L.s, "pv"), 4)
            if L.first:
                pe.sem_inc(sem(L.s, "o_ps"), 2)
            pe.wait_ge(sem(L.s, "zero"), at(L.s, "zero") + 2)
            if L.mask:
                pe.wait_ge(sem(L.s, "mask"), at(L.s, "mask") + 3 if L.mask == "keys" else 2)

            def T(g, j):
                turn(pe, s, g, j, None if isinstance(g, int) and g == 0 else (sem(L.s, "qT"), at(L.s, "qT") + 2 * g))

            def Q(b, g, j, odd):
                pe.wait_ge(sem(L.s, "hT"), at(L.s, "hT") + g + 1)
                if odd:
                    pe.wait_ge(sem(L.s, "qT"), at(L.s, "qT") + b)
                src = hT[:, j, 256 * odd:256 * odd + 256]
                ins = pe.matmul(bank(0)[:, 0:256], W[s + "_wq"], src, start=True, stop=True)
                if L.rope:
                    ins = pe.matmul(bank(0)[:, 256:512], W[s + "_wqs"], src, start=True, stop=True)
                ins.then_inc(sem(L.s, "q_ps"), 1)

            def MX(b, j, u):
                if u == 0:
                    pe.wait_ge(sem(L.s, "q16"), at(L.s, "q16") + b + 1)
                    pe.wait_ge(sem(L.s, "kv"), at(L.s, "kv") + 3 * b + 1)
                pe.wait_ge(sem(L.s, "mx"), at(L.s, "mx") + b * L.U + u + 1)
                t, hf = u * L.MW // (L.H * SK), u % (L.U // 2)
                out = bank(1 + u % 2)[:, 0:L.MW]
                q = L.q16[j][:, t * P:(t + 1) * P]
                rhs = L.kbd16[j][:, hf * L.MW:(hf + 1) * L.MW]
                ins = pe.matmul(out, q, rhs, start=True, stop=not L.mask)
                if L.mask == "full":
                    ins = pe.matmul(out, ident16[:, :], tile_of(L.m16, 2 * b + t), start=False, stop=True)
                if L.mask == "keys":
                    rhs = L.km16[:, ds(b * SK, SK)].unsqueeze(1).to_broadcast([P, L.MH, SK])
                    ins = pe.matmul(out.rearrange("p (h k) -> p h k", k=SK), row0_16[:, :], rhs,
                                    start=False, stop=True)
                ins.then_inc(sem(L.s, "mx_ps"), 1)

            def MXT(b, j):
                pe.wait_ge(sem(L.s, "mx"), at(L.s, "mx") + (b + 1) * L.U + 2)
                pe.wait_ge(sem(L.s, "nmT"), at(L.s, "nmT") + b + 1)
                for t in range(2):
                    ins = pe.transpose(bank(6)[0:L.H, t * P:(t + 1) * P], L.nm[j][:, t * L.H:(t + 1) * L.H], ident)
                ins.then_inc(sem(L.s, "nm_ps"), 1)

            def ST(b, j, p):
                if p == 0:
                    pe.wait_ge(sem(L.s, "nmT"), at(L.s, "nmT") + b + 1 + 1)
                    pe.wait_ge(sem(L.s, "kv"), at(L.s, "kv") + 3 * b + 2)
                pe.wait_ge(sem(L.s, "pt"), at(L.s, "pt") + b * L.NP + p + 1)
                bk = bank(3 + (p % 2 if L.NP > 1 else j))
                for e in range(L.PC):
                    c = L.PC * p + e
                    out = bk[:, 256 * e:256 * e + 256]
                    pe.matmul(out, L.kbd[j][:, c * P:(c + 1) * P], L.qT[j], start=True, stop=False)
                    if L.mask == "full":
                        for t in range(2):
                            pe.matmul(out[:, t * P:(t + 1) * P], tile_of(L.m16, 2 * b + t), ident16[:, :],
                                      start=False, stop=False)
                    ins = pe.matmul(out, L.hsel[:, c * P:(c + 1) * P], L.nmT[j], start=False, stop=True)
                ins.then_inc(sem(L.s, "st_ps"), 1)

            def PV(b, j, p):
                if p == 0:
                    pe.wait_ge(sem(L.s, "kv"), at(L.s, "kv") + 3 * b + 3)
                    pe.wait_ge(sem(L.s, "oT"), at(L.s, "oT") + b + 1)
                pe.wait_ge(sem(L.s, "pt"), at(L.s, "pt") + b * L.NP + p + 1 + 2)
                if L.NP == 1:
                    pe.matmul(bank(5)[:, 0:256], L.vw[j][:, 0:P], L.pt[j][:, 0:256], start=True, stop=True)
                    ins = pe.matmul(bank(5)[:, 256:512], L.vmask, L.pt[j][:, 0:256], start=True, stop=True)
                else:
                    rows = slice(32 * p, 32 * p + 32)
                    for half, w in ((0, L.vw[j][:, 64 * p:64 * p + 64]), (256, L.vmask)):
                        for e in range(2):
                            ins = pe.matmul(bank(5)[rows, half:half + 256], w[:, 32 * e:32 * e + 32],
                                            L.pt[p][:, 256 * e:256 * e + 256], start=(e == 0), stop=(e == 1))
                ins.then_inc(sem(L.s, "pv"), 1)

            def O(b, g, odd):
                pe.wait_ge(sem(L.s, "oT"), at(L.s, "oT") + b + 1 + 1)
                if not odd:
                    pe.wait_ge(sem(L.s, "res"), at(L.s, "res") + g + 1)
                for t in range(2):
                    ins = pe.matmul(bank(7)[:, (2 * odd + t) * P:(2 * odd + t + 1) * P],
                                    L.oT[odd][:, t * P:(t + 1) * P], W[s + "_wo"], start=True, stop=True)
                ins.then_inc(sem(L.s, "o_ps"), 1)

            T(0, 0)
            Q(0, 0, 0, 0)
            for u in range(L.U):
                MX(0, 0, u)
            MXT(0, 0)

            def body(g, jg, last, first=False):
                for odd in range(2):
                    b = 2 * g + odd
                    nb = not (last and odd)
                    ng, njg = (g, jg) if not odd else (g + 1, 1 - jg)
                    units = list(range(L.U)) if nb else []
                    ST(b, odd, 0)
                    if nb:
                        Q(b + 1, ng, njg, 1 - odd)
                    if L.NP > 1:
                        ST(b, odd, 1)
                    if odd or not first:
                        O(b - 1, g if odd else g - 1, 1 - odd)
                    PV(b, odd, 0)
                    for p in range(2, L.NP):
                        if units:
                            MX(b + 1, 1 - odd, units.pop(0))
                        ST(b, odd, p)
                        PV(b, odd, p - 1)
                    for u in units:
                        MX(b + 1, 1 - odd, u)
                    if L.NP > 1:
                        PV(b, odd, L.NP - 1)
                    if not odd and not last:
                        T(g + 1, 1 - jg)
                    if nb:
                        MXT(b + 1, 1 - odd)

            body(0, 0, False, first=True)
            with pe.Fori(0, N_GROUPS // 2 - 1) as k:
                body(2 * k + 1, 1, False)
                body(2 * k + 2, 0, False)
            body(N_GROUPS - 1, 1, True)
            O(B - 1, N_GROUPS - 1, 1)

        def att_act(act, L):
            if L.first:
                act.sem_inc(sem(L.s, "nmT"), 1)
            if L.first:
                act.sem_inc(sem(L.s, "pt"), 2)
            act.activation(qs[:, 30:31], qs[:, 31:32], ACT.Exp)

            def takeQ(b, j):
                act.wait_ge(sem(L.s, "q_ps"), at(L.s, "q_ps") + b + 1)
                act.activation(L.qT[j], bank(0)[:, 0:256], ACT.Identity,
                               bias=col(L.s + "_bq") if L.bias else 0.0).then_inc(sem(L.s, "qT"), 1)

            def takeN(b, j):
                act.wait_ge(sem(L.s, "nm_ps"), at(L.s, "nm_ps") + b + 1)
                act.activation(L.nmT[j][0:L.H, :], bank(6)[0:L.H, 0:256], ACT.Copy).then_inc(sem(L.s, "nmT"), 1)

            def exp(b, j, p):
                act.wait_ge(sem(L.s, "st_ps"), at(L.s, "st_ps") + b * L.NP + p + 1)
                act.wait_ge(sem(L.s, "pv"), at(L.s, "pv") + b * L.NP + p + 1 + 4 - L.NPT)
                bk, out = (bank(3 + p % 2), L.pt[p]) if L.NP > 1 else (bank(3 + j), L.pt[j])
                n = 256 * L.PC
                if L.mask == "keys":
                    settle(act)
                bias = L.kmT[:, ds(b, 1)] if L.mask == "keys" else 0.0
                act.activation(out[:, 0:n], bk[:, 0:n], ACT.Exp, bias=bias, scale=L.scale).then_inc(sem(L.s, "pt"), 1)

            take_turned(act, L.s, 0, 0)
            if not L.rope:
                takeQ(0, 0)
            act.wait_ge(sem(L.s, "zero"), at(L.s, "zero") + 2)
            takeN(0, 0)
            if L.mask == "keys":
                act.wait_ge(sem(L.s, "mask"), at(L.s, "mask") + 3)

            def body(g, jg, last):
                for odd in range(2):
                    b = 2 * g + odd
                    nb = not (last and odd)
                    exp(b, odd, 0)
                    if nb and not L.rope:
                        takeQ(b + 1, 1 - odd)
                    for p in range(1, L.NP):
                        exp(b, odd, p)
                    if not odd and not last:
                        take_turned(act, L.s, g + 1, 1 - jg)
                    if nb:
                        takeN(b + 1, 1 - odd)

            per_group(act, body)

        def att_dve(dve, L, nxt):
            s = L.s
            if L.first:
                dve.sem_inc(sem(L.s, "mx"), 2)
            if L.first:
                dve.sem_inc(sem(L.s, "oT"), 1)
            if L.first:
                dve.sem_inc(sem(L.s, "res"), 1)

            def takeQ(b, j):
                dve.wait_ge(sem(L.s, "q_ps"), at(L.s, "q_ps") + b + 1)
                dve.scalar_tensor_tensor(out=L.t1[:, 0:256], in0=bank(0)[:, 0:256], scalar=col(s + "_bq"),
                                         in1=W["cosq"], op0=ALU.add, op1=ALU.mult).then_inc(sem(L.s, "r"), 1)
                dve.scalar_tensor_tensor(out=L.t2[:, 0:256], in0=bank(0)[:, 256:512], scalar=col(s + "_bqs"),
                                         in1=W["sinq"], op0=ALU.add, op1=ALU.mult).then_inc(sem(L.s, "r"), 1)
                dve.wait_ge(sem(L.s, "r"), at(L.s, "r") + 2 * b + 2)
                dve.tensor_tensor(L.qT[j], L.t1[:, 0:256], L.t2[:, 0:256], ALU.add).then_inc(sem(L.s, "qT"), 1)

            def q16(b, j):
                dve.wait_ge(sem(L.s, "qT"), at(L.s, "qT") + b + 1)
                dve.tensor_copy(L.q16[j], L.qT[j]).then_inc(sem(L.s, "q16"), 1)

            def mx(b, j, u):
                t, hf = u * L.MW // (L.H * SK), u % (L.U // 2)
                dve.wait_ge(sem(L.s, "mx_ps"), at(L.s, "mx_ps") + b * L.U + u + 1)
                dve.tensor_reduce(L.nm[j][:, t * L.H + hf * L.MH:t * L.H + (hf + 1) * L.MH],
                                  bank(1 + u % 2)[:, 0:L.MW].rearrange("p (h k) -> p h k", k=SK),
                                  AX.X, ALU.max, negate=True).then_inc(sem(L.s, "mx"), 1)

            def norm(b, j):
                dve.wait_ge(sem(L.s, "pv"), at(L.s, "pv") + (b + 1) * L.NP + 4)
                dve.wait_ge(sem(L.s, "o_ps"), at(L.s, "o_ps") + b + 1)
                dve.reciprocal(L.rz, bank(5)[:, 256:512]).then_inc(sem(L.s, "rz"), 1)
                dve.wait_ge(sem(L.s, "rz"), at(L.s, "rz") + b + 1)
                dve.tensor_tensor(L.oT[j], bank(5)[:, 0:256], L.rz, ALU.mult).then_inc(sem(L.s, "oT"), 1)

            def res(g):
                residual(dve, s, g, bank(7), False, (sem(L.s, "o_ps"), at(L.s, "o_ps") + 2 * g + 2 + 2))

            normalise(dve, s, 0, 0)
            if L.rope:
                takeQ(0, 0)
            q16(0, 0)
            for u in range(L.U):
                mx(0, 0, u)

            def body(g, jg, last, first=False):
                for odd in range(2):
                    b = 2 * g + odd
                    nb = not (last and odd)
                    if not odd and not last:
                        normalise(dve, s, g + 1, 1 - jg)
                    if nb:
                        if L.rope:
                            takeQ(b + 1, 1 - odd)
                        q16(b + 1, 1 - odd)
                    if not odd and not first:
                        res(g - 1)
                    if nb:
                        for u in range(L.U):
                            mx(b + 1, 1 - odd, u)
                    norm(b, odd)

            body(0, 0, False, first=True)
            with dve.Fori(0, N_GROUPS // 2 - 1) as k:
                body(2 * k + 1, 1, False)
                body(2 * k + 2, 0, False)
            body(N_GROUPS - 1, 1, True)
            res(N_GROUPS - 1)
            stats_done(dve, s, nxt)
            dve.sem_inc(sem(nxt, "go"), 1)

        f0w = {n: sb("f0_" + n + "T", [P, I0]) for n in ("gate", "up", "down")}
        amax = sb("amax", [P, 4, 8])
        wsc = sb("wsc", [P, 2, 12])

        def f0_weights_dve(dve):
            c = [0]
            step = link(dve, S("f0_w"), c)
            dve.wait_ge(S("ld_f0"), 16)
            for n in ("gate", "up", "down"):
                w = W["f0_" + n].rearrange("p (b k) -> p b k", k=QBLOCK)
                sc, inv = wsc[:, 0, :], wsc[:, 1, :]
                step(dve.tensor_reduce(sc, w, AX.X, ALU.max, apply_absolute_value=True))
                step(dve.tensor_scalar(sc, sc, 1.0 / QMAX4, TINY, ALU.mult, ALU.max))
                step(dve.reciprocal(inv, sc))
                step(dve.tensor_tensor(w, w, inv.unsqueeze(2).to_broadcast([P, 12, QBLOCK]), ALU.mult))
                step(dve.tensor_scalar(w, w, ROUND, ROUND, ALU.add, ALU.subtract))
                step(dve.tensor_tensor(w, w, sc.unsqueeze(2).to_broadcast([P, 12, QBLOCK]), ALU.mult))
            dve.sem_inc(S("f0_wq"), 1)

        def f0_weights_pe(pe):
            pe.wait_ge(S("f0_wq"), 1)
            for i, n in enumerate(("gate", "up", "down")):
                for c in range(NC0):
                    ins = pe.transpose(bank(1 + i)[:, c * P:(c + 1) * P], W["f0_" + n][:, c * P:(c + 1) * P], ident)
            ins.then_inc(S("f0_wT"), 1)

        def f0_weights_act(act):
            act.wait_ge(S("f0_wT"), 1)
            for i, n in enumerate(("gate", "up", "down")):
                act.activation(f0w[n][:, :], bank(1 + i)[:, 0:I0], ACT.Copy).then_inc(S("f0_wr"), 1)

        def scale_of(dve, which, n, c, step):
            for i in range(n):
                w = which + i
                step(dve.tensor_reduce(qs[:, 16 + w:17 + w], amax[:, w, :], AX.X, ALU.max))
            dve.sem_inc(S("f0_pmax"), 1)

        def scale_finish(dve, which, n, k, step):
            dve.wait_ge(S("f0_gmax"), k)
            for i in range(n):
                w = which + i
                step(dve.tensor_scalar(qs[:, 2 * w:2 * w + 1], qs[:, 20 + w:21 + w], 1.0 / QMAX16, TINY,
                                       ALU.mult, ALU.max))
                step(dve.reciprocal(qs[:, 2 * w + 1:2 * w + 2], qs[:, 2 * w:2 * w + 1]))

        def sc(w):
            return qs[:, 2 * w:2 * w + 1]

        def inv(w):
            return qs[:, 2 * w + 1:2 * w + 2]

        def f0_pool(pool):
            for k, (w, n) in enumerate(((0, 1), (1, 2), (3, 1), (0, 1))):
                pool.wait_ge(S("f0_pmax"), k + 1)
                pool.partition_all_reduce(qs[:, 20 + w:20 + w + n], qs[:, 16 + w:16 + w + n], P,
                                          bass.bass_isa.ReduceOp.max).then_inc(S("f0_gmax"), 1)

        def f0_dve(dve):
            s = "f0"
            c = [0]
            step = link(dve, S("f0_q"), c)
            with dve.Fori(0, N_GROUPS) as g:
                for t in range(GT):
                    dve.tensor_scalar(H0[:, ds(g, 1), t * P:(t + 1) * P].rearrange("p a b -> p (a b)"),
                                      tile_of(X, 4 * g + t), mean[:, ds(4 * g + t, 1)], rstd[:, ds(4 * g + t, 1)],
                                      ALU.subtract, ALU.mult).then_inc(S("f0_a"), 1)
                dve.wait_ge(S("f0_a"), 4 * g + 4)
                dve.tensor_reduce(amax[:, 0, ds(g, 1)], tile_of(H0, g), AX.X, ALU.max,
                                  apply_absolute_value=True).then_inc(S("f0_am"), 1)
            dve.wait_ge(S("f0_am"), N_GROUPS)
            scale_of(dve, 0, 1, c, step)
            scale_finish(dve, 0, 1, 1, step)

            def quant(g, j):
                dve.wait_ge(sem("f0", "turned"), at("f0", "turned") + g + 1)
                dve.tensor_scalar(hrow[:, j, :], tile_of(H0, g), inv(0), ROUND, ALU.mult, ALU.add)\
                    .then_inc(S("f0_r"), 1)
                dve.wait_ge(S("f0_r"), g + 1)
                dve.tensor_scalar(hrow[:, j, :], hrow[:, j, :], ROUND, sc(0), ALU.subtract, ALU.mult)\
                    .then_inc(sem("f0", "normed"), 1)

            quant(0, 0)

            def b_body(g, j, last):
                if not last:
                    quant(g + 1, 1 - j)
                for i, A in ((1, GATE), (2, UP)):
                    dve.wait_ge(S("f0_gu"), 2 * g + i + 2)
                    dve.tensor_reduce(amax[:, i, ds(g, 1)], tile_of(A, g), AX.X, ALU.max,
                                      apply_absolute_value=True).then_inc(S("f0_am"), 1)

            per_group(dve, b_body)
            dve.wait_ge(S("f0_am"), 3 * N_GROUPS)
            scale_of(dve, 1, 2, c, step)
            scale_finish(dve, 1, 2, 2, step)

            def c1(g, j):
                t = tmp[:, j, 0, :]
                dve.wait_ge(S("f0_c2"), g + 1)
                dve.tensor_scalar(t, tile_of(GATE, g), inv(1), ROUND, ALU.mult, ALU.add).then_inc(S("f0_c0"), 1)
                dve.wait_ge(S("f0_c0"), g + 1)
                dve.tensor_scalar(t, t, ROUND, sc(1), ALU.subtract, ALU.mult).then_inc(S("f0_c1"), 1)

            dve.sem_inc(S("f0_c2"), 2)
            c1(0, 0)

            def c_body(g, j, last):
                if not last:
                    c1(g + 1, 1 - j)
                t, y = tmp[:, j, 0, :], tmp[:, j, 1, :]
                dve.wait_ge(S("f0_sig"), g + 1)
                dve.tensor_scalar(y, y, 65536.0, ROUND, ALU.mult, ALU.add).then_inc(S("f0_cc"), 1)
                dve.wait_ge(S("f0_cc"), 2 * g + 1)
                dve.tensor_scalar(y, y, ROUND + 65535.0, ROUND, ALU.min, ALU.subtract).then_inc(S("f0_cc"), 1)
                dve.wait_ge(S("f0_cc"), 2 * g + 2)
                dve.scalar_tensor_tensor(out=tile_of(GATE, g), in0=y, scalar=2.0 ** -16, in1=t,
                                         op0=ALU.mult, op1=ALU.mult).then_inc(S("f0_c2"), 1)
                dve.wait_ge(S("f0_c2"), g + 1 + 2)
                dve.tensor_reduce(amax[:, 3, ds(g, 1)], tile_of(GATE, g), AX.X, ALU.max,
                                  apply_absolute_value=True).then_inc(S("f0_am"), 1)

            per_group(dve, c_body)
            dve.wait_ge(S("f0_am"), 4 * N_GROUPS)
            scale_of(dve, 3, 1, c, step)
            scale_finish(dve, 3, 1, 3, step)
            step(dve.tensor_tensor(qs[:, 12:13], sc(3), sc(2), ALU.mult))

            def d_body(g, j, last):
                t, y = tmp[:, j, 0, :], tmp[:, j, 1, :]
                dve.tensor_scalar(t, tile_of(GATE, g), inv(3), ROUND, ALU.mult, ALU.add).then_inc(S("f0_d"), 1)
                dve.tensor_scalar(y, tile_of(UP, g), inv(2), ROUND, ALU.mult, ALU.add).then_inc(S("f0_d"), 1)
                dve.wait_ge(S("f0_d"), 4 * g + 1)
                dve.tensor_scalar(t, t, ROUND, qs[:, 12:13], ALU.subtract, ALU.mult).then_inc(S("f0_d"), 1)
                dve.wait_ge(S("f0_d"), 4 * g + 3)
                dve.scalar_tensor_tensor(out=tile_of(GATE, g), in0=y, scalar=ROUND, in1=t,
                                         op0=ALU.subtract, op1=ALU.mult).then_inc(S("f0_d"), 1)
                dve.wait_ge(S("f0_d"), 4 * g + 4)
                dve.tensor_reduce(amax[:, 0, ds(g, 1)], tile_of(GATE, g), AX.X, ALU.max,
                                  apply_absolute_value=True).then_inc(S("f0_am"), 1)

            per_group(dve, d_body)
            dve.wait_ge(S("f0_am"), 5 * N_GROUPS)
            scale_of(dve, 0, 1, c, step)
            scale_finish(dve, 0, 1, 4, step)

            def e1(g, j):
                t = tmp[:, j, 0, :]
                dve.wait_ge(S("f0_o_ps"), g + 1)
                dve.tensor_scalar(t, tile_of(GATE, g), inv(0), ROUND, ALU.mult, ALU.add).then_inc(S("f0_e"), 1)
                dve.wait_ge(S("f0_e"), g + 1)
                dve.tensor_scalar(t, t, ROUND, sc(0), ALU.subtract, ALU.mult).then_inc(S("f0_oq"), 1)

            e1(0, 0)

            def e_body(g, j, last):
                if not last:
                    e1(g + 1, 1 - j)
                residual(dve, s, g, bank(7), False, (S("f0_o_ps"), g + 1 + 2))

            per_group(dve, e_body)
            stats_done(dve, s, "a1")
            dve.sem_inc(sem("a1", "go"), 1)

        def f0_act(act):
            act.sem_inc(S("f0_gu"), 2)
            take_turned(act, "f0", 0, 0)

            def b_body(g, j, last):
                if not last:
                    take_turned(act, "f0", g + 1, 1 - j)
                for i, A in enumerate((GATE, UP)):
                    act.wait_ge(S("f0_gu_ps"), 2 * g + i + 1)
                    settle(act)
                    act.activation(tile_of(A, g), psum[:, 1 + 3 * i:4 + 3 * i, :].rearrange("p c n -> p (c n)"),
                                   ACT.Copy).then_inc(S("f0_gu"), 1)

            per_group(act, b_body)
            act.activation(qs[:, 30:31], qs[:, 31:32], ACT.Sigmoid)

            def c_body(g, j, last):
                act.wait_ge(S("f0_c1"), g + 1)
                act.activation(tmp[:, j, 1, :], tmp[:, j, 0, :], ACT.Sigmoid).then_inc(S("f0_sig"), 1)

            per_group(act, c_body)

        def f0_pe(pe):
            pe.wait_ge(S("f0_wr"), 3)
            turn(pe, "f0", 0, 0)

            def b_body(g, j, last):
                if not last:
                    turn(pe, "f0", g + 1, 1 - j, (sem("f0", "hT"), at("f0", "hT") + g + 1))
                pe.wait_ge(sem("f0", "hT"), at("f0", "hT") + g + 1)
                for i, n in enumerate(("gate", "up")):
                    pe.wait_ge(S("f0_gu"), 2 * g + i + 1)
                    for c in range(NC0):
                        ins = pe.matmul(bank(1 + 3 * i + c), f0w[n][:, c * P:(c + 1) * P], hT[:, j, :],
                                        start=True, stop=True)
                    ins.then_inc(S("f0_gu_ps"), 1)

            per_group(pe, b_body)
            pe.sem_inc(S("f0_o_ps"), 2)

            def e_body(g, j, last):
                pe.wait_ge(S("f0_oq"), g + 1)
                pe.wait_ge(sem("f0", "res"), at("f0", "res") + g + 1)
                for t in range(GT):
                    for c in range(NC0):
                        ins = pe.matmul(bank(7)[:, t * P:(t + 1) * P],
                                        tmp[:, j, 0, c * GN + t * P:c * GN + (t + 1) * P],
                                        f0w["down"][:, c * P:(c + 1) * P], start=(c == 0), stop=(c == NC0 - 1))
                ins.then_inc(S("f0_o_ps"), 1)

            per_group(pe, e_body)

        f1 = Carve()
        prob1 = [f1.take(GT * MOE1_E) for _ in range(2)]
        top1 = f1.take(GT * 8).rearrange("p (t k) -> p t k", t=GT)
        f1s = f1.take(GT * 2).rearrange("p (i t) -> p i t", i=2)
        gate1 = f1.take(GT * MOE1_E)
        hid1 = [f1.take(512) for _ in range(2)]
        hidT1 = [f1.take(512) for _ in range(2)]

        def f1_pe(pe):
            s = "f1"
            pe.wait_ge(S("ld_f1"), 16)
            turn(pe, s, 0, 0)

            def body(g, j, last):
                pe.wait_ge(sem("f1", "hT"), at("f1", "hT") + g + 1)
                pe.wait_ge(S("f1_prob"), g + 1)
                for t in range(GT):
                    ins = pe.matmul(bank(1)[:, t * MOE1_E:(t + 1) * MOE1_E], hT[:, j, t * P:(t + 1) * P],
                                    W["f1_sel"], start=True, stop=True)
                ins.then_inc(S("f1_lg"), 1)
                if not last:
                    turn(pe, s, g + 1, 1 - j, (sem("f1", "hT"), at("f1", "hT") + g + 1))

                def keys(t):
                    pe.wait_ge(S("f1_hid"), 4 * g + t + 1)
                    pe.matmul(bank(2 + t % 2), hT[:, j, t * P:(t + 1) * P], W["f1_keys"], start=True, stop=True)\
                        .then_inc(S("f1_h_ps"), 1)

                def tr(t):
                    pe.wait_ge(S("f1_hid"), 4 * g + t + 1 + 2)
                    pe.wait_ge(S("f1_hidT"), 4 * g + t + 1)
                    for c in range(4):
                        ins = pe.transpose(bank(4 + t % 2)[:, c * P:(c + 1) * P], hid1[t % 2][:, c * P:(c + 1) * P],
                                           ident)
                    ins.then_inc(S("f1_tr"), 1)

                def val(t):
                    if t == 0:
                        pe.wait_ge(sem("f1", "res"), at("f1", "res") + g + 1)
                    pe.wait_ge(S("f1_hidT"), 4 * g + t + 1 + 2)
                    for c in range(4):
                        ins = pe.matmul(bank(7)[:, t * P:(t + 1) * P], hidT1[t % 2][:, c * P:(c + 1) * P],
                                        W["f1_values"][:, c * P:(c + 1) * P], start=(c == 0), stop=(c == 3))
                    ins.then_inc(S("f1_val"), 1)

                keys(0)
                keys(1)
                tr(0)
                keys(2)
                tr(1)
                val(0)
                keys(3)
                tr(2)
                val(1)
                tr(3)
                val(2)
                val(3)

            per_group(pe, body)

        def f1_act(act):
            act.sem_inc(S("f1_prob"), 1)
            act.sem_inc(S("f1_hidT"), 2)
            act.activation(qs[:, 30:31], qs[:, 31:32], ACT.Sigmoid)
            take_turned(act, "f1", 0, 0)

            def body(g, j, last):
                act.wait_ge(S("f1_lg"), g + 1)
                act.activation(prob1[j], bank(1)[:, 0:GT * MOE1_E], ACT.Sigmoid).then_inc(S("f1_prob"), 1)
                if not last:
                    take_turned(act, "f1", g + 1, 1 - j)
                for t in range(GT):
                    act.wait_ge(S("f1_tr"), 4 * g + t + 1)
                    if t >= 2:
                        act.wait_ge(S("f1_val"), 4 * g + t - 1)
                    act.activation(hidT1[t % 2], bank(4 + t % 2), ACT.Copy).then_inc(S("f1_hidT"), 1)

            per_group(act, body)

        def f1_dve(dve):
            s = "f1"
            dve.sem_inc(S("f1_hid"), 2)
            normalise(dve, s, 0, 0)

            def body(g, j, last):
                if not last:
                    normalise(dve, s, g + 1, 1 - j)
                pr = prob1[j].rearrange("p (t e) -> p t e", t=GT)
                ga = gate1.rearrange("p (t e) -> p t e", t=GT)
                dve.wait_ge(S("f1_prob"), g + 1 + 1)
                settle(dve)
                for t in range(GT):
                    dve.max(top1[:, t, :], pr[:, t, :]).then_inc(S("f1_top"), 1)
                dve.wait_ge(S("f1_top"), 4 * g + 4)
                dve.tensor_reduce(f1s[:, 0, :], top1[:, :, 0:MOE1_K], AX.X, ALU.add).then_inc(S("f1_g"), 1)
                dve.tensor_tensor(ga, pr, top1[:, :, MOE1_K - 1:MOE1_K].to_broadcast([P, GT, MOE1_E]), ALU.is_ge)\
                    .then_inc(S("f1_g"), 1)
                dve.wait_ge(S("f1_g"), 6 * g + 1)
                dve.tensor_scalar(f1s[:, 0, :], f1s[:, 0, :], 1e-9, None, ALU.max).then_inc(S("f1_g"), 1)
                dve.wait_ge(S("f1_g"), 6 * g + 3)
                dve.reciprocal(f1s[:, 1, :], f1s[:, 0, :]).then_inc(S("f1_g"), 1)
                dve.tensor_tensor(ga, ga, pr, ALU.mult).then_inc(S("f1_g"), 1)
                dve.wait_ge(S("f1_g"), 6 * g + 5)
                dve.scalar_tensor_tensor(out=ga, in0=ga, scalar=rscale[:, 0:1],
                                         in1=f1s[:, 1, :].unsqueeze(2).to_broadcast([P, GT, MOE1_E]),
                                         op0=ALU.mult, op1=ALU.mult).then_inc(S("f1_g"), 1)
                dve.wait_ge(S("f1_g"), 6 * g + 6)
                for t in range(GT):
                    dve.wait_ge(S("f1_h_ps"), 4 * g + t + 1)
                    if t >= 2:
                        dve.wait_ge(S("f1_tr"), 4 * g + t - 1)
                    dve.scalar_tensor_tensor(out=hid1[t % 2].rearrange("p (e h) -> p e h", h=MOE1_H),
                                             in0=bank(2 + t % 2).rearrange("p (e h) -> p e h", h=MOE1_H), scalar=0.0,
                                             in1=ga[:, t, :].unsqueeze(2).to_broadcast([P, MOE1_E, MOE1_H]),
                                             op0=ALU.max, op1=ALU.mult).then_inc(S("f1_hid"), 1)
                residual(dve, s, g, bank(7), False, (S("f1_val"), 4 * g + 4))

            per_group(dve, body)
            stats_done(dve, s, "a2")
            dve.sem_inc(sem("a2", "go"), 1)

        f2 = Carve()
        sim = [f2.take(GT * 512) for _ in range(2)]
        top2 = f2.take(GT * 8 * 8).rearrange("p (t c k) -> p t c k", t=GT, c=8)
        pair2 = f2.take(GT * 4 * 64).rearrange("p (t h n) -> p t h n", t=GT, h=NH2)
        best2 = f2.take(GT * 4 * 8).rearrange("p (t h k) -> p t h k", t=GT, h=NH2)
        lneg2 = f2.take(GT * NH2)
        e8 = f2.take(GT * 4 * 8).rearrange("p (t h k) -> p t h k", t=GT, h=NH2)
        z2 = f2.take(GT * NH2)
        rz2 = f2.take(GT * NH2)
        ssum = [f2.take(NH2 * 512) for _ in range(2)]
        ew = [f2.take(NH2 * 512) for _ in range(2)]
        mw = f2.take(NH2 * 512)
        acc2 = f2.take(GT * 512).rearrange("p (t n) -> p t n", t=GT)
        tot2 = f2.take(GT)
        sg = [f2.take(512) for _ in range(2)]
        pw = [f2.take(512) for _ in range(2)]
        pwT = [f2.take(512) for _ in range(2)]
        sl = [f2.take(512) for _ in range(2)]
        aT = f2.take(4 * 512).rearrange("p (c n) -> p c n", c=4)

        def f2_pe(pe):
            s = "f2"
            pe.wait_ge(S("f2_simw"), 1)
            turn(pe, s, 0, 0)

            def sims(g, j):
                pe.wait_ge(sem("f2", "hT"), at("f2", "hT") + g + 1)
                for t in range(GT):
                    pe.wait_ge(S("f2_sim"), 4 * g + t + 1)
                    pe.matmul(bank(1 + t % 2), hT[:, j, t * P:(t + 1) * P], simw[:, :], start=True, stop=True)\
                        .then_inc(S("f2_sim_ps"), 1)

            sims(0, 0)

            def body(g, j, last):
                if not last:
                    turn(pe, s, g + 1, 1 - j, (sem("f2", "hT"), at("f2", "hT") + g + 1))
                for c in range(4):
                    pe.wait_ge(S("f2_sl"), 4 * g + c + 1)
                    pe.matmul(bank(3), W["f2_wg"][:, c * P:(c + 1) * P], hT[:, j, :], start=True, stop=True)\
                        .then_inc(S("f2_g_ps"), 1)
                    pe.wait_ge(S("f2_aT"), 4 * g + c + 1)
                    pe.matmul(bank(4), W["f2_wu"][:, c * P:(c + 1) * P], hT[:, j, :], start=True, stop=True)\
                        .then_inc(S("f2_u_ps"), 1)
                if not last:
                    sims(g + 1, 1 - j)
                for t in range(GT):
                    pe.wait_ge(S("f2_sg"), 4 * g + t + 1)
                    pe.matmul(bank(5), hT[:, j, t * P:(t + 1) * P], W["f2_downT"], start=True, stop=True)\
                        .then_inc(S("f2_e_ps"), 1)
                    if t == 0:
                        pe.wait_ge(sem("f2", "res"), at("f2", "res") + g + 1)
                    pe.wait_ge(S("f2_aT"), 4 * g + 4 + 1)
                    for c in range(4):
                        pe.matmul(bank(7)[:, t * P:(t + 1) * P], aT[:, c, t * P:(t + 1) * P],
                                  W["f2_wd"][:, c * P:(c + 1) * P], start=(c == 0), stop=False)
                    pe.wait_ge(S("f2_pw"), 4 * g + t + 1 + 2)
                    pe.wait_ge(S("f2_pwT"), 4 * g + t + 1)
                    for c in range(4):
                        ins = pe.transpose(bank(6)[:, c * P:(c + 1) * P], pw[t % 2][:, c * P:(c + 1) * P], ident)
                    ins.then_inc(S("f2_tr"), 1)
                    pe.wait_ge(S("f2_pwT"), 4 * g + t + 1 + 1)
                    for c in range(4):
                        ins = pe.matmul(bank(7)[:, t * P:(t + 1) * P], pwT[t % 2][:, c * P:(c + 1) * P],
                                        W["f2_upE"][:, c * P:(c + 1) * P], start=False, stop=(c == 3))
                    ins.then_inc(S("f2_o_ps"), 1)

            per_group(pe, body)

        def f2_act(act):
            act.sem_inc(S("f2_sim"), 2)
            act.sem_inc(S("f2_sl"), 1)
            act.sem_inc(S("f2_sg"), 1)
            act.sem_inc(S("f2_pwT"), 1)
            take_turned(act, "f2", 0, 0)

            def sims(g, j):
                for t in range(GT):
                    act.wait_ge(S("f2_sim_ps"), 4 * g + t + 1)
                    act.activation(sim[j][:, t * 512:(t + 1) * 512], bank(1 + t % 2), ACT.Copy)\
                        .then_inc(S("f2_sim"), 1)

            def exps(g, j):
                act.wait_ge(S("f2_m"), g + 1)
                act.activation(e8.rearrange("p t h k -> p (t h k)"), e8.rearrange("p t h k -> p (t h k)"), ACT.Exp)\
                    .then_inc(S("f2_e8"), 1)
                for t in range(GT):
                    act.wait_ge(S("f2_S"), 4 * g + t + 1)
                    act.wait_ge(S("f2_acc"), 4 * g + t + 1)
                    for h in range(NH2):
                        ins = act.activation(ew[t % 2][:, h * 512:(h + 1) * 512], ssum[t % 2][:, h * 512:(h + 1) * 512],
                                             ACT.Exp, bias=lneg2[:, t * NH2 + h:t * NH2 + h + 1])
                    ins.then_inc(S("f2_ew"), 1)

            sims(0, 0)
            exps(0, 0)

            def body(g, j, last):
                if not last:
                    take_turned(act, "f2", g + 1, 1 - j)
                for c in range(4):
                    act.wait_ge(S("f2_g_ps"), 4 * g + c + 1)
                    act.wait_ge(S("f2_aT"), 4 * g + c + 1 - 1) if c else None
                    act.activation(sl[c % 2], bank(3), ACT.Silu, bias=col("f2_bg%d" % c)).then_inc(S("f2_sl"), 1)
                if not last:
                    sims(g + 1, 1 - j)
                for t in range(GT):
                    act.wait_ge(S("f2_e_ps"), 4 * g + t + 1)
                    act.wait_ge(S("f2_pw"), 4 * g + t + 1)
                    act.activation(sg[t % 2], bank(5), ACT.Silu).then_inc(S("f2_sg"), 1)
                    act.wait_ge(S("f2_tr"), 4 * g + t + 1)
                    act.activation(pwT[t % 2], bank(6), ACT.Copy).then_inc(S("f2_pwT"), 1)
                if not last:
                    exps(g + 1, 1 - j)

            per_group(act, body)

        def f2_pool(pool):
            row = addrow[:, HAS_ROW["f2"], :]
            def tiles(g, j):
                for t in range(GT):
                    pool.wait_ge(S("f2_acc"), 4 * g + t + 1)
                    st = sim[j][:, t * 512:(t + 1) * 512].rearrange("p (c h k) -> p c h k", c=2, h=NH2)
                    for h in range(NH2):
                        ins = pool.tensor_tensor(
                            ssum[t % 2][:, h * 512:(h + 1) * 512].rearrange("p (i j) -> p i j", i=ROWS2),
                            st[:, 0, h, 0:ROWS2].unsqueeze(2).to_broadcast([P, ROWS2, NK2]),
                            st[:, 1, h, :].unsqueeze(1).to_broadcast([P, ROWS2, NK2]), ALU.add)
                    ins.then_inc(S("f2_S"), 1)

            def bias(g):
                pool.wait_ge(sem("f2", "normed"), at("f2", "normed") + g + 1)
                xg = X[:, ds(4 * g, 4), :]
                pool.tensor_tensor(xg, xg, row.unsqueeze(1).to_broadcast([P, GT, P]), ALU.add)\
                    .then_inc(sem("f2", "biased"), 1)

            with pool.Fori(0, N_GROUPS // 2) as k:
                for j in range(2):
                    g = 2 * k + j
                    bias(g)
                    pool.wait_ge(S("f2_sim"), 4 * g + 4 + 2)
                    tiles(g, j)

        def f2_dve(dve):
            s = "f2"
            for n, v in (("aT", 1), ("pw", 2), ("acc", 2)):
                dve.sem_inc(S("f2_" + n), v)
            normalise(dve, s, 0, 0)

            def top(g, j):
                for t in range(GT):
                    dve.wait_ge(S("f2_sim"), 4 * g + t + 1 + 2)
                    settle(dve)
                    for c in range(8):
                        dve.max(top2[:, t, c, :], sim[j][:, t * 512 + c * 64:t * 512 + (c + 1) * 64])\
                            .then_inc(S("f2_t1"), 1)
                dve.wait_ge(S("f2_t1"), 32 * g + 32)
                for t in range(GT):
                    dve.tensor_tensor(pair2[:, t].rearrange("p h (a b) -> p h a b", a=8),
                                      top2[:, t, 0:4, :].unsqueeze(3).to_broadcast([P, NH2, 8, 8]),
                                      top2[:, t, 4:8, :].unsqueeze(2).to_broadcast([P, NH2, 8, 8]), ALU.add)\
                        .then_inc(S("f2_t2"), 1)
                for t in range(GT):
                    dve.wait_ge(S("f2_t2"), 4 * g + t + 1)
                    settle(dve)
                    for h in range(NH2):
                        dve.max(best2[:, t, h, :], pair2[:, t, h, :]).then_inc(S("f2_t3"), 1)
                dve.wait_ge(S("f2_t3"), 16 * g + 16)
                dve.tensor_scalar(lneg2.rearrange("p (t h) -> p t h", t=GT), best2[:, :, :, 0], -1.0, None, ALU.mult)
                dve.tensor_tensor(e8, best2, best2[:, :, :, 0:1].to_broadcast([P, GT, NH2, 8]), ALU.subtract)\
                    .then_inc(S("f2_m"), 1)
                dve.wait_ge(S("f2_e8"), g + 1)
                dve.tensor_reduce(z2.rearrange("p (t h) -> p t h", t=GT), e8, AX.X, ALU.add).then_inc(S("f2_z"), 1)
                dve.wait_ge(S("f2_z"), 2 * g + 1)
                dve.reciprocal(rz2, z2).then_inc(S("f2_z"), 1)
                dve.wait_ge(S("f2_z"), 2 * g + 2)

            def weigh(g, j):
                for t in range(GT):
                    n = 4 * g + t
                    dve.wait_ge(S("f2_ew"), n + 1)
                    for h in range(NH2):
                        blk = slice(h * 512, (h + 1) * 512)
                        dve.scalar_tensor_tensor(out=mw[:, blk], in0=ssum[t % 2][:, blk],
                                                 scalar=best2[:, t, h, 7:8], in1=ew[t % 2][:, blk],
                                                 op0=ALU.is_ge, op1=ALU.mult).then_inc(S("f2_mw"), 1)
                    for h in range(NH2):
                        blk = slice(h * 512, (h + 1) * 512)
                        r = rz2[:, t * NH2 + h:t * NH2 + h + 1]
                        dve.wait_ge(S("f2_mw"), 4 * n + h + 1)
                        if h == 0:
                            ins = dve.tensor_scalar(acc2[:, t, :], mw[:, blk], r, None, ALU.mult)
                        else:
                            dve.wait_ge(S("f2_ac"), 4 * n + h)
                            ins = dve.scalar_tensor_tensor(out=acc2[:, t, :], in0=mw[:, blk], scalar=r,
                                                           in1=acc2[:, t, :], op0=ALU.mult, op1=ALU.add)
                        ins.then_inc(S("f2_ac"), 1)
                    dve.wait_ge(S("f2_ac"), 4 * n + 4)
                    dve.tensor_reduce(tot2[:, t:t + 1], acc2[:, t, :], AX.X, ALU.add).then_inc(S("f2_acc"), 1)
                dve.wait_ge(S("f2_acc"), 4 * g + 4 + 2)
                dve.tensor_scalar(tot2, tot2, -1.0, float(NH2), ALU.mult, ALU.add).then_inc(S("f2_tt"), 1)
                dve.wait_ge(S("f2_tt"), 2 * g + 1)
                last_col = acc2[:, :, NEXP2 - 1]
                dve.tensor_tensor(last_col, last_col, tot2, ALU.add).then_inc(S("f2_tt"), 1)
                dve.wait_ge(S("f2_tt"), 2 * g + 2)

            top(0, 0)
            weigh(0, 0)

            def body(g, j, last):
                if not last:
                    normalise(dve, s, g + 1, 1 - j)
                for c in range(4):
                    n = 4 * g + c
                    dve.wait_ge(S("f2_sl"), n + 1 + 1)
                    dve.wait_ge(S("f2_u_ps"), n + 1)
                    dve.scalar_tensor_tensor(out=aT[:, c, :], in0=bank(4), scalar=col("f2_bu%d" % c), in1=sl[c % 2],
                                             op0=ALU.add, op1=ALU.mult).then_inc(S("f2_aT"), 1)
                for t in range(GT):
                    n = 4 * g + t
                    dve.wait_ge(S("f2_sg"), n + 1 + 1)
                    if t >= 2:
                        dve.wait_ge(S("f2_tr"), n - 1)
                    dve.tensor_tensor(pw[t % 2], acc2[:, t, :], sg[t % 2], ALU.mult).then_inc(S("f2_pw"), 1)
                residual(dve, s, g, bank(7), False, (S("f2_o_ps"), 4 * g + 4))
                if not last:
                    top(g + 1, 1 - j)
                    weigh(g + 1, 1 - j)

            per_group(dve, body)
            stats_done(dve, s, "a3")
            dve.sem_inc(sem("a3", "go"), 1)

        f3 = Carve()
        p3 = [f3.take(GT * E3) for _ in range(2)]
        w3b = f3.take(GT * E3)
        top3 = f3.take(GT * 8).rearrange("p (t k) -> p t k", t=GT)
        s3 = f3.take(GT * 4).rearrange("p (i t) -> p i t", i=4)
        gate3 = f3.take(GT * E3)
        sil3 = [f3.take(512) for _ in range(2)]
        hid3 = [f3.take(512) for _ in range(2)]

        def f3_pe(pe):
            s = "f3"
            pe.wait_ge(S("ld_f3"), 16)
            turn(pe, s, 0, 0)

            def logits(g, j):
                pe.wait_ge(sem("f3", "hT"), at("f3", "hT") + g + 1)
                pe.wait_ge(S("f3_p"), g + 1)
                for t in range(GT):
                    ins = pe.matmul(bank(7)[:, t * E3:(t + 1) * E3], hT[:, j, t * P:(t + 1) * P], W["f3_gate"],
                                    start=True, stop=True)
                ins.then_inc(S("f3_lg"), 1)

            logits(0, 0)

            def body(g, j, last):
                def up(e):
                    n = CH3 * g + e
                    pe.wait_ge(S("f3_sil"), n + 1)
                    pe.matmul(bank(1 + e % 2), W["f3_w1"][:, e * P:(e + 1) * P], hT[:, j, :], start=True, stop=True)\
                        .then_inc(S("f3_1_ps"), 1)
                    pe.wait_ge(S("f3_hid"), n + 1)
                    pe.matmul(bank(3 + e % 2), W["f3_w3"][:, e * P:(e + 1) * P], hT[:, j, :], start=True, stop=True)\
                        .then_inc(S("f3_3_ps"), 1)

                def down(e):
                    n = CH3 * g + e
                    pe.wait_ge(S("f3_hid"), n + 1 + 2)
                    if e < CH3 - 1:
                        pe.wait_ge(S("f3_y"), 9 * g + (e + 1 if e else 2))
                    bk = bank(5 + min(e, E3) % 2)
                    for t in range(GT):
                        ins = pe.matmul(bk[:, t * P:(t + 1) * P], hid3[e % 2][:, t * P:(t + 1) * P],
                                        W["f3_w2"][:, e * P:(e + 1) * P], start=True, stop=True) \
                            if e < E3 else \
                            pe.matmul(bk[:, t * P:(t + 1) * P], hid3[e % 2][:, t * P:(t + 1) * P],
                                      W["f3_w2"][:, e * P:(e + 1) * P], start=(e == E3 and t == 0),
                                      stop=(e == E3 + 1), skip_group_check=True)
                    ins.then_inc(S("f3_y_ps"), 1)

                up(0)
                for e in range(1, CH3):
                    up(e)
                    down(e - 1)
                    if e == 4 and not last:
                        turn(pe, s, g + 1, 1 - j, (sem("f3", "hT"), at("f3", "hT") + g + 1))
                down(CH3 - 1)
                if not last:
                    logits(g + 1, 1 - j)

            per_group(pe, body)

        def f3_act(act):
            act.sem_inc(S("f3_p"), 1)
            act.sem_inc(S("f3_sil"), 2)
            take_turned(act, "f3", 0, 0)

            def probs(g, j):
                act.wait_ge(S("f3_mx"), g + 1)
                act.activation(p3[j], p3[j], ACT.Exp).then_inc(S("f3_ex"), 1)

            probs(0, 0)

            def body(g, j, last):
                for e in range(CH3):
                    n = CH3 * g + e
                    act.wait_ge(S("f3_1_ps"), n + 1)
                    act.wait_ge(S("f3_hid"), n + 1)
                    act.activation(sil3[e % 2], bank(1 + e % 2), ACT.Silu).then_inc(S("f3_sil"), 1)
                    if e == 4 and not last:
                        take_turned(act, "f3", g + 1, 1 - j)
                if not last:
                    probs(g + 1, 1 - j)

            per_group(act, body)

        def f3_dve(dve):
            s = "f3"
            dve.wait_ge(S("ld_rows"), 48)
            for n, v in (("hid", 2), ("y", 2)):
                dve.sem_inc(S("f3_" + n), v)
            normalise(dve, s, 0, 0)
            v3 = lambda a: a.rearrange("p (t e) -> p t e", t=GT)
            bc = lambda a: a.unsqueeze(2).to_broadcast([P, GT, E3])

            def gates(g, j):
                dve.wait_ge(S("f3_lg"), g + 1)
                dve.tensor_reduce(s3[:, 0, :], v3(bank(7)[:, 0:GT * E3]), AX.X, ALU.max).then_inc(S("f3_g"), 1)
                dve.wait_ge(S("f3_g"), 9 * g + 1)
                dve.tensor_tensor(v3(p3[j]), v3(bank(7)[:, 0:GT * E3]), bc(s3[:, 0, :]), ALU.subtract)\
                    .then_inc(S("f3_mx"), 1)
                dve.wait_ge(S("f3_ex"), g + 1)
                dve.tensor_reduce(s3[:, 1, :], v3(p3[j]), AX.X, ALU.add).then_inc(S("f3_g"), 1)
                dve.wait_ge(S("f3_g"), 9 * g + 2)
                dve.reciprocal(s3[:, 2, :], s3[:, 1, :]).then_inc(S("f3_g"), 1)
                dve.wait_ge(S("f3_g"), 9 * g + 3)
                dve.tensor_tensor(v3(p3[j]), v3(p3[j]), bc(s3[:, 2, :]), ALU.mult).then_inc(S("f3_p"), 1)
                dve.wait_ge(S("f3_p"), g + 1 + 1)
                dve.tensor_tensor(v3(w3b), v3(p3[j]), gbias3[:, :].unsqueeze(1).to_broadcast([P, GT, E3]), ALU.add)\
                    .then_inc(S("f3_g"), 1)
                dve.wait_ge(S("f3_g"), 9 * g + 4)
                settle(dve)
                for t in range(GT):
                    dve.max(top3[:, t, :], w3b[:, t * E3:(t + 1) * E3]).then_inc(S("f3_g"), 1)
                dve.wait_ge(S("f3_g"), 9 * g + 8)
                dve.tensor_tensor(v3(gate3), v3(w3b), top3[:, :, TOPK3 - 1:TOPK3].to_broadcast([P, GT, E3]), ALU.is_ge)\
                    .then_inc(S("f3_g"), 1)
                dve.wait_ge(S("f3_g"), 9 * g + 9)
                dve.tensor_tensor(gate3, gate3, p3[j], ALU.mult).then_inc(S("f3_gate"), 1)
                dve.wait_ge(S("f3_gate"), g + 1)

            gates(0, 0)

            def body(g, j, last):
                if not last:
                    normalise(dve, s, g + 1, 1 - j)

                def hid(e):
                    n = CH3 * g + e
                    dve.wait_ge(S("f3_sil"), n + 1 + 2)
                    dve.wait_ge(S("f3_3_ps"), n + 1)
                    if e >= 2:
                        dve.wait_ge(S("f3_y_ps"), n - 1)
                    dve.tensor_tensor(hid3[e % 2], sil3[e % 2], bank(3 + e % 2), ALU.mult).then_inc(S("f3_hid"), 1)

                def add(e):
                    n = CH3 * g + e
                    dve.wait_ge(S("f3_y_ps"), n + 1)
                    for t in range(GT):
                        xt = tile_of(X, 4 * g + t)
                        if e:
                            dve.wait_ge(S("f3_x"), 4 * (E3 * g + e - 1) + t + 1)
                        dve.scalar_tensor_tensor(out=xt, in0=bank(5 + e % 2)[:, t * P:(t + 1) * P],
                                                 scalar=gate3[:, t * E3 + e:t * E3 + e + 1], in1=xt,
                                                 op0=ALU.mult, op1=ALU.add).then_inc(S("f3_x"), 1)
                    dve.wait_ge(S("f3_x"), 4 * (E3 * g + e) + 4)
                    dve.sem_inc(S("f3_y"), 1)

                hid(0)
                for e in range(1, CH3):
                    hid(e)
                    if e - 1 < E3:
                        add(e - 1)
                dve.wait_ge(S("f3_y_ps"), CH3 * g + CH3)
                xg = X[:, ds(4 * g, 4), :]
                dve.tensor_tensor(xg, xg, bank(5).rearrange("p (t n) -> p t n", t=GT), ALU.add)\
                    .then_inc(S("f3_y"), 1)
                dve.wait_ge(S("f3_y"), 9 * g + 9 + 2)
                dve.sem_inc(sem("f3", "res"), 1)
                if not last:
                    gates(g + 1, 1 - j)

            per_group(dve, body)

        def setup_dve(dve):
            dve.wait_ge(S("ld_const"), 16)
            dve.wait_ge(S("ld_once"), 16)
            dve.memset(qs[:, :], 0.0).then_inc(S("cst"), 1)
            for dst, src in ((ident16[:, :], ident), (hsel16[8][:, :], W["hsel8"]), (hsel16[64][:, :], W["hsel64"]),
                             (row0_16[:, :], W["row0"])):
                dve.tensor_copy(dst, src).then_inc(S("cst"), 1)
            dve.wait_ge(S("ld_x"), 16)
            with dve.Fori(0, N_TILES) as t:
                dve.bn_stats(tile_of(stats, t), tile_of(X, t)).then_inc(S("bn0"), 1)
            dve.wait_ge(S("bn0"), N_TILES)
            dve.sem_inc(sem("a0", "stats"), 1)

        def rows_dve(dve):
            dve.wait_ge(S("ld_rows"), 48)
            for i in range(3):
                dve.tensor_scalar(bvmat[:, i, :], ident, 0.0, col("a%d_bv" % (i + 1)), ALU.mult, ALU.add)\
                    .then_inc(S("bvm"), 1)
            dve.wait_ge(S("bvwo"), 1)
            dve.tensor_tensor(addrow[:, 0:3, :].rearrange("p i n -> p (i n)"), bank(1)[:, 0:3 * P],
                              rows_bc[:, 0:3 * P], ALU.add).then_inc(S("rw"), 1)
            dve.tensor_copy(addrow[:, 3, :], rows_bc[:, 3 * P:4 * P]).then_inc(S("rw"), 1)
            dve.tensor_copy(simw[:, :], bank(2)).then_inc(S("rw"), 1)
            dve.wait_ge(S("rw"), 3)
            dve.sem_inc(S("rows"), 1)
            dve.sem_inc(S("f2_simw"), 1)

        def rows_pe(pe):
            for k in ("a1", "a2", "a3", "f2"):
                pe.wait_ge(S("ld_" + k), 16)
            pe.wait_ge(S("bvm"), 3)
            pe.wait_ge(S("f0_go"), 1)
            for i in range(3):
                pe.matmul(bank(1)[:, i * P:(i + 1) * P], bvmat[:, i, :], W["a%d_wo" % (i + 1)], start=True, stop=True)
            for c in range(8):
                ins = pe.matmul(bank(2)[:, c * NK2:(c + 1) * NK2], W["f2_wqT"][0:64, c * P:(c + 1) * P],
                                W["f2_keysT"][0:64, c * NK2:(c + 1) * NK2], start=True, stop=True)
            ins.then_inc(S("bvwo"), 1)

        block = ctx.enter_context(nc.Block())

        @block.sync
        def _(sp):
            sp.dma_start(pack_sb["const"][:, :], dram["pack_const"]).then_inc(S("ld_const"), 16)
            sp.dma_start(pack_sb["once"][:, :], dram["pack_once"]).then_inc(S("ld_once"), 16)
            sp.dma_start(X[:, :, :], dram["x"].rearrange("(t p) d -> p t d", p=P)).then_inc(S("ld_x"), 16)
            sp.dma_start(pack_sb["a0"][:, :], dram["pack_a0"]).then_inc(S("ld_a0"), 16)
            sp.dma_start(ctxd[:, :, :, :].rearrange("p b a k -> p (b a k)"), dram["ctxd"]).then_inc(S("ld_ctx"), 16)
            sp.dma_start(mask_u8[:, :], dram["mask"]).then_inc(S("ld_mask"), 16)
            sp.dma_start(kmrow_u8[:, :], dram["kmrow"]).then_inc(S("ld_mask"), 16)
            sp.dma_start(kmT_u8[:, :], dram["kmT"]).then_inc(S("ld_mask"), 16)
            sp.dma_start(rows_bc[:, :], dram["rows"].to_broadcast([P, 4 * P])).then_inc(S("ld_rows"), 16)
            sp.dma_start(gbias3[:, :], dram["gbias"].to_broadcast([P, E3])).then_inc(S("ld_rows"), 16)
            sp.dma_start(rscale[:, :], dram["rscale"].to_broadcast([P, 1])).then_inc(S("ld_rows"), 16)
            for k in ("f0", "a1", "f1", "a2", "f2", "a3", "f3"):
                if k == "f3":
                    sp.wait_ge(sem("a1", "go"), 1)
                sp.dma_start(pack_sb[k][:, :], dram["pack_" + k]).then_inc(S("ld_" + k), 16)
            with sp.Fori(0, N_GROUPS) as g:
                sp.wait_ge(sem("f3", "res"), at("f3", "res") + g + 1 + 1)
                sp.dma_start(dram["out"].rearrange("(g t p) d -> p g t d", p=P, t=GT)[:, ds(g, 1)]
                             .rearrange("p a t d -> p (a t) d"), X[:, ds(4 * g, 4), :]).then_inc(S("stored"), 16)
            sp.wait_ge(S("stored"), 16 * N_GROUPS)

        @block.vector
        def _(dve):
            setup_dve(dve)
            for s, nxt in (("a0", "f0"), ("a1", "f1"), ("a2", "f2"), ("a3", "f3")):
                att_prep_dve(dve, atts[s])
                ln_finish_dve(dve, s)
                att_dve(dve, atts[s], nxt)
                if s == "a0":
                    f0_weights_dve(dve)
                    rows_dve(dve)
                ln_finish_dve(dve, nxt)
                {"f0": f0_dve, "f1": f1_dve, "f2": f2_dve, "f3": f3_dve}[nxt](dve)

        @block.scalar
        def _(act):
            act.wait_ge(S("cst"), 5)
            for s, nxt in (("a0", "f0"), ("a1", "f1"), ("a2", "f2"), ("a3", "f3")):
                att_prep_act(act, atts[s])
                ln_finish_act(act, s)
                att_act(act, atts[s])
                if s == "a0":
                    f0_weights_act(act)
                ln_finish_act(act, nxt)
                {"f0": f0_act, "f1": f1_act, "f2": f2_act, "f3": f3_act}[nxt](act)

        @block.tensor
        def _(pe):
            pe.wait_ge(S("cst"), 5)
            for s, nxt in (("a0", "f0"), ("a1", "f1"), ("a2", "f2"), ("a3", "f3")):
                att_prep_pe(pe, atts[s])
                att_pe(pe, atts[s])
                if s == "a0":
                    f0_weights_pe(pe)
                    pe.wait_ge(S("f0_wr"), 3)
                    rows_pe(pe)
                    pe.wait_ge(S("rows"), 1)
                {"f0": f0_pe, "f1": f1_pe, "f2": f2_pe, "f3": f3_pe}[nxt](pe)

        @block.gpsimd
        def _(pool):
            pool.wait_ge(S("ld_const"), 16)
            att_pool(pool, atts["a0"])
            f0_pool(pool)
            att_pool(pool, atts["a1"])
            att_pool(pool, atts["a2"])
            f2_pool(pool)
            att_pool(pool, atts["a3"])


def constants():
    p = np.arange(P)
    c = {"ident": np.eye(P)}
    for hd in (8, 64):
        H = D // hd
        c["kmask%d" % hd] = (p[:, None] // hd == np.arange(H)[None, :])
        c["hsel%d" % hd] = (p[:, None] == np.arange(H * SK)[None, :] // SK)
    e, hp = np.arange(64) // 32, (np.arange(64) % 16) // 8
    c["vmask8"] = (p[:, None] // SK == hp[None, :]) & ((np.arange(64) % 32 // 16)[None, :] == e[None, :])
    c["vmask64"] = p[:, None] // SK == p[None, :] // 64
    c["row0"] = np.broadcast_to(p[:, None] == 0, (P, P))
    freq = (1.0 / np.float32(10000.0) ** (np.arange(0, 8, 2, dtype=np.float32) / np.float32(8)))[(p % 8) // 2]
    for n, L in (("q", SQ), ("k", SK)):
        pos = np.float32(10.0) * (np.arange(L, dtype=np.float32) / np.float32(L))
        ang = pos[None, :] * freq[:, None].astype(np.float32)
        c["cos" + n] = np.cos(ang)
        c["sin" + n] = np.sin(ang) * np.where(p % 2 == 0, -1.0, 1.0)[:, None]
    return {k: np.asarray(v, np.float32) for k, v in c.items()}


def layout(i):
    i = {k: np.asarray(v) for k, v in i.items()}

    def rows_to_cols(w, n):
        return w.reshape(n, P, -1).transpose(1, 0, 2).reshape(P, -1)

    def swap(w):
        return w.reshape(w.shape[:-1] + (-1, 2))[..., ::-1].reshape(w.shape)

    t = constants()
    w = dict(t)
    w["a0_wq"], w["a0_wk"], w["a0_wv"] = i["L0_xattn_Wq"], i["L0_xattn_Wkv"][:, :D], i["L0_xattn_Wkv"][:, D:]
    w["a0_wo"] = i["L0_xattn_Wo"]
    w["f0_gate"], w["f0_up"] = rows_to_cols(i["L0_ffn_w_gate"], NC0), rows_to_cols(i["L0_ffn_w_up"], NC0)
    w["f0_down"] = i["L0_ffn_w_down"]
    w["a1_wq"], w["a1_wk"], w["a1_wv"], w["a1_wo"] = (i["L1_xattn_W" + k] for k in "qkvo")
    w["f1_sel"] = i["L1_ffn_expert_sel"].T
    w["f1_keys"] = i["L1_ffn_keys"].transpose(1, 0, 2).reshape(D, -1)
    w["f1_values"] = rows_to_cols(i["L1_ffn_values"].reshape(-1, D), 4)
    w["a2_wq"], w["a2_wk"], w["a2_wv"] = i["L2_xattn_Wq"], i["L2_xattn_Wkv"][:, :D], i["L2_xattn_Wkv"][:, D:]
    w["a2_wo"], w["a2_wqs"], w["a2_wks"] = i["L2_xattn_Wo"], swap(w["a2_wq"]), swap(w["a2_wk"])
    w["f2_wg"], w["f2_wu"], w["f2_wd"] = i["L2_ffn_Wg"], i["L2_ffn_Wu"], rows_to_cols(i["L2_ffn_Wd"], 4)
    half = lambda a: np.concatenate([a, a], 0)
    w["f2_wqT"] = half(i["L2_ffn_Wq"].reshape(D, 8, 64).transpose(2, 1, 0).reshape(64, -1))
    w["f2_keysT"] = half(i["L2_ffn_keys"].transpose(3, 2, 0, 1).reshape(64, -1))
    w["f2_downT"], w["f2_upE"] = i["L2_ffn_down_embed"].T, rows_to_cols(i["L2_ffn_up_embed"], 4)
    for k, n in zip("qkv", ("wq_w", "wk_w", "wv_w")):
        w["a3_w" + k] = i["L3_xattn_" + n].T
    w["a3_wo"] = i["L3_xattn_dense_w"].T
    w["f3_gate"] = i["L3_ffn_gate_w"].T
    for n in ("w1", "w3"):
        e = i["L3_ffn_" + n].transpose(2, 0, 1).reshape(D, -1)
        w["f3_" + n] = np.concatenate([e, i["L3_ffn_s" + n].T], 1)
    w["f3_w2"] = np.concatenate([i["L3_ffn_w2"].transpose(2, 0, 1).reshape(P, -1),
                                 rows_to_cols(np.ascontiguousarray(i["L3_ffn_sw2"].T), 2)], 1)
    kv = i["L2_xattn_bkv"]
    c = {"a1_bq": i["L1_xattn_bq"], "a1_bk": i["L1_xattn_bk"], "a1_bv": i["L1_xattn_bv"],
         "a2_bq": i["L2_xattn_bq"], "a2_bk": kv[:D], "a2_bv": kv[D:],
         "a2_bqs": swap(i["L2_xattn_bq"]), "a2_bks": swap(kv[:D]),
         "a3_bq": i["L3_xattn_wq_b"], "a3_bk": i["L3_xattn_wk_b"], "a3_bv": i["L3_xattn_wv_b"]}
    for j in range(4):
        c["f2_bg%d" % j] = i["L2_ffn_bg"][j * P:(j + 1) * P]
        c["f2_bu%d" % j] = i["L2_ffn_bu"][j * P:(j + 1) * P]
    cols = np.zeros((P, 24), np.float32)
    for n, name in enumerate(COLS):
        cols[:, n] = c[name]
    w["cols"] = cols
    out = {"pack_" + k: np.ascontiguousarray(np.concatenate([w[n] for n, _ in parts], 1))
           for k, parts in PACKS.items()}
    for k, parts in PACKS.items():
        assert out["pack_" + k].shape == (P, WIDTH[k]), k
    out["x"] = i["x"].reshape(B * SQ, D)
    cT = i["ctx_1024"].transpose(2, 0, 1)
    out["ctxd"] = np.ascontiguousarray(np.stack([cT, cT], 2).reshape(D, -1))
    m = i["mask_BxSxS2_bf1"].view(np.uint8)
    out["mask"] = np.ascontiguousarray(m.reshape(N_TILES, P, SK).transpose(1, 0, 2).reshape(P, -1))
    km = i["mask_BxS2_bf1"].view(np.uint8)
    out["kmrow"] = np.ascontiguousarray(km.reshape(1, -1))
    out["kmT"] = np.ascontiguousarray(np.concatenate([km.T, km.T], 0))
    out["rows"] = np.concatenate([i["L1_xattn_bo"], i["L2_xattn_bo"], i["L3_xattn_dense_b"], i["L2_ffn_bd"]])[None]
    out["gbias"] = i["L3_ffn_gate_bias"][None]
    out["rscale"] = i["L1_ffn_route_scale"][None]
    return out


def kernel(**inputs):
    import concourse.bacc as bacc
    from concourse.bass_utils import run_bass_kernel_spmd

    arrays = {k: np.ascontiguousarray(v) for k, v in layout(inputs).items()}
    nc = bacc.Bacc("TRN2", target_bir_lowering=False, num_devices=1)
    dram = {k: nc.dram_tensor("in_" + k, v.shape, mybir.dt.from_np(v.dtype), kind="ExternalInput").ap()
            for k, v in arrays.items()}
    dram["out"] = nc.dram_tensor("out", (B * SQ, D), F32, kind="ExternalOutput").ap()
    build(nc, dram)
    r = run_bass_kernel_spmd(nc, [{"in_" + k: v for k, v in arrays.items()}], core_ids=[0])
    return r.results[0]["out"].reshape(B, SQ, D)
```

```python
from contextlib import ExitStack

import concourse.bass as bass
import numpy as np
from concourse import mybir

F32 = mybir.dt.float32
BF16 = mybir.dt.bfloat16
U8 = mybir.dt.uint8
ALU = mybir.AluOpType
ACT = mybir.ActivationFunctionType
AX = mybir.AxisListType
ds = bass.ds

P = 128
B, SQ, SK, D = 16, 256, 64, 128
N_TILES = B * SQ // P
N_GROUPS = N_TILES // 4
GT = 4
GN = GT * P
LN_EPS = 1e-5
MASKED = 1e30
ROUND = 1.5 * 2.0 ** 23
QMAX16 = 2.0 ** 15 - 1.0
QMAX4 = 2.0 ** 3 - 1.0
QBLOCK = 32
TINY = 1e-12
I0 = 384
NC0 = I0 // P
MOE1_E, MOE1_H, MOE1_K = 16, 32, 4
NH2, NK2 = 4, 64
NEXP2 = 512
ROWS2 = NEXP2 // NK2
E3 = 8
TOPK3 = 2
CH3 = E3 + 2

PACKS = {
    "const": [("ident", P), ("kmask8", 16), ("kmask64", 2), ("vmask8", 64), ("vmask64", P),
              ("cosq", SQ), ("sinq", SQ), ("cosk", SK), ("sink", SK),
              ("cols", 24), ("hsel64", P)],
    "once": [("hsel8", 8 * P), ("row0", P), ("f2_wqT", 8 * P), ("f2_keysT", 8 * NK2)],
    "a0": [("a0_wq", P), ("a0_wk", P), ("a0_wv", P), ("a0_wo", P)],
    "f0": [("f0_gate", NC0 * P), ("f0_up", NC0 * P), ("f0_down", I0)],
    "a1": [("a1_wq", P), ("a1_wk", P), ("a1_wv", P), ("a1_wo", P)],
    "f1": [("f1_sel", MOE1_E), ("f1_keys", 512), ("f1_values", 512)],
    "a2": [("a2_wq", P), ("a2_wk", P), ("a2_wv", P), ("a2_wo", P), ("a2_wqs", P), ("a2_wks", P)],
    "f2": [("f2_wg", 512), ("f2_wu", 512), ("f2_wd", 512), ("f2_downT", 512), ("f2_upE", 512)],
    "a3": [("a3_wq", P), ("a3_wk", P), ("a3_wv", P), ("a3_wo", P)],
    "f3": [("f3_gate", E3), ("f3_w1", CH3 * P), ("f3_w3", CH3 * P), ("f3_w2", CH3 * P)],
}
COLS = ["a1_bq", "a1_bk", "a1_bv", "a2_bq", "a2_bk", "a2_bv", "a2_bqs", "a2_bks", "a3_bq", "a3_bk", "a3_bv",
        "f2_bg0", "f2_bg1", "f2_bg2", "f2_bg3", "f2_bu0", "f2_bu1", "f2_bu2", "f2_bu3"]
ROWS = ["a1_bo", "a2_bo", "a3_bo", "f2_bd"]
WIDTH = {k: sum(n for _, n in v) for k, v in PACKS.items()}


def build(nc, dram):
    with ExitStack() as ctx:
        def sb(name, shape, dt=F32):
            return ctx.enter_context(nc.sbuf_tensor(name, shape, dt))

        sems = {}

        def S(name):
            if name not in sems:
                sems[name] = ctx.enter_context(nc.semaphore(name))
            return sems[name]

        X = sb("X", [P, N_TILES, D])
        stats = sb("stats", [P, N_TILES, 6])
        W = {}
        pack_sb = {}
        big = sb("big", [P, 2 * N_GROUPS * NC0 * GN])
        HALF = N_GROUPS * NC0 * GN
        F0N = NC0 * GN
        tmp_all = sb("tmp", [P, 4 * F0N])
        tmp = tmp_all[:, :].rearrange("p (j i n) -> p j i n", j=2, i=2)
        shared = {"once": big[:, HALF:HALF + WIDTH["once"]], "f3": tmp_all[:, 0:WIDTH["f3"]]}
        for k, parts in PACKS.items():
            pack_sb[k] = shared[k] if k in shared else sb("w_" + k, [P, WIDTH[k]])
            at = 0
            for name, n in parts:
                W[name] = pack_sb[k][:, at:at + n]
                at += n

        def col(name):
            i = COLS.index(name)
            return W["cols"][:, i:i + 1]

        ident = W["ident"]
        ident16 = sb("ident16", [P, P], BF16)
        hsel16 = {8: sb("hsel16_8", [P, 8 * P], BF16), 64: sb("hsel16_64", [P, P], BF16)}
        row0_16 = sb("row0_16", [P, P], BF16)
        rows_bc = sb("rows_bc", [P, 4 * P])
        addrow = sb("addrow", [P, 4, P])
        bvmat = sb("bvmat", [P, 3, P])
        simw = sb("simw", [P, 512])
        gbias3 = sb("gbias3", [P, E3])
        rscale = sb("rscale", [P, 1])
        lnw = sb("lnw", [P, 10, N_TILES])
        hrow = sb("hrow", [P, 2, GN])
        hT = sb("hT", [P, 2, GN])
        qs = sb("qs", [P, 32])
        UP = big[:, 0:HALF].rearrange("p (g n) -> p g n", g=N_GROUPS)
        GATE = big[:, HALF:2 * HALF].rearrange("p (g n) -> p g n", g=N_GROUPS)
        H0 = big[:, 2 * HALF - N_GROUPS * GN:2 * HALF].rearrange("p (g n) -> p g n", g=N_GROUPS)

        class Carve:

            def __init__(self, limit=2 * HALF):
                self.at, self.limit = 0, limit

            def take(self, n, dt=F32):
                words = n if dt == F32 else (n + 1) // 2
                piece = big[:, self.at:self.at + words]
                self.at += words
                assert self.at <= self.limit
                return piece if dt == F32 else piece.bitcast(dt)[:, 0:n]

        psum = ctx.enter_context(nc.psum_tensor("psum", [P, 8, 512], F32))

        def bank(i):
            return psum[:, i, :]

        def tile_of(A, t):
            return A[:, ds(t, 1), :].rearrange("p a b -> p (a b)")

        def per_group(eng, body, first=0):
            with eng.Fori(0, N_GROUPS // 2 - 1) as k:
                for j in range(2):
                    body(2 * k + j, j, False)
            for g in (N_GROUPS - 2, N_GROUPS - 1):
                body(g, g % 2, g == N_GROUPS - 1)

        def groups2(eng, body):
            with eng.Fori(0, N_GROUPS // 2 - 1) as k:
                for j in range(2):
                    body(2 * k + j, j, True, True)
            body(N_GROUPS - 2, 0, True, False)
            body(N_GROUPS - 1, 1, False, False)

        SUB = ("a0", "f0", "a1", "f1", "a2", "f2", "a3", "f3")
        HAS_ROW = {"a1": 0, "a2": 1, "a3": 2, "f2": 3}
        ALL = dict(stats=1, ln=10, var=1, std=1, normed=N_GROUPS, turned=N_GROUPS, hT=N_GROUPS, biased=N_GROUPS,
                   res=N_GROUPS, bn=N_TILES)
        ATT = dict(go=1, k_ps=1, v_ps=4, k=2, v=4, zero=2, kv=3 * B, q_ps=B, qT=B, q16=B, mx_ps=4 * B, mx=4 * B,
                   nm_ps=B, nmT=B, st_ps=4 * B, pt=4 * B, pv=4 * B, rz=B, oT=B, o_ps=B, mask=0, r=0, prep=0)
        ATT_A0 = dict(ATT, go=0, mx_ps=2 * B, mx=2 * B, st_ps=B, pt=B, pv=B, mask=2)

        def count(s, name):
            if name in ALL:
                return 0 if name == "biased" and s not in HAS_ROW else ALL[name]
            if s[0] == "f":
                return 0
            return (ATT_A0 if s == "a0" else ATT)[name]

        def sem(s, name):
            return S("all_" + name if name in ALL else "att_" + name if s[0] == "a" else s + "_" + name)

        def at(s, name):
            if name not in ALL and s[0] == "f":
                return 0
            return sum(count(x, name) for x in SUB[:SUB.index(s)])


        def settle(eng):
            eng.sem_inc(S("settled"), 1)

        def link(eng, chain, counter):
            def step(ins):
                counter[0] += 1
                ins.then_inc(chain, 1)
                eng.wait_ge(chain, counter[0])
            return step

        mean, rstd = lnw[:, 0, :], lnw[:, 1, :]

        def ln_finish_dve(dve, s):
            me, mo, ve, vo = (stats[:, :, i] for i in (1, 4, 2, 5))
            diff, sq, var, std, y, e = (lnw[:, i, :] for i in range(2, 8))
            c = [at(s, "ln")]
            step = link(dve, sem(s, "ln"), c)
            dve.wait_ge(sem(s, "stats"), at(s, "stats") + 1)
            step(dve.tensor_tensor(mean, me, mo, ALU.add))
            step(dve.tensor_scalar(mean, mean, 0.5, None, ALU.mult))
            step(dve.tensor_tensor(diff, me, mo, ALU.subtract))
            step(dve.scalar_tensor_tensor(out=sq, in0=diff, scalar=0.25, in1=diff, op0=ALU.mult, op1=ALU.mult))
            step(dve.tensor_tensor(var, ve, vo, ALU.add))
            step(dve.scalar_tensor_tensor(out=var, in0=var, scalar=1.0 / D, in1=sq, op0=ALU.mult, op1=ALU.add))
            dve.tensor_scalar(var, var, LN_EPS, None, ALU.add).then_inc(sem(s, "var"), 1)
            dve.wait_ge(sem(s, "std"), at(s, "std") + 1)
            step(dve.reciprocal(y, std))
            step(dve.tensor_tensor(e, y, y, ALU.mult))
            step(dve.scalar_tensor_tensor(out=e, in0=e, scalar=-0.5, in1=var, op0=ALU.mult, op1=ALU.mult))
            step(dve.scalar_tensor_tensor(out=rstd, in0=e, scalar=1.5, in1=y, op0=ALU.add, op1=ALU.mult))

        def ln_finish_act(act, s):
            act.wait_ge(sem(s, "var"), at(s, "var") + 1)
            act.activation(lnw[:, 5, :], lnw[:, 4, :], ACT.Sqrt).then_inc(sem(s, "std"), 1)

        def normalise(dve, s, g, j):
            dve.wait_ge(sem(s, "turned"), at(s, "turned") + g + 1)
            for t in range(GT):
                ins = dve.tensor_scalar(hrow[:, j, t * P:(t + 1) * P], tile_of(X, 4 * g + t),
                                        mean[:, ds(4 * g + t, 1)], rstd[:, ds(4 * g + t, 1)],
                                        ALU.subtract, ALU.mult)
            ins.then_inc(sem(s, "normed"), 1)

        def turn(pe, s, g, j, bank_free=None):
            pe.wait_ge(sem(s, "normed"), at(s, "normed") + g + 1)
            if bank_free is not None:
                pe.wait_ge(*bank_free)
            for t in range(GT):
                ins = pe.transpose(bank(0)[:, t * P:(t + 1) * P], hrow[:, j, t * P:(t + 1) * P], ident)
            ins.then_inc(sem(s, "turned"), 1)

        def take_turned(act, s, g, j):
            act.wait_ge(sem(s, "turned"), at(s, "turned") + g + 1 + 2)
            act.activation(hT[:, j, :], bank(0), ACT.Copy).then_inc(sem(s, "hT"), 1)

        def residual(dve, s, g, src, last_sub, ready):
            dve.wait_ge(*ready)
            if s in HAS_ROW:
                dve.wait_ge(sem(s, "biased"), at(s, "biased") + g + 1)
            xg = X[:, ds(4 * g, 4), :]
            dve.tensor_tensor(xg, xg, src.rearrange("p (t n) -> p t n", t=GT), ALU.add).then_inc(sem(s, "res"), 1)
            tail_stats(dve, s, g, last_sub)

        def tail_stats(dve, s, g, last_sub):
            if not last_sub:
                dve.wait_ge(sem(s, "res"), at(s, "res") + g + 1 + 1)
                for t in range(GT):
                    dve.bn_stats(tile_of(stats, 4 * g + t), tile_of(X, 4 * g + t)).then_inc(sem(s, "bn"), 1)

        def stats_done(dve, s, nxt):
            dve.wait_ge(sem(s, "bn"), at(s, "bn") + N_TILES)
            dve.sem_inc(sem(nxt, "stats"), 1)

        def bias_rows(pool, s):
            row = addrow[:, HAS_ROW[s], :]
            pool.wait_ge(S("rows"), 1)
            with pool.Fori(0, N_GROUPS) as g:
                pool.wait_ge(sem(s, "normed"), at(s, "normed") + g + 1)
                xg = X[:, ds(4 * g, 4), :]
                pool.tensor_tensor(xg, xg, row.unsqueeze(1).to_broadcast([P, GT, P]), ALU.add)\
                    .then_inc(sem(s, "biased"), 1)

        class Attn:
            def __init__(self, s, hd, scale, bias, rope, mask):
                self.s, self.hd, self.scale, self.bias, self.rope, self.mask = s, hd, scale, bias, rope, mask
                self.first = s == "a0"
                self.H = D // hd
                self.C = self.H // 2
                self.NP = max(1, self.C // 2)
                self.PC = min(2, self.C)
                self.MW = min(512, self.H * SK)
                self.MH = self.MW // SK
                self.U = 2 * self.H * SK // self.MW
                self.NPT = 4 if self.NP == 4 else 2
                a = Carve(HALF if s == "a0" else 2 * HALF)
                self.kT = a.take(B * SK)
                self.V2 = a.take(B * P).rearrange("p (b n) -> p b n", b=B)
                self.kbd = [a.take(self.C * P) for _ in range(2)]
                self.kbd16 = [a.take(self.C * P, BF16) for _ in range(2)]
                self.vw = [a.take(256) for _ in range(2)]
                self.pt = [a.take(512) for _ in range(self.NPT)]
                self.qT = [a.take(256) for _ in range(2)]
                self.q16 = [a.take(256, BF16) for _ in range(2)]
                self.nm = [a.take(2 * self.H) for _ in range(2)]
                self.nmT = [a.take(256, BF16) for _ in range(2)]
                self.oT = [a.take(256) for _ in range(2)]
                self.rz = a.take(256)
                self.t1, self.t2 = a.take(512), a.take(512)
                self.m16 = a.take(N_TILES * 2 * SK, BF16).rearrange("p (t n) -> p t n", t=N_TILES)
                self.km16 = a.take(B * SK, BF16)
                self.kmT = a.take(B)
                self.end = a.at
                self.kmask = W["kmask%d" % hd]
                self.vmask = W["vmask%d" % hd]
                self.hsel = hsel16[hd]

        atts = {
            "a0": Attn("a0", 64, 64 ** -0.5, False, False, "full"),
            "a1": Attn("a1", 8, 8 ** -0.5, True, False, None),
            "a2": Attn("a2", 8, 64 ** -0.5, True, True, "keys"),
            "a3": Attn("a3", 8, 8 ** -0.5, True, False, None),
        }
        mask_u8 = sb("mask_u8", [P, N_TILES * SK], U8)
        kmrow_u8 = sb("kmrow_u8", [1, B * SK], U8)
        kmT_u8 = sb("kmT_u8", [P, B], U8)
        ctxd = sb("ctxd", [P, B, 2, SK])

        def att_prep_pe(pe, L):
            s = L.s
            pe.wait_ge(S("ld_" + s), 16)
            pe.wait_ge(S("ld_ctx"), 16)
            if s != "a0":
                pe.wait_ge(sem(s, "go"), at(s, "go") + 1)
            for i in range(2):
                ins = pe.matmul(bank(1 + i), W[s + "_wk"], ctxd[:, 8 * i:8 * i + 8, 0, :], start=True, stop=True)
                if L.rope:
                    ins = pe.matmul(bank(3 + i), W[s + "_wks"], ctxd[:, 8 * i:8 * i + 8, 0, :], start=True, stop=True)
            ins.then_inc(sem(L.s, "k_ps"), 1)
            for i in range(4):
                if i > 1:
                    pe.wait_ge(sem(L.s, "v"), at(L.s, "v") + i - 1)
                for m in range(4):
                    b = 4 * i + m
                    ins = pe.matmul(bank(5 + i % 2)[:, m * P:(m + 1) * P], ctxd[:, b].rearrange("p a k -> p (a k)"),
                                    W[s + "_wv"], start=True, stop=True)
                ins.then_inc(sem(L.s, "v_ps"), 1)

        def att_prep_act(act, L):
            act.wait_ge(sem(L.s, "k_ps"), at(L.s, "k_ps") + 1)
            if not L.rope:
                for i in range(2):
                    act.activation(L.kT[:, 512 * i:512 * i + 512], bank(1 + i), ACT.Identity,
                                   bias=col(L.s + "_bk") if L.bias else 0.0).then_inc(sem(L.s, "k"), 1)
            for i in range(4):
                act.wait_ge(sem(L.s, "v_ps"), at(L.s, "v_ps") + i + 1)
                act.activation(L.V2[:, 4 * i:4 * i + 4, :].rearrange("p b n -> p (b n)"), bank(5 + i % 2), ACT.Copy)\
                    .then_inc(sem(L.s, "v"), 1)

        def att_prep_dve(dve, L):
            c = [0]
            step = link(dve, sem(L.s, "prep"), c)
            if L.rope:
                dve.wait_ge(sem(L.s, "k_ps"), at(L.s, "k_ps") + 1)
                for i in range(2):
                    v = lambda a: a.rearrange("p (b k) -> p b k", k=SK)
                    step(dve.scalar_tensor_tensor(
                        out=v(L.t1), in0=v(bank(1 + i)), scalar=col(L.s + "_bk"),
                        in1=W["cosk"].unsqueeze(1).to_broadcast([P, 8, SK]), op0=ALU.add, op1=ALU.mult))
                    step(dve.scalar_tensor_tensor(
                        out=v(L.t2), in0=v(bank(3 + i)), scalar=col(L.s + "_bks"),
                        in1=W["sink"].unsqueeze(1).to_broadcast([P, 8, SK]), op0=ALU.add, op1=ALU.mult))
                    ins = dve.tensor_tensor(L.kT[:, 512 * i:512 * i + 512], L.t1, L.t2, ALU.add)
                    ins.then_inc(sem(L.s, "k"), 1)
                    dve.wait_ge(sem(L.s, "k"), at(L.s, "k") + i + 1)
            dve.memset(L.nmT[0], 0.0).then_inc(sem(L.s, "zero"), 1)
            dve.memset(L.nmT[1], 0.0).then_inc(sem(L.s, "zero"), 1)
            if L.mask == "full":
                dve.wait_ge(S("ld_mask"), 48)
                m = mask_u8[:, :].rearrange("p (t k) -> p t k", t=N_TILES)
                for h in range(2):
                    dve.tensor_scalar(L.m16[:, :, h * SK:(h + 1) * SK], m, 1.0, MASKED, ALU.subtract, ALU.mult)\
                        .then_inc(sem(L.s, "mask"), 1)
            if L.mask == "keys":
                dve.wait_ge(S("ld_mask"), 48)
                dve.memset(L.km16, 0.0).then_inc(sem(L.s, "mask"), 1)
                dve.wait_ge(sem(L.s, "mask"), at(L.s, "mask") + 1)
                dve.tensor_scalar(L.km16[0:1, :], kmrow_u8[:, :], 1.0, MASKED, ALU.subtract, ALU.mult)\
                    .then_inc(sem(L.s, "mask"), 1)
                dve.tensor_scalar(L.kmT, kmT_u8[:, :], 1.0, MASKED, ALU.subtract, ALU.mult)\
                    .then_inc(sem(L.s, "mask"), 1)

        def att_pool(pool, L):
            pool.wait_ge(sem(L.s, "k"), at(L.s, "k") + 2)
            pool.wait_ge(sem(L.s, "v"), at(L.s, "v") + 4)
            row = L.s in HAS_ROW
            if row:
                pool.wait_ge(S("rows"), 1)

            def batch(b, j):
                pool.wait_ge(sem(L.s, "pv"), at(L.s, "pv") + (b - 1) * L.NP + 4)
                k = L.kT[:, ds(b * SK, SK)].unsqueeze(1).to_broadcast([P, L.H, SK])
                m = L.kmask.unsqueeze(2).to_broadcast([P, L.H, SK])
                pool.tensor_tensor(L.kbd16[j].rearrange("p (h k) -> p h k", h=L.H), k, m, ALU.mult)\
                    .then_inc(sem(L.s, "kv"), 1)
                pool.tensor_tensor(L.kbd[j].rearrange("p (h k) -> p h k", h=L.H), k, m, ALU.mult)\
                    .then_inc(sem(L.s, "kv"), 1)
                v = tile_of(L.V2, b)
                if L.hd == 64:
                    pool.tensor_tensor(L.vw[j][:, 0:P], v, L.vmask, ALU.mult).then_inc(sem(L.s, "kv"), 1)
                else:
                    pool.tensor_tensor(
                        L.vw[j].rearrange("p (q e n) -> p q e n", q=4, e=2),
                        v.rearrange("p (q n) -> p q n", q=4).unsqueeze(2).to_broadcast([P, 4, 2, 32]),
                        L.vmask.rearrange("p (e n) -> p e n", e=2).unsqueeze(1).to_broadcast([P, 4, 2, 32]),
                        ALU.mult).then_inc(sem(L.s, "kv"), 1)

            def bias(g):
                pool.wait_ge(sem(L.s, "normed"), at(L.s, "normed") + g + 1)
                xg = X[:, ds(4 * g, 4), :]
                r = addrow[:, HAS_ROW[L.s], :]
                pool.tensor_tensor(xg, xg, r.unsqueeze(1).to_broadcast([P, GT, P]), ALU.add)\
                    .then_inc(sem(L.s, "biased"), 1)

            with pool.Fori(0, N_GROUPS) as g:
                batch(2 * g, 0)
                batch(2 * g + 1, 1)
                if row:
                    bias(g)

        def att_pe(pe, L):
            s = L.s
            if L.first:
                pe.sem_inc(sem(L.s, "turned"), 2)
            if L.first:
                pe.sem_inc(sem(L.s, "pv"), 4)
            if L.first:
                pe.sem_inc(sem(L.s, "o_ps"), 2)
            pe.wait_ge(sem(L.s, "zero"), at(L.s, "zero") + 2)
            if L.mask:
                pe.wait_ge(sem(L.s, "mask"), at(L.s, "mask") + 3 if L.mask == "keys" else 2)

            def T(g, j):
                turn(pe, s, g, j, None if isinstance(g, int) and g == 0 else (sem(L.s, "qT"), at(L.s, "qT") + 2 * g))

            def Q(b, g, j, odd):
                pe.wait_ge(sem(L.s, "hT"), at(L.s, "hT") + g + 1)
                if odd:
                    pe.wait_ge(sem(L.s, "qT"), at(L.s, "qT") + b)
                src = hT[:, j, 256 * odd:256 * odd + 256]
                ins = pe.matmul(bank(0)[:, 0:256], W[s + "_wq"], src, start=True, stop=True)
                if L.rope:
                    ins = pe.matmul(bank(0)[:, 256:512], W[s + "_wqs"], src, start=True, stop=True)
                ins.then_inc(sem(L.s, "q_ps"), 1)

            def MX(b, j, u):
                if u == 0:
                    pe.wait_ge(sem(L.s, "q16"), at(L.s, "q16") + b + 1)
                    pe.wait_ge(sem(L.s, "kv"), at(L.s, "kv") + 3 * b + 1)
                pe.wait_ge(sem(L.s, "mx"), at(L.s, "mx") + b * L.U + u + 1)
                t, hf = u * L.MW // (L.H * SK), u % (L.U // 2)
                out = bank(1 + u % 2)[:, 0:L.MW]
                q = L.q16[j][:, t * P:(t + 1) * P]
                rhs = L.kbd16[j][:, hf * L.MW:(hf + 1) * L.MW]
                ins = pe.matmul(out, q, rhs, start=True, stop=not L.mask)
                if L.mask == "full":
                    ins = pe.matmul(out, ident16[:, :], tile_of(L.m16, 2 * b + t), start=False, stop=True)
                if L.mask == "keys":
                    rhs = L.km16[:, ds(b * SK, SK)].unsqueeze(1).to_broadcast([P, L.MH, SK])
                    ins = pe.matmul(out.rearrange("p (h k) -> p h k", k=SK), row0_16[:, :], rhs,
                                    start=False, stop=True)
                ins.then_inc(sem(L.s, "mx_ps"), 1)

            def MXT(b, j):
                pe.wait_ge(sem(L.s, "mx"), at(L.s, "mx") + (b + 1) * L.U + 2)
                pe.wait_ge(sem(L.s, "nmT"), at(L.s, "nmT") + b + 1)
                for t in range(2):
                    ins = pe.transpose(bank(6)[0:L.H, t * P:(t + 1) * P], L.nm[j][:, t * L.H:(t + 1) * L.H], ident)
                ins.then_inc(sem(L.s, "nm_ps"), 1)

            def ST(b, j, p):
                if p == 0:
                    pe.wait_ge(sem(L.s, "nmT"), at(L.s, "nmT") + b + 1 + 1)
                    pe.wait_ge(sem(L.s, "kv"), at(L.s, "kv") + 3 * b + 2)
                pe.wait_ge(sem(L.s, "pt"), at(L.s, "pt") + b * L.NP + p + 1)
                bk = bank(3 + (p % 2 if L.NP > 1 else j))
                for e in range(L.PC):
                    c = L.PC * p + e
                    out = bk[:, 256 * e:256 * e + 256]
                    pe.matmul(out, L.kbd[j][:, c * P:(c + 1) * P], L.qT[j], start=True, stop=False)
                    if L.mask == "full":
                        for t in range(2):
                            pe.matmul(out[:, t * P:(t + 1) * P], tile_of(L.m16, 2 * b + t), ident16[:, :],
                                      start=False, stop=False)
                    ins = pe.matmul(out, L.hsel[:, c * P:(c + 1) * P], L.nmT[j], start=False, stop=True)
                ins.then_inc(sem(L.s, "st_ps"), 1)

            def PV(b, j, p):
                if p == 0:
                    pe.wait_ge(sem(L.s, "kv"), at(L.s, "kv") + 3 * b + 3)
                    pe.wait_ge(sem(L.s, "oT"), at(L.s, "oT") + b + 1)
                pe.wait_ge(sem(L.s, "pt"), at(L.s, "pt") + b * L.NP + p + 1 + 2)
                if L.NP == 1:
                    pe.matmul(bank(5)[:, 0:256], L.vw[j][:, 0:P], L.pt[j][:, 0:256], start=True, stop=True)
                    ins = pe.matmul(bank(5)[:, 256:512], L.vmask, L.pt[j][:, 0:256], start=True, stop=True)
                else:
                    rows = slice(32 * p, 32 * p + 32)
                    for half, w in ((0, L.vw[j][:, 64 * p:64 * p + 64]), (256, L.vmask)):
                        for e in range(2):
                            ins = pe.matmul(bank(5)[rows, half:half + 256], w[:, 32 * e:32 * e + 32],
                                            L.pt[p][:, 256 * e:256 * e + 256], start=(e == 0), stop=(e == 1))
                ins.then_inc(sem(L.s, "pv"), 1)

            def O(b, g, odd):
                pe.wait_ge(sem(L.s, "oT"), at(L.s, "oT") + b + 1 + 1)
                if not odd:
                    pe.wait_ge(sem(L.s, "res"), at(L.s, "res") + g + 1)
                for t in range(2):
                    ins = pe.matmul(bank(7)[:, (2 * odd + t) * P:(2 * odd + t + 1) * P],
                                    L.oT[odd][:, t * P:(t + 1) * P], W[s + "_wo"], start=True, stop=True)
                ins.then_inc(sem(L.s, "o_ps"), 1)

            T(0, 0)
            Q(0, 0, 0, 0)
            for u in range(L.U):
                MX(0, 0, u)
            MXT(0, 0)

            def body(g, jg, last, first=False):
                for odd in range(2):
                    b = 2 * g + odd
                    nb = not (last and odd)
                    ng, njg = (g, jg) if not odd else (g + 1, 1 - jg)
                    units = list(range(L.U)) if nb else []
                    if nb:
                        Q(b + 1, ng, njg, 1 - odd)
                    ST(b, odd, 0)
                    def next_maxima():
                        if units:
                            MX(b + 1, 1 - odd, units.pop(0))

                    if L.NP > 1:
                        ST(b, odd, 1)
                    if odd or not first:
                        O(b - 1, g if odd else g - 1, 1 - odd)
                    PV(b, odd, 0)
                    next_maxima()
                    if L.NP > 1:
                        ST(b, odd, 2)
                        next_maxima()
                        PV(b, odd, 1)
                        next_maxima()
                        ST(b, odd, 3)
                        next_maxima()
                        PV(b, odd, 2)
                        if not odd and not last:
                            T(g + 1, 1 - jg)
                        PV(b, odd, 3)
                        if nb:
                            MXT(b + 1, 1 - odd)
                    else:
                        while units:
                            next_maxima()
                        if not odd and not last:
                            T(g + 1, 1 - jg)
                        if nb:
                            MXT(b + 1, 1 - odd)

            body(0, 0, False, first=True)
            with pe.Fori(0, N_GROUPS // 2 - 1) as k:
                body(2 * k + 1, 1, False)
                body(2 * k + 2, 0, False)
            body(N_GROUPS - 1, 1, True)
            O(B - 1, N_GROUPS - 1, 1)

        def att_act(act, L):
            if L.first:
                act.sem_inc(sem(L.s, "nmT"), 1)
            if L.first:
                act.sem_inc(sem(L.s, "pt"), 2)
            act.activation(qs[:, 30:31], qs[:, 31:32], ACT.Exp)

            def takeQ(b, j):
                act.wait_ge(sem(L.s, "q_ps"), at(L.s, "q_ps") + b + 1)
                act.activation(L.qT[j], bank(0)[:, 0:256], ACT.Identity,
                               bias=col(L.s + "_bq") if L.bias else 0.0).then_inc(sem(L.s, "qT"), 1)

            def takeN(b, j):
                act.wait_ge(sem(L.s, "nm_ps"), at(L.s, "nm_ps") + b + 1)
                act.activation(L.nmT[j][0:L.H, :], bank(6)[0:L.H, 0:256], ACT.Copy).then_inc(sem(L.s, "nmT"), 1)

            def exp(b, j, p):
                act.wait_ge(sem(L.s, "st_ps"), at(L.s, "st_ps") + b * L.NP + p + 1)
                act.wait_ge(sem(L.s, "pv"), at(L.s, "pv") + b * L.NP + p + 1 + 4 - L.NPT)
                bk, out = (bank(3 + p % 2), L.pt[p]) if L.NP > 1 else (bank(3 + j), L.pt[j])
                n = 256 * L.PC
                if L.mask == "keys":
                    settle(act)
                bias = L.kmT[:, ds(b, 1)] if L.mask == "keys" else 0.0
                act.activation(out[:, 0:n], bk[:, 0:n], ACT.Exp, bias=bias, scale=L.scale).then_inc(sem(L.s, "pt"), 1)

            take_turned(act, L.s, 0, 0)
            if not L.rope:
                takeQ(0, 0)
            act.wait_ge(sem(L.s, "zero"), at(L.s, "zero") + 2)
            takeN(0, 0)
            if L.mask == "keys":
                act.wait_ge(sem(L.s, "mask"), at(L.s, "mask") + 3)

            def body(g, jg, last):
                for odd in range(2):
                    b = 2 * g + odd
                    nb = not (last and odd)
                    exp(b, odd, 0)
                    if nb and not L.rope:
                        takeQ(b + 1, 1 - odd)
                    for p in range(1, L.NP):
                        exp(b, odd, p)
                    if not odd and not last:
                        take_turned(act, L.s, g + 1, 1 - jg)
                    if nb:
                        takeN(b + 1, 1 - odd)

            per_group(act, body)

        def att_dve(dve, L, nxt):
            s = L.s
            if L.first:
                dve.sem_inc(sem(L.s, "mx"), 2)
            if L.first:
                dve.sem_inc(sem(L.s, "oT"), 1)
            if L.first:
                dve.sem_inc(sem(L.s, "res"), 1)

            def takeQ(b, j):
                dve.wait_ge(sem(L.s, "q_ps"), at(L.s, "q_ps") + b + 1)
                dve.scalar_tensor_tensor(out=L.t1[:, 0:256], in0=bank(0)[:, 0:256], scalar=col(s + "_bq"),
                                         in1=W["cosq"], op0=ALU.add, op1=ALU.mult).then_inc(sem(L.s, "r"), 1)
                dve.scalar_tensor_tensor(out=L.t2[:, 0:256], in0=bank(0)[:, 256:512], scalar=col(s + "_bqs"),
                                         in1=W["sinq"], op0=ALU.add, op1=ALU.mult).then_inc(sem(L.s, "r"), 1)
                dve.wait_ge(sem(L.s, "r"), at(L.s, "r") + 2 * b + 2)
                dve.tensor_tensor(L.qT[j], L.t1[:, 0:256], L.t2[:, 0:256], ALU.add).then_inc(sem(L.s, "qT"), 1)

            def q16(b, j):
                dve.wait_ge(sem(L.s, "qT"), at(L.s, "qT") + b + 1)
                dve.tensor_copy(L.q16[j], L.qT[j]).then_inc(sem(L.s, "q16"), 1)

            def mx(b, j, u):
                t, hf = u * L.MW // (L.H * SK), u % (L.U // 2)
                dve.wait_ge(sem(L.s, "mx_ps"), at(L.s, "mx_ps") + b * L.U + u + 1)
                dve.tensor_reduce(L.nm[j][:, t * L.H + hf * L.MH:t * L.H + (hf + 1) * L.MH],
                                  bank(1 + u % 2)[:, 0:L.MW].rearrange("p (h k) -> p h k", k=SK),
                                  AX.X, ALU.max, negate=True).then_inc(sem(L.s, "mx"), 1)

            def norm(b, j):
                dve.wait_ge(sem(L.s, "pv"), at(L.s, "pv") + (b + 1) * L.NP + 4)
                dve.wait_ge(sem(L.s, "o_ps"), at(L.s, "o_ps") + b + 1)
                dve.reciprocal(L.rz, bank(5)[:, 256:512]).then_inc(sem(L.s, "rz"), 1)
                dve.wait_ge(sem(L.s, "rz"), at(L.s, "rz") + b + 1)
                dve.tensor_tensor(L.oT[j], bank(5)[:, 0:256], L.rz, ALU.mult).then_inc(sem(L.s, "oT"), 1)

            def res(g):
                residual(dve, s, g, bank(7), False, (sem(L.s, "o_ps"), at(L.s, "o_ps") + 2 * g + 2 + 2))

            normalise(dve, s, 0, 0)
            if L.rope:
                takeQ(0, 0)
            q16(0, 0)
            for u in range(L.U):
                mx(0, 0, u)

            def body(g, jg, last, first=False):
                for odd in range(2):
                    b = 2 * g + odd
                    nb = not (last and odd)
                    if not odd and not last:
                        normalise(dve, s, g + 1, 1 - jg)
                    if nb:
                        if L.rope:
                            takeQ(b + 1, 1 - odd)
                        q16(b + 1, 1 - odd)
                    if not odd and not first:
                        res(g - 1)
                    if nb:
                        for u in range(L.U):
                            mx(b + 1, 1 - odd, u)
                    norm(b, odd)

            body(0, 0, False, first=True)
            cuts = [0, 1, 2, N_GROUPS // 2 - 1] if L.first else [0, N_GROUPS // 2 - 1]
            for part, (k0, k1) in enumerate(zip(cuts, cuts[1:])):
                with dve.Fori(k0, k1) as k:
                    body(2 * k + 1, 1, False)
                    body(2 * k + 2, 0, False)
                if L.first:
                    f0_weights_dve(dve, part)
                    if part == 2:
                        rows_dve(dve)
            body(N_GROUPS - 1, 1, True)
            res(N_GROUPS - 1)
            stats_done(dve, s, nxt)
            dve.sem_inc(sem(nxt, "go"), 1)

        f0w = {n: sb("f0_" + n + "T", [P, I0]) for n in ("gate", "up", "down")}
        amax = sb("amax", [P, 4, 8])
        wsc = sb("wsc", [P, 2, 12])

        def f0_weights_dve(dve, part):
            c = [6 * part]
            step = link(dve, S("f0_w"), c)
            dve.wait_ge(S("ld_f0"), 16)
            for n in (("gate", "up", "down")[part],):
                w = W["f0_" + n].rearrange("p (b k) -> p b k", k=QBLOCK)
                sc, inv = wsc[:, 0, :], wsc[:, 1, :]
                step(dve.tensor_reduce(sc, w, AX.X, ALU.max, apply_absolute_value=True))
                step(dve.tensor_scalar(sc, sc, 1.0 / QMAX4, TINY, ALU.mult, ALU.max))
                step(dve.reciprocal(inv, sc))
                step(dve.tensor_tensor(w, w, inv.unsqueeze(2).to_broadcast([P, 12, QBLOCK]), ALU.mult))
                step(dve.tensor_scalar(w, w, ROUND, ROUND, ALU.add, ALU.subtract))
                step(dve.tensor_tensor(w, w, sc.unsqueeze(2).to_broadcast([P, 12, QBLOCK]), ALU.mult))
            if part == 2:
                dve.sem_inc(S("f0_wq"), 1)

        def f0_weights_pe(pe):
            pe.wait_ge(S("f0_wq"), 1)
            for i, n in enumerate(("gate", "up", "down")):
                for c in range(NC0):
                    ins = pe.transpose(bank(1 + i)[:, c * P:(c + 1) * P], W["f0_" + n][:, c * P:(c + 1) * P], ident)
            ins.then_inc(S("f0_wT"), 1)

        def f0_weights_act(act):
            act.wait_ge(S("f0_wT"), 1)
            for i, n in enumerate(("gate", "up", "down")):
                act.activation(f0w[n][:, :], bank(1 + i)[:, 0:I0], ACT.Copy).then_inc(S("f0_wr"), 1)

        def scale_of(dve, which, n, c, step):
            for i in range(n):
                w = which + i
                step(dve.tensor_reduce(qs[:, 16 + w:17 + w], amax[:, w, :], AX.X, ALU.max))
            dve.sem_inc(S("f0_pmax"), 1)

        def scale_finish(dve, which, n, k, step):
            dve.wait_ge(S("f0_gmax"), k)
            for i in range(n):
                w = which + i
                step(dve.tensor_scalar(qs[:, 2 * w:2 * w + 1], qs[:, 20 + w:21 + w], 1.0 / QMAX16, TINY,
                                       ALU.mult, ALU.max))
                step(dve.reciprocal(qs[:, 2 * w + 1:2 * w + 2], qs[:, 2 * w:2 * w + 1]))

        def sc(w):
            return qs[:, 2 * w:2 * w + 1]

        def inv(w):
            return qs[:, 2 * w + 1:2 * w + 2]

        def f0_pool(pool):
            for k, (w, n) in enumerate(((0, 1), (1, 2), (3, 1), (0, 1))):
                pool.wait_ge(S("f0_pmax"), k + 1)
                pool.partition_all_reduce(qs[:, 20 + w:20 + w + n], qs[:, 16 + w:16 + w + n], P,
                                          bass.bass_isa.ReduceOp.max).then_inc(S("f0_gmax"), 1)

        def f0_dve(dve):
            s = "f0"
            c = [0]
            step = link(dve, S("f0_q"), c)
            with dve.Fori(0, N_GROUPS // 4) as k:
                for g in (4 * k + i for i in range(4)):
                    for t in range(GT):
                        dve.tensor_scalar(H0[:, ds(g, 1), t * P:(t + 1) * P].rearrange("p a b -> p (a b)"),
                                          tile_of(X, 4 * g + t), mean[:, ds(4 * g + t, 1)],
                                          rstd[:, ds(4 * g + t, 1)], ALU.subtract, ALU.mult).then_inc(S("f0_a"), 1)
                for g in (4 * k + i for i in range(4)):
                    dve.wait_ge(S("f0_a"), 4 * g + 4)
                    dve.tensor_reduce(amax[:, 0, ds(g, 1)], tile_of(H0, g), AX.X, ALU.max,
                                      apply_absolute_value=True).then_inc(S("f0_am"), 1)
            dve.wait_ge(S("f0_am"), N_GROUPS)
            scale_of(dve, 0, 1, c, step)
            rows_finish_dve(dve)
            scale_finish(dve, 0, 1, 1, step)

            def quant(g, j):
                dve.wait_ge(sem("f0", "turned"), at("f0", "turned") + g + 1)
                dve.tensor_scalar(hrow[:, j, :], tile_of(H0, g), inv(0), ROUND, ALU.mult, ALU.add)\
                    .then_inc(S("f0_r"), 1)
                dve.wait_ge(S("f0_r"), g + 1)
                dve.tensor_scalar(hrow[:, j, :], hrow[:, j, :], ROUND, sc(0), ALU.subtract, ALU.mult)\
                    .then_inc(sem("f0", "normed"), 1)

            quant(0, 0)
            quant(1, 1)

            def b_body(g, j, one_more, two_more):
                if two_more:
                    quant(g + 2, j)
                for i, A in ((1, GATE), (2, UP)):
                    dve.wait_ge(S("f0_gu"), 2 * g + i + 2)
                    dve.tensor_reduce(amax[:, i, ds(g, 1)], tile_of(A, g), AX.X, ALU.max,
                                      apply_absolute_value=True).then_inc(S("f0_am"), 1)

            groups2(dve, b_body)
            dve.wait_ge(S("f0_am"), 3 * N_GROUPS)
            scale_of(dve, 1, 2, c, step)
            scale_finish(dve, 1, 2, 2, step)

            def c1(g, j):
                t = tmp[:, j, 0, :]
                dve.wait_ge(S("f0_c0"), g + 1)
                dve.tensor_scalar(t, t, ROUND, sc(1), ALU.subtract, ALU.mult).then_inc(S("f0_c1"), 1)

            dve.sem_inc(S("f0_c2"), 2)
            dve.sem_inc(S("f0_cgo"), 1)
            c1(0, 0)

            def c_body(g, j, last):
                t, y = tmp[:, j, 0, :], tmp[:, j, 1, :]
                dve.wait_ge(S("f0_sig"), g + 1)
                dve.tensor_scalar(y, y, ROUND + 65535.0, ROUND, ALU.min, ALU.subtract).then_inc(S("f0_cc"), 1)
                if not last:
                    c1(g + 1, 1 - j)
                dve.wait_ge(S("f0_cc"), g + 1)
                dve.scalar_tensor_tensor(out=tile_of(GATE, g), in0=y, scalar=2.0 ** -16, in1=t,
                                         op0=ALU.mult, op1=ALU.mult).then_inc(S("f0_c2"), 1)
                dve.wait_ge(S("f0_c2"), g + 1 + 2)
                dve.tensor_reduce(amax[:, 3, ds(g, 1)], tile_of(GATE, g), AX.X, ALU.max,
                                  apply_absolute_value=True).then_inc(S("f0_am"), 1)

            per_group(dve, c_body)
            dve.wait_ge(S("f0_am"), 4 * N_GROUPS)
            scale_of(dve, 3, 1, c, step)
            scale_finish(dve, 3, 1, 3, step)
            step(dve.tensor_tensor(qs[:, 12:13], sc(3), sc(2), ALU.mult))
            dve.sem_inc(S("f0_dgo"), 1)

            dve.sem_inc(S("f0_d2"), 2)

            def d_body(g, j, last):
                t, y = tmp[:, j, 0, :], tmp[:, j, 1, :]
                dve.wait_ge(S("f0_dr"), 2 * g + 2)
                dve.tensor_scalar(t, t, ROUND, qs[:, 12:13], ALU.subtract, ALU.mult).then_inc(S("f0_d1"), 1)
                dve.wait_ge(S("f0_d1"), g + 1)
                dve.scalar_tensor_tensor(out=tile_of(GATE, g), in0=y, scalar=ROUND, in1=t,
                                         op0=ALU.subtract, op1=ALU.mult).then_inc(S("f0_d2"), 1)
                dve.wait_ge(S("f0_d2"), g + 1 + 2)
                dve.tensor_reduce(amax[:, 0, ds(g, 1)], tile_of(GATE, g), AX.X, ALU.max,
                                  apply_absolute_value=True).then_inc(S("f0_am"), 1)

            per_group(dve, d_body)
            dve.wait_ge(S("f0_am"), 5 * N_GROUPS)
            scale_of(dve, 0, 1, c, step)
            scale_finish(dve, 0, 1, 4, step)

            dve.sem_inc(S("f0_ego"), 1)

            def e1(g, j):
                t = tmp[:, j, 0, :]
                dve.wait_ge(S("f0_e"), g + 1)
                dve.tensor_scalar(t, t, ROUND, sc(0), ALU.subtract, ALU.mult).then_inc(S("f0_oq"), 1)

            e1(0, 0)

            def e_body(g, j, last):
                if not last:
                    e1(g + 1, 1 - j)
                residual(dve, s, g, bank(7), False, (S("f0_o_ps"), g + 1 + 2))

            per_group(dve, e_body)
            stats_done(dve, s, "a1")
            dve.sem_inc(sem("a1", "go"), 1)

        def f0_act(act):
            act.sem_inc(S("f0_gu"), 2)
            take_turned(act, "f0", 0, 0)

            def b_body(g, j, last):
                if not last:
                    take_turned(act, "f0", g + 1, 1 - j)
                for i, A in enumerate((GATE, UP)):
                    act.wait_ge(S("f0_gu_ps"), 2 * g + i + 1)
                    settle(act)
                    act.activation(tile_of(A, g), psum[:, 1 + 3 * i:4 + 3 * i, :].rearrange("p c n -> p (c n)"),
                                   ACT.Copy).then_inc(S("f0_gu"), 1)

            per_group(act, b_body)
            act.activation(qs[:, 30:31], qs[:, 31:32], ACT.Sigmoid)

            def rounded(out, x, w):
                return act.activation(out, x, ACT.Identity, scale=inv(w), bias=qs[:, 13:14])

            def c0(g, j):
                act.wait_ge(S("f0_c2"), g + 1)
                settle(act)
                rounded(tmp[:, j, 0, :], tile_of(GATE, g), 1).then_inc(S("f0_c0"), 1)

            act.wait_ge(S("f0_cgo"), 1)
            c0(0, 0)

            def c_body(g, j, last):
                act.wait_ge(S("f0_c1"), g + 1)
                act.activation(tmp[:, j, 1, :], tmp[:, j, 0, :], ACT.Sigmoid).then_inc(S("f0_sg"), 1)
                act.wait_ge(S("f0_sg"), g + 1)
                act.activation(tmp[:, j, 1, :], tmp[:, j, 1, :], ACT.Identity, scale=65536.0, bias=qs[:, 13:14])\
                    .then_inc(S("f0_sig"), 1)
                if not last:
                    c0(g + 1, 1 - j)

            per_group(act, c_body)
            act.wait_ge(S("f0_dgo"), 1)

            def d_body(g, j, last):
                act.wait_ge(S("f0_d2"), g + 1)
                settle(act)
                rounded(tmp[:, j, 0, :], tile_of(GATE, g), 3).then_inc(S("f0_dr"), 1)
                rounded(tmp[:, j, 1, :], tile_of(UP, g), 2).then_inc(S("f0_dr"), 1)

            per_group(act, d_body)
            act.wait_ge(S("f0_ego"), 1)

            def e_body(g, j, last):
                act.wait_ge(S("f0_o_ps"), g + 1)
                settle(act)
                rounded(tmp[:, j, 0, :], tile_of(GATE, g), 0).then_inc(S("f0_e"), 1)

            per_group(act, e_body)

        def f0_pe(pe):
            pe.wait_ge(S("f0_wr"), 3)
            turn(pe, "f0", 0, 0)

            def b_body(g, j, last):
                if not last:
                    turn(pe, "f0", g + 1, 1 - j, (sem("f0", "hT"), at("f0", "hT") + g + 1))
                pe.wait_ge(sem("f0", "hT"), at("f0", "hT") + g + 1)
                for i, n in enumerate(("gate", "up")):
                    pe.wait_ge(S("f0_gu"), 2 * g + i + 1)
                    for c in range(NC0):
                        ins = pe.matmul(bank(1 + 3 * i + c), f0w[n][:, c * P:(c + 1) * P], hT[:, j, :],
                                        start=True, stop=True)
                    ins.then_inc(S("f0_gu_ps"), 1)

            per_group(pe, b_body)
            pe.sem_inc(S("f0_o_ps"), 2)

            def e_body(g, j, last):
                pe.wait_ge(S("f0_oq"), g + 1)
                pe.wait_ge(sem("f0", "res"), at("f0", "res") + g + 1)
                for t in range(GT):
                    for c in range(NC0):
                        ins = pe.matmul(bank(7)[:, t * P:(t + 1) * P],
                                        tmp[:, j, 0, c * GN + t * P:c * GN + (t + 1) * P],
                                        f0w["down"][:, c * P:(c + 1) * P], start=(c == 0), stop=(c == NC0 - 1))
                ins.then_inc(S("f0_o_ps"), 1)

            per_group(pe, e_body)

        f1 = Carve()
        prob1 = [f1.take(GT * MOE1_E) for _ in range(2)]
        top1 = f1.take(GT * 8).rearrange("p (t k) -> p t k", t=GT)
        f1s = f1.take(GT * 2).rearrange("p (i t) -> p i t", i=2)
        gate1 = f1.take(GT * MOE1_E)
        hid1 = [f1.take(512) for _ in range(2)]
        hidT1 = [f1.take(512) for _ in range(2)]

        def f1_pe(pe):
            s = "f1"
            pe.wait_ge(S("ld_f1"), 16)
            turn(pe, s, 0, 0)

            def logits(g, j):
                pe.wait_ge(sem("f1", "hT"), at("f1", "hT") + g + 1)
                pe.wait_ge(S("f1_prob"), g + 1)
                for t in range(GT):
                    ins = pe.matmul(bank(1)[:, t * MOE1_E:(t + 1) * MOE1_E], hT[:, j, t * P:(t + 1) * P],
                                    W["f1_sel"], start=True, stop=True)
                ins.then_inc(S("f1_lg"), 1)

            logits(0, 0)

            def body(g, j, last):
                if not last:
                    turn(pe, s, g + 1, 1 - j, (sem("f1", "hT"), at("f1", "hT") + g + 1))

                def keys(t):
                    pe.wait_ge(S("f1_hid"), 4 * g + t + 1)
                    pe.matmul(bank(2 + t % 2), hT[:, j, t * P:(t + 1) * P], W["f1_keys"], start=True, stop=True)\
                        .then_inc(S("f1_h_ps"), 1)

                def tr(t):
                    pe.wait_ge(S("f1_hid"), 4 * g + t + 1 + 2)
                    pe.wait_ge(S("f1_hidT"), 4 * g + t + 1)
                    for c in range(4):
                        ins = pe.transpose(bank(4 + t % 2)[:, c * P:(c + 1) * P], hid1[t % 2][:, c * P:(c + 1) * P],
                                           ident)
                    ins.then_inc(S("f1_tr"), 1)

                def val(t):
                    if t == 0:
                        pe.wait_ge(sem("f1", "res"), at("f1", "res") + g + 1)
                    pe.wait_ge(S("f1_hidT"), 4 * g + t + 1 + 2)
                    for c in range(4):
                        ins = pe.matmul(bank(7)[:, t * P:(t + 1) * P], hidT1[t % 2][:, c * P:(c + 1) * P],
                                        W["f1_values"][:, c * P:(c + 1) * P], start=(c == 0), stop=(c == 3))
                    ins.then_inc(S("f1_val"), 1)

                keys(0)
                keys(1)
                tr(0)
                keys(2)
                tr(1)
                if not last:
                    logits(g + 1, 1 - j)
                val(0)
                keys(3)
                tr(2)
                val(1)
                tr(3)
                val(2)
                val(3)

            per_group(pe, body)

        def f1_act(act):
            act.sem_inc(S("f1_prob"), 1)
            act.sem_inc(S("f1_hidT"), 2)
            act.activation(qs[:, 30:31], qs[:, 31:32], ACT.Sigmoid)
            take_turned(act, "f1", 0, 0)

            def probs(g, j):
                act.wait_ge(S("f1_lg"), g + 1)
                act.activation(prob1[j], bank(1)[:, 0:GT * MOE1_E], ACT.Sigmoid).then_inc(S("f1_prob"), 1)

            probs(0, 0)

            def body(g, j, last):
                if not last:
                    take_turned(act, "f1", g + 1, 1 - j)
                for t in range(GT):
                    act.wait_ge(S("f1_tr"), 4 * g + t + 1)
                    if t >= 2:
                        act.wait_ge(S("f1_val"), 4 * g + t - 1)
                    act.activation(hidT1[t % 2], bank(4 + t % 2), ACT.Copy).then_inc(S("f1_hidT"), 1)
                    if t == 1 and not last:
                        probs(g + 1, 1 - j)

            per_group(act, body)

        def f1_dve(dve):
            s = "f1"
            dve.sem_inc(S("f1_hid"), 2)
            normalise(dve, s, 0, 0)
            normalise(dve, s, 1, 1)

            def gates(g, j):
                pr = prob1[j].rearrange("p (t e) -> p t e", t=GT)
                ga = gate1.rearrange("p (t e) -> p t e", t=GT)
                dve.wait_ge(S("f1_prob"), g + 1 + 1)
                settle(dve)
                for t in range(GT):
                    dve.max(top1[:, t, :], pr[:, t, :]).then_inc(S("f1_top"), 1)
                dve.wait_ge(S("f1_top"), 4 * g + 4)
                dve.tensor_reduce(f1s[:, 0, :], top1[:, :, 0:MOE1_K], AX.X, ALU.add).then_inc(S("f1_g"), 1)
                dve.tensor_tensor(ga, pr, top1[:, :, MOE1_K - 1:MOE1_K].to_broadcast([P, GT, MOE1_E]), ALU.is_ge)\
                    .then_inc(S("f1_g"), 1)
                dve.wait_ge(S("f1_g"), 6 * g + 1)
                dve.tensor_scalar(f1s[:, 0, :], f1s[:, 0, :], 1e-9, None, ALU.max).then_inc(S("f1_g"), 1)
                dve.wait_ge(S("f1_g"), 6 * g + 3)
                dve.reciprocal(f1s[:, 1, :], f1s[:, 0, :]).then_inc(S("f1_g"), 1)
                dve.tensor_tensor(ga, ga, pr, ALU.mult).then_inc(S("f1_g"), 1)
                dve.wait_ge(S("f1_g"), 6 * g + 5)
                dve.scalar_tensor_tensor(out=ga, in0=ga, scalar=rscale[:, 0:1],
                                         in1=f1s[:, 1, :].unsqueeze(2).to_broadcast([P, GT, MOE1_E]),
                                         op0=ALU.mult, op1=ALU.mult).then_inc(S("f1_g"), 1)
                dve.wait_ge(S("f1_g"), 6 * g + 6)

            gates(0, 0)
            ga = gate1.rearrange("p (t e) -> p t e", t=GT)

            def hidden(g, t):
                dve.wait_ge(S("f1_h_ps"), 4 * g + t + 1)
                if t >= 2:
                    dve.wait_ge(S("f1_tr"), 4 * g + t - 1)
                dve.scalar_tensor_tensor(out=hid1[t % 2].rearrange("p (e h) -> p e h", h=MOE1_H),
                                         in0=bank(2 + t % 2).rearrange("p (e h) -> p e h", h=MOE1_H), scalar=0.0,
                                         in1=ga[:, t, :].unsqueeze(2).to_broadcast([P, MOE1_E, MOE1_H]),
                                         op0=ALU.max, op1=ALU.mult).then_inc(S("f1_hid"), 1)

            def res(g):
                residual(dve, s, g, bank(7), False, (S("f1_val"), 4 * g + 4))

            def body(g, j):
                fixed = isinstance(g, int)
                hidden(g, 0)
                hidden(g, 1)
                if not (fixed and g == 0):
                    res(g - 1)
                hidden(g, 2)
                hidden(g, 3)
                if not (fixed and g == N_GROUPS - 1):
                    gates(g + 1, 1 - j)
                if not (fixed and g >= N_GROUPS - 2):
                    normalise(dve, s, g + 2, j)

            body(0, 0)
            with dve.Fori(0, 2) as k:
                body(2 * k + 1, 1)
                body(2 * k + 2, 0)
            for g in range(5, N_GROUPS):
                body(g, g % 2)
            res(N_GROUPS - 1)
            stats_done(dve, s, "a2")
            dve.sem_inc(sem("a2", "go"), 1)

        f2 = Carve()
        sim = f2.take(GT * 512)
        ssum = [f2.take(NH2 * 512) for _ in range(GT)]
        ew_all = f2.take(GT * NH2 * 512)
        ew = [ew_all[:, t * NH2 * 512:(t + 1) * NH2 * 512] for t in range(GT)]
        ew_v = ew_all.rearrange("p (t n) -> p t n", t=GT)
        acc2 = ew_v[:, :, 0:512]
        aT = f2.take(4 * 512).rearrange("p (c n) -> p c n", c=4)
        sg = [f2.take(512) for _ in range(GT)]
        pwT = [f2.take(512) for _ in range(2)]
        sl = [f2.take(512) for _ in range(2)]
        f2_small = [WIDTH["f3"]]

        def small(n):
            f2_small[0] += n
            assert f2_small[0] <= 4 * F0N
            return tmp_all[:, f2_small[0] - n:f2_small[0]]

        top2 = small(GT * 8 * 8).rearrange("p (t c k) -> p t c k", t=GT, c=8)
        pair2 = small(GT * 4 * 64).rearrange("p (t h n) -> p t h n", t=GT, h=NH2)
        best2 = small(GT * 4 * 8).rearrange("p (t h k) -> p t h k", t=GT, h=NH2)
        e8 = small(GT * 4 * 8).rearrange("p (t h k) -> p t h k", t=GT, h=NH2)
        z2, lnz2, shift2, tots2 = (small(GT * NH2) for _ in range(4))
        tot2 = small(GT)

        def f2_pe(pe):
            s = "f2"

            def T(G, j, first=False):
                turn(pe, s, G, j, None if first else (sem(s, "hT"), at(s, "hT") + G))

            def sims(G, j, t):
                pe.wait_ge(sem(s, "hT"), at(s, "hT") + G + 1)
                pe.wait_ge(S("f2_sim"), 4 * G + t + 1)
                pe.matmul(bank(1 + t % 2), hT[:, j, t * P:(t + 1) * P], simw[:, :], start=True, stop=True)\
                    .then_inc(S("f2_sim_ps"), 1)

            pe.wait_ge(S("f2_simw"), 1)
            T(0, 0, first=True)
            for t in range(GT):
                sims(0, 0, t)
            T(1, 1)
            for t in range(GT):
                sims(1, 1, t)

            def body(g, j, one_more, two_more):
                for c in range(4):
                    pe.wait_ge(S("f2_sl"), 4 * g + c + 1)
                    pe.matmul(bank(3), W["f2_wg"][:, c * P:(c + 1) * P], hT[:, j, :], start=True, stop=True)\
                        .then_inc(S("f2_g_ps"), 1)
                    pe.wait_ge(S("f2_sg"), 4 * g + c + 1)
                    pe.matmul(bank(5), hT[:, j, c * P:(c + 1) * P], W["f2_downT"], start=True, stop=True)\
                        .then_inc(S("f2_e_ps"), 1)
                    if c >= 2:
                        pe.wait_ge(S("f2_aT"), 4 * g + c)
                    pe.matmul(bank(4 + 2 * (c % 2)), W["f2_wu"][:, c * P:(c + 1) * P], hT[:, j, :],
                              start=True, stop=True)\
                        .then_inc(S("f2_u_ps"), 1)
                if two_more:
                    T(g + 2, j)
                pe.wait_ge(sem(s, "res"), at(s, "res") + g + 1)
                pe.wait_ge(S("f2_aT"), 4 * g + 4 + 1)
                for t in range(GT):
                    for c in range(4):
                        pe.matmul(bank(7)[:, t * P:(t + 1) * P], aT[:, c, t * P:(t + 1) * P],
                                  W["f2_wd"][:, c * P:(c + 1) * P], start=(t == 0 and c == 0), stop=False,
                                  skip_group_check=True)

                def turn_weights(t):
                    pe.wait_ge(S("f2_pw"), 4 * g + t + 1)
                    for c in range(4):
                        ins = pe.transpose(bank(6 - 2 * (t % 2))[:, c * P:(c + 1) * P], sg[t][:, c * P:(c + 1) * P],
                                           ident)
                    ins.then_inc(S("f2_tr"), 1)
                    if two_more:
                        sims(g + 2, j, t)

                def rows_out(t):
                    pe.wait_ge(S("f2_pwT"), 4 * g + t + 1)
                    for c in range(4):
                        ins = pe.matmul(bank(7)[:, t * P:(t + 1) * P], pwT[t % 2][:, c * P:(c + 1) * P],
                                        W["f2_upE"][:, c * P:(c + 1) * P], start=False, stop=(c == 3 and t == GT - 1),
                                        skip_group_check=True)
                    ins.then_inc(S("f2_o_ps"), 1)

                turn_weights(0)
                turn_weights(1)
                for t in range(GT):
                    rows_out(t)
                    if t + 2 < GT:
                        turn_weights(t + 2)

            groups2(pe, body)

        def f2_act(act):
            s = "f2"
            act.sem_inc(S("f2_sim"), 2)
            act.sem_inc(S("f2_sl"), 1)
            act.sem_inc(S("f2_sg"), 1)
            take_turned(act, s, 0, 0)

            def sims(G, t, before=None):
                act.wait_ge(S("f2_sim_ps"), 4 * G + t + 1)
                if before is not None:
                    act.wait_ge(S("f2_S"), 4 * before + t + 1)
                    act.wait_ge(S("f2_t1"), 32 * before + 8 * t + 8)
                act.activation(sim[:, t * 512:(t + 1) * 512], bank(1 + t % 2), ACT.Copy).then_inc(S("f2_sim"), 1)

            def logs(G):
                act.wait_ge(S("f2_m"), G + 1)
                act.activation(e8.rearrange("p t h k -> p (t h k)"), e8.rearrange("p t h k -> p (t h k)"), ACT.Exp)\
                    .then_inc(S("f2_e8"), 1)

            def logz(G):
                act.wait_ge(S("f2_z"), G + 1)
                act.activation(lnz2, z2, ACT.Ln).then_inc(S("f2_lnz"), 1)

            def exps(G, t, before=None):
                if t == 0:
                    act.wait_ge(S("f2_shift"), G + 1)
                act.wait_ge(S("f2_S"), 4 * G + t + 1)
                if before is not None:
                    act.wait_ge(S("f2_pw"), 4 * before + t + 1)
                for h in range(NH2):
                    ins = act.activation(ew[t][:, h * 512:(h + 1) * 512], ssum[t][:, h * 512:(h + 1) * 512],
                                         ACT.Exp, bias=shift2[:, t * NH2 + h:t * NH2 + h + 1])
                ins.then_inc(S("f2_ew"), 1)

            for t in range(GT):
                sims(0, t)
            take_turned(act, s, 1, 1)
            logs(0)
            logz(0)
            for t in range(GT):
                exps(0, t)
                sims(1, t, 0)

            def body(g, j, one_more, two_more):
                for c in range(4):
                    act.wait_ge(S("f2_g_ps"), 4 * g + c + 1)
                    if c:
                        act.wait_ge(S("f2_aT"), 4 * g + c)
                    act.activation(sl[c % 2], bank(3), ACT.Silu, bias=col("f2_bg%d" % c)).then_inc(S("f2_sl"), 1)
                    act.wait_ge(S("f2_e_ps"), 4 * g + c + 1)
                    act.activation(sg[c], bank(5), ACT.Silu).then_inc(S("f2_sg"), 1)
                if one_more:
                    logs(g + 1)
                if two_more:
                    take_turned(act, s, g + 2, j)
                if one_more:
                    logz(g + 1)
                for t in range(GT):
                    if one_more:
                        exps(g + 1, t, g)
                    act.wait_ge(S("f2_tr"), 4 * g + t + 1)
                    act.activation(pwT[t % 2], bank(6 - 2 * (t % 2)), ACT.Copy).then_inc(S("f2_pwT"), 1)
                    if two_more:
                        sims(g + 2, t, g + 1)

            groups2(act, body)

        def f2_pool(pool):
            s = "f2"
            row = addrow[:, HAS_ROW[s], :]

            def pairs(G, t, before=None):
                pool.wait_ge(S("f2_sim"), 4 * G + t + 1 + 2)
                if before is not None:
                    pool.wait_ge(S("f2_mw"), 16 * before + 4 * t + 4)
                st = sim[:, t * 512:(t + 1) * 512].rearrange("p (c h k) -> p c h k", c=2, h=NH2)
                for h in range(NH2):
                    ins = pool.tensor_tensor(
                        ssum[t][:, h * 512:(h + 1) * 512].rearrange("p (i j) -> p i j", i=ROWS2),
                        st[:, 0, h, 0:ROWS2].unsqueeze(2).to_broadcast([P, ROWS2, NK2]),
                        st[:, 1, h, :].unsqueeze(1).to_broadcast([P, ROWS2, NK2]), ALU.add)
                ins.then_inc(S("f2_S"), 1)

            def fold(G, t):
                pool.wait_ge(S("f2_mw"), 16 * G + 4 * t + 4)
                pool.tensor_tensor(ew[t][:, 0:1024], ew[t][:, 0:1024], ew[t][:, 1024:2048], ALU.add)\
                    .then_inc(S("f2_fold"), 1)

            def bias(g):
                pool.wait_ge(sem(s, "normed"), at(s, "normed") + g + 1)
                xg = X[:, ds(4 * g, 4), :]
                pool.tensor_tensor(xg, xg, row.unsqueeze(1).to_broadcast([P, GT, P]), ALU.add)\
                    .then_inc(sem(s, "biased"), 1)

            def fold_and_pairs(G, more):
                fold(G, 0)
                fold(G, 1)
                if more:
                    pairs(G + 1, 0, G)
                fold(G, 2)
                fold(G, 3)
                if more:
                    for t in range(1, GT):
                        pairs(G + 1, t, G)

            for t in range(GT):
                pairs(0, t)
            with pool.Fori(0, N_GROUPS - 1) as g:
                bias(g)
                fold_and_pairs(g, True)
            bias(N_GROUPS - 1)
            fold_and_pairs(N_GROUPS - 1, False)

        def f2_dve(dve):
            s = "f2"
            dve.sem_inc(S("f2_aT"), 1)
            normalise(dve, s, 0, 0)
            normalise(dve, s, 1, 1)

            def top(G, t):
                dve.wait_ge(S("f2_sim"), 4 * G + t + 1 + 2)
                settle(dve)
                for c in range(8):
                    dve.max(top2[:, t, c, :], sim[:, t * 512 + c * 64:t * 512 + (c + 1) * 64])\
                        .then_inc(S("f2_t1"), 1)
                dve.wait_ge(S("f2_t1"), 32 * G + 8 * t + 8)
                dve.tensor_tensor(pair2[:, t].rearrange("p h (a b) -> p h a b", a=8),
                                  top2[:, t, 0:4, :].unsqueeze(3).to_broadcast([P, NH2, 8, 8]),
                                  top2[:, t, 4:8, :].unsqueeze(2).to_broadcast([P, NH2, 8, 8]), ALU.add)\
                    .then_inc(S("f2_t2"), 1)

            def best(G, t):
                dve.wait_ge(S("f2_t2"), 4 * G + t + 1)
                settle(dve)
                for h in range(NH2):
                    dve.max(best2[:, t, h, :], pair2[:, t, h, :]).then_inc(S("f2_t3"), 1)

            def less_best(G):
                dve.wait_ge(S("f2_t3"), 16 * G + 16)
                dve.tensor_tensor(e8, best2, best2[:, :, :, 0:1].to_broadcast([P, GT, NH2, 8]), ALU.subtract)\
                    .then_inc(S("f2_m"), 1)

            def z(G):
                dve.wait_ge(S("f2_e8"), G + 1)
                dve.tensor_reduce(z2.rearrange("p (t h) -> p t h", t=GT), e8, AX.X, ALU.add).then_inc(S("f2_z"), 1)

            def shift(G):
                dve.wait_ge(S("f2_lnz"), G + 1)
                dve.scalar_tensor_tensor(out=shift2.rearrange("p (t h) -> p t h", t=GT), in0=best2[:, :, :, 0],
                                         scalar=-1.0, in1=lnz2.rearrange("p (t h) -> p t h", t=GT),
                                         op0=ALU.mult, op1=ALU.subtract).then_inc(S("f2_shift"), 1)

            def weigh(G, t):
                dve.wait_ge(S("f2_ew"), 4 * G + t + 1)
                for h in range(NH2):
                    blk = slice(h * 512, (h + 1) * 512)
                    dve.scalar_tensor_tensor(out=ew[t][:, blk], in0=ssum[t][:, blk], scalar=best2[:, t, h, 7:8],
                                             in1=ew[t][:, blk], op0=ALU.is_ge, op1=ALU.mult,
                                             accum_out=tots2[:, t * NH2 + h:t * NH2 + h + 1])\
                        .then_inc(S("f2_mw"), 1)

            def total(G):
                dve.wait_ge(S("f2_mw"), 16 * G + 16)
                dve.tensor_reduce(tot2, tots2.rearrange("p (t h) -> p t h", t=GT), AX.X, ALU.add)\
                    .then_inc(S("f2_tt"), 1)
                dve.wait_ge(S("f2_fold"), 4 * G + 4)
                dve.tensor_tensor(acc2, acc2, ew_v[:, :, 512:1024], ALU.add).then_inc(S("f2_tt"), 1)
                dve.wait_ge(S("f2_tt"), 4 * G + 1)
                dve.tensor_scalar(tot2, tot2, -1.0, float(NH2), ALU.mult, ALU.add).then_inc(S("f2_tt"), 1)
                dve.wait_ge(S("f2_tt"), 4 * G + 3)
                last_col = acc2[:, :, NEXP2 - 1]
                dve.tensor_tensor(last_col, last_col, tot2, ALU.add).then_inc(S("f2_tt"), 1)

            for t in range(GT):
                top(0, t)
            for t in range(GT):
                best(0, t)
            less_best(0)
            z(0)
            shift(0)
            for t in range(GT):
                weigh(0, t)

            def body(g, j, one_more, two_more):
                if one_more:
                    top(g + 1, 0)
                for c in range(4):
                    n = 4 * g + c
                    dve.wait_ge(S("f2_sl"), n + 1 + 1)
                    dve.wait_ge(S("f2_u_ps"), n + 1)
                    dve.scalar_tensor_tensor(out=aT[:, c, :], in0=bank(4 + 2 * (c % 2)),
                                             scalar=col("f2_bu%d" % c), in1=sl[c % 2],
                                             op0=ALU.add, op1=ALU.mult).then_inc(S("f2_aT"), 1)
                    if one_more:
                        best(g + 1, c)
                        if c < 3:
                            top(g + 1, c + 1)
                if one_more:
                    less_best(g + 1)
                if two_more:
                    normalise(dve, s, g + 2, j)
                total(g)
                if one_more:
                    z(g + 1)
                dve.wait_ge(S("f2_tt"), 4 * g + 4)

                def pw(t):
                    dve.wait_ge(S("f2_sg"), 4 * g + t + 1 + 1)
                    dve.tensor_tensor(sg[t], acc2[:, t, :], sg[t], ALU.mult).then_inc(S("f2_pw"), 1)

                pw(0)
                pw(1)
                if one_more:
                    shift(g + 1)
                pw(2)
                pw(3)
                if one_more:
                    for t in range(GT):
                        weigh(g + 1, t)
                residual(dve, s, g, bank(7), False, (S("f2_o_ps"), 4 * g + 4))

            groups2(dve, body)
            stats_done(dve, s, "a3")
            dve.sem_inc(sem("a3", "go"), 1)

        f3 = Carve()
        p3 = [f3.take(GT * E3) for _ in range(2)]
        w3b = f3.take(GT * E3)
        top3 = f3.take(GT * 8).rearrange("p (t k) -> p t k", t=GT)
        s3 = f3.take(GT * 4).rearrange("p (i t) -> p i t", i=4)
        gate3 = f3.take(GT * E3)
        sil3 = [f3.take(512) for _ in range(2)]
        hid3 = [f3.take(512) for _ in range(2)]

        def f3_pe(pe):
            s = "f3"
            pe.wait_ge(S("ld_f3"), 16)
            turn(pe, s, 0, 0)

            def logits(g, j):
                pe.wait_ge(sem("f3", "hT"), at("f3", "hT") + g + 1)
                pe.wait_ge(S("f3_p"), g + 1)
                for t in range(GT):
                    ins = pe.matmul(bank(7)[:, t * E3:(t + 1) * E3], hT[:, j, t * P:(t + 1) * P], W["f3_gate"],
                                    start=True, stop=True)
                ins.then_inc(S("f3_lg"), 1)

            logits(0, 0)

            def body(g, j, last):
                def up(e):
                    n = CH3 * g + e
                    pe.wait_ge(S("f3_sil"), n + 1)
                    pe.matmul(bank(1 + e % 2), W["f3_w1"][:, e * P:(e + 1) * P], hT[:, j, :], start=True, stop=True)\
                        .then_inc(S("f3_1_ps"), 1)
                    pe.wait_ge(S("f3_hid"), n + 1)
                    pe.matmul(bank(3 + e % 2), W["f3_w3"][:, e * P:(e + 1) * P], hT[:, j, :], start=True, stop=True)\
                        .then_inc(S("f3_3_ps"), 1)

                def down(e):
                    n = CH3 * g + e
                    pe.wait_ge(S("f3_hid"), n + 1 + 2)
                    if e < CH3 - 1:
                        pe.wait_ge(S("f3_y"), 9 * g + (e + 1 if e else 2))
                    bk = bank(5 + min(e, E3) % 2)
                    for t in range(GT):
                        ins = pe.matmul(bk[:, t * P:(t + 1) * P], hid3[e % 2][:, t * P:(t + 1) * P],
                                        W["f3_w2"][:, e * P:(e + 1) * P], start=True, stop=True) \
                            if e < E3 else \
                            pe.matmul(bk[:, t * P:(t + 1) * P], hid3[e % 2][:, t * P:(t + 1) * P],
                                      W["f3_w2"][:, e * P:(e + 1) * P], start=(e == E3 and t == 0),
                                      stop=(e == E3 + 1), skip_group_check=True)
                    ins.then_inc(S("f3_y_ps"), 1)

                up(0)
                for e in range(1, CH3):
                    up(e)
                    down(e - 1)
                    if e == 4 and not last:
                        turn(pe, s, g + 1, 1 - j, (sem("f3", "hT"), at("f3", "hT") + g + 1))
                    if e == CH3 - 2 and not last:
                        logits(g + 1, 1 - j)
                down(CH3 - 1)

            per_group(pe, body)

        def f3_act(act):
            act.sem_inc(S("f3_p"), 1)
            act.sem_inc(S("f3_sil"), 2)
            take_turned(act, "f3", 0, 0)

            def probs(g, j):
                act.wait_ge(S("f3_mx"), g + 1)
                act.activation(p3[j], p3[j], ACT.Exp).then_inc(S("f3_ex"), 1)

            probs(0, 0)

            def body(g, j, last):
                for e in range(CH3):
                    n = CH3 * g + e
                    act.wait_ge(S("f3_1_ps"), n + 1)
                    act.wait_ge(S("f3_hid"), n + 1)
                    act.activation(sil3[e % 2], bank(1 + e % 2), ACT.Silu).then_inc(S("f3_sil"), 1)
                    if e == 4 and not last:
                        take_turned(act, "f3", g + 1, 1 - j)
                if not last:
                    probs(g + 1, 1 - j)

            per_group(act, body)

        def f3_dve(dve):
            s = "f3"
            dve.wait_ge(S("ld_rows"), 48)
            for n, v in (("hid", 2), ("y", 2)):
                dve.sem_inc(S("f3_" + n), v)
            normalise(dve, s, 0, 0)
            normalise(dve, s, 1, 1)
            v3 = lambda a: a.rearrange("p (t e) -> p t e", t=GT)
            bc = lambda a: a.unsqueeze(2).to_broadcast([P, GT, E3])

            def gates(g, j):
                dve.wait_ge(S("f3_lg"), g + 1)
                dve.tensor_reduce(s3[:, 0, :], v3(bank(7)[:, 0:GT * E3]), AX.X, ALU.max).then_inc(S("f3_g"), 1)
                dve.wait_ge(S("f3_g"), 9 * g + 1)
                dve.tensor_tensor(v3(p3[j]), v3(bank(7)[:, 0:GT * E3]), bc(s3[:, 0, :]), ALU.subtract)\
                    .then_inc(S("f3_mx"), 1)
                dve.wait_ge(S("f3_ex"), g + 1)
                dve.tensor_reduce(s3[:, 1, :], v3(p3[j]), AX.X, ALU.add).then_inc(S("f3_g"), 1)
                dve.wait_ge(S("f3_g"), 9 * g + 2)
                dve.reciprocal(s3[:, 2, :], s3[:, 1, :]).then_inc(S("f3_g"), 1)
                dve.wait_ge(S("f3_g"), 9 * g + 3)
                dve.tensor_tensor(v3(p3[j]), v3(p3[j]), bc(s3[:, 2, :]), ALU.mult).then_inc(S("f3_p"), 1)
                dve.wait_ge(S("f3_p"), g + 1 + 1)
                dve.tensor_tensor(v3(w3b), v3(p3[j]), gbias3[:, :].unsqueeze(1).to_broadcast([P, GT, E3]), ALU.add)\
                    .then_inc(S("f3_g"), 1)
                dve.wait_ge(S("f3_g"), 9 * g + 4)
                settle(dve)
                for t in range(GT):
                    dve.max(top3[:, t, :], w3b[:, t * E3:(t + 1) * E3]).then_inc(S("f3_g"), 1)
                dve.wait_ge(S("f3_g"), 9 * g + 8)
                dve.tensor_tensor(v3(gate3), v3(w3b), top3[:, :, TOPK3 - 1:TOPK3].to_broadcast([P, GT, E3]), ALU.is_ge)\
                    .then_inc(S("f3_g"), 1)
                dve.wait_ge(S("f3_g"), 9 * g + 9)
                dve.tensor_tensor(gate3, gate3, p3[j], ALU.mult).then_inc(S("f3_gate"), 1)
                dve.wait_ge(S("f3_gate"), g + 1)

            gates(0, 0)

            def body(g, j, one_more, two_more):
                def hid(e):
                    n = CH3 * g + e
                    dve.wait_ge(S("f3_sil"), n + 1 + 2)
                    dve.wait_ge(S("f3_3_ps"), n + 1)
                    if e >= 2:
                        dve.wait_ge(S("f3_y_ps"), n - 1)
                    dve.tensor_tensor(hid3[e % 2], sil3[e % 2], bank(3 + e % 2), ALU.mult).then_inc(S("f3_hid"), 1)

                def add(e):
                    n = CH3 * g + e
                    dve.wait_ge(S("f3_y_ps"), n + 1)
                    for t in range(GT):
                        xt = tile_of(X, 4 * g + t)
                        if e:
                            dve.wait_ge(S("f3_x"), 4 * (E3 * g + e - 1) + t + 1)
                        dve.scalar_tensor_tensor(out=xt, in0=bank(5 + e % 2)[:, t * P:(t + 1) * P],
                                                 scalar=gate3[:, t * E3 + e:t * E3 + e + 1], in1=xt,
                                                 op0=ALU.mult, op1=ALU.add).then_inc(S("f3_x"), 1)
                    dve.wait_ge(S("f3_x"), 4 * (E3 * g + e) + 4)
                    dve.sem_inc(S("f3_y"), 1)

                hid(0)
                for e in range(1, CH3):
                    hid(e)
                    if e - 1 < E3:
                        add(e - 1)
                if one_more:
                    gates(g + 1, 1 - j)
                if two_more:
                    normalise(dve, s, g + 2, j)
                dve.wait_ge(S("f3_y_ps"), CH3 * g + CH3)
                xg = X[:, ds(4 * g, 4), :]
                dve.tensor_tensor(xg, xg, bank(5).rearrange("p (t n) -> p t n", t=GT), ALU.add)\
                    .then_inc(S("f3_y"), 1)
                dve.wait_ge(S("f3_y"), 9 * g + 9 + 2)
                dve.sem_inc(sem("f3", "res"), 1)

            groups2(dve, body)

        def setup_dve(dve):
            dve.wait_ge(S("ld_const"), 16)
            dve.memset(qs[:, 14:32], 0.0).then_inc(S("cst"), 1)
            dve.memset(qs[:, 13:14], ROUND).then_inc(S("cst"), 1)
            for dst, src in ((ident16[:, :], ident), (hsel16[64][:, :], W["hsel64"])):
                dve.tensor_copy(dst, src).then_inc(S("cst"), 1)
            dve.wait_ge(S("ld_x"), 16)
            with dve.Fori(0, N_TILES // 8) as i:
                for t in range(8):
                    dve.bn_stats(tile_of(stats, 8 * i + t), tile_of(X, 8 * i + t)).then_inc(S("bn0"), 1)
            dve.wait_ge(S("bn0"), N_TILES)
            dve.sem_inc(sem("a0", "stats"), 1)

        def rows_dve(dve):
            dve.wait_ge(S("ld_rows"), 48)
            dve.wait_ge(S("ld_once"), 16)
            for i in range(3):
                dve.tensor_scalar(bvmat[:, i, :], ident, 0.0, col("a%d_bv" % (i + 1)), ALU.mult, ALU.add)\
                    .then_inc(S("bvm"), 1)

        def rows_finish_dve(dve):
            for dst, src in ((hsel16[8][:, :], W["hsel8"]), (row0_16[:, :], W["row0"])):
                dve.tensor_copy(dst, src).then_inc(S("rw"), 1)
            dve.wait_ge(S("bvwo"), 1)
            dve.tensor_tensor(addrow[:, 0:3, :].rearrange("p i n -> p (i n)"), bank(1)[:, 0:3 * P],
                              rows_bc[:, 0:3 * P], ALU.add).then_inc(S("rw"), 1)
            dve.tensor_copy(addrow[:, 3, :], rows_bc[:, 3 * P:4 * P]).then_inc(S("rw"), 1)
            dve.tensor_copy(simw[:, :], bank(2)).then_inc(S("rw"), 1)
            dve.wait_ge(S("rw"), 5)
            dve.sem_inc(S("rows"), 1)
            dve.sem_inc(S("f2_simw"), 1)

        def rows_pe(pe):
            for k in ("a1", "a2", "a3", "f2"):
                pe.wait_ge(S("ld_" + k), 16)
            pe.wait_ge(S("bvm"), 3)
            pe.wait_ge(S("f0_go"), 1)
            for i in range(3):
                pe.matmul(bank(1)[:, i * P:(i + 1) * P], bvmat[:, i, :], W["a%d_wo" % (i + 1)], start=True, stop=True)
            for c in range(8):
                ins = pe.matmul(bank(2)[:, c * NK2:(c + 1) * NK2], W["f2_wqT"][0:64, c * P:(c + 1) * P],
                                W["f2_keysT"][0:64, c * NK2:(c + 1) * NK2], start=True, stop=True)
            ins.then_inc(S("bvwo"), 1)

        block = ctx.enter_context(nc.Block())

        @block.sync
        def _(sp):
            sp.dma_start(pack_sb["const"][:, :], dram["pack_const"]).then_inc(S("ld_const"), 16)
            sp.dma_start(X[:, :, :], dram["x"].rearrange("(t p) d -> p t d", p=P)).then_inc(S("ld_x"), 16)
            sp.dma_start(pack_sb["a0"][:, :], dram["pack_a0"]).then_inc(S("ld_a0"), 16)
            sp.dma_start(ctxd[:, :, :, :].rearrange("p b a k -> p (b a k)"), dram["ctxd"]).then_inc(S("ld_ctx"), 16)
            sp.dma_start(mask_u8[:, :], dram["mask"]).then_inc(S("ld_mask"), 16)
            sp.dma_start(kmrow_u8[:, :], dram["kmrow"]).then_inc(S("ld_mask"), 16)
            sp.dma_start(kmT_u8[:, :], dram["kmT"]).then_inc(S("ld_mask"), 16)
            sp.dma_start(rows_bc[:, :], dram["rows"].to_broadcast([P, 4 * P])).then_inc(S("ld_rows"), 16)
            sp.dma_start(gbias3[:, :], dram["gbias"].to_broadcast([P, E3])).then_inc(S("ld_rows"), 16)
            sp.dma_start(rscale[:, :], dram["rscale"].to_broadcast([P, 1])).then_inc(S("ld_rows"), 16)
            sp.dma_start(pack_sb["once"][:, :], dram["pack_once"]).then_inc(S("ld_once"), 16)
            for k in ("f0", "a1", "f1", "a2", "f2", "a3", "f3"):
                if k == "f3":
                    sp.wait_ge(sem("a1", "go"), 1)
                sp.dma_start(pack_sb[k][:, :], dram["pack_" + k]).then_inc(S("ld_" + k), 16)
            with sp.Fori(0, N_GROUPS) as g:
                sp.wait_ge(sem("f3", "res"), at("f3", "res") + g + 1 + 1)
                sp.dma_start(dram["out"].rearrange("(g t p) d -> p g t d", p=P, t=GT)[:, ds(g, 1)]
                             .rearrange("p a t d -> p (a t) d"), X[:, ds(4 * g, 4), :]).then_inc(S("stored"), 16)
            sp.wait_ge(S("stored"), 16 * N_GROUPS)

        @block.vector
        def _(dve):
            setup_dve(dve)
            for s, nxt in (("a0", "f0"), ("a1", "f1"), ("a2", "f2"), ("a3", "f3")):
                att_prep_dve(dve, atts[s])
                ln_finish_dve(dve, s)
                att_dve(dve, atts[s], nxt)
                ln_finish_dve(dve, nxt)
                {"f0": f0_dve, "f1": f1_dve, "f2": f2_dve, "f3": f3_dve}[nxt](dve)

        @block.scalar
        def _(act):
            act.wait_ge(S("cst"), 4)
            for s, nxt in (("a0", "f0"), ("a1", "f1"), ("a2", "f2"), ("a3", "f3")):
                att_prep_act(act, atts[s])
                ln_finish_act(act, s)
                att_act(act, atts[s])
                if s == "a0":
                    f0_weights_act(act)
                ln_finish_act(act, nxt)
                {"f0": f0_act, "f1": f1_act, "f2": f2_act, "f3": f3_act}[nxt](act)

        @block.tensor
        def _(pe):
            pe.wait_ge(S("cst"), 4)
            for s, nxt in (("a0", "f0"), ("a1", "f1"), ("a2", "f2"), ("a3", "f3")):
                att_prep_pe(pe, atts[s])
                att_pe(pe, atts[s])
                if s == "a0":
                    f0_weights_pe(pe)
                    pe.wait_ge(S("f0_wr"), 3)
                    rows_pe(pe)
                    pe.wait_ge(S("rows"), 1)
                {"f0": f0_pe, "f1": f1_pe, "f2": f2_pe, "f3": f3_pe}[nxt](pe)

        @block.gpsimd
        def _(pool):
            pool.wait_ge(S("ld_const"), 16)
            att_pool(pool, atts["a0"])
            f0_pool(pool)
            att_pool(pool, atts["a1"])
            att_pool(pool, atts["a2"])
            f2_pool(pool)
            att_pool(pool, atts["a3"])


def constants():
    p = np.arange(P)
    c = {"ident": np.eye(P)}
    for hd in (8, 64):
        H = D // hd
        c["kmask%d" % hd] = (p[:, None] // hd == np.arange(H)[None, :])
        c["hsel%d" % hd] = (p[:, None] == np.arange(H * SK)[None, :] // SK)
    e, hp = np.arange(64) // 32, (np.arange(64) % 16) // 8
    c["vmask8"] = (p[:, None] // SK == hp[None, :]) & ((np.arange(64) % 32 // 16)[None, :] == e[None, :])
    c["vmask64"] = p[:, None] // SK == p[None, :] // 64
    c["row0"] = np.broadcast_to(p[:, None] == 0, (P, P))
    freq = (1.0 / np.float32(10000.0) ** (np.arange(0, 8, 2, dtype=np.float32) / np.float32(8)))[(p % 8) // 2]
    for n, L in (("q", SQ), ("k", SK)):
        pos = np.float32(10.0) * (np.arange(L, dtype=np.float32) / np.float32(L))
        ang = pos[None, :] * freq[:, None].astype(np.float32)
        c["cos" + n] = np.cos(ang)
        c["sin" + n] = np.sin(ang) * np.where(p % 2 == 0, -1.0, 1.0)[:, None]
    return {k: np.asarray(v, np.float32) for k, v in c.items()}


def layout(i):
    i = {k: np.asarray(v) for k, v in i.items()}

    def rows_to_cols(w, n):
        return w.reshape(n, P, -1).transpose(1, 0, 2).reshape(P, -1)

    def swap(w):
        return w.reshape(w.shape[:-1] + (-1, 2))[..., ::-1].reshape(w.shape)

    t = constants()
    w = dict(t)
    w["a0_wq"], w["a0_wk"], w["a0_wv"] = i["L0_xattn_Wq"], i["L0_xattn_Wkv"][:, :D], i["L0_xattn_Wkv"][:, D:]
    w["a0_wo"] = i["L0_xattn_Wo"]
    w["f0_gate"], w["f0_up"] = rows_to_cols(i["L0_ffn_w_gate"], NC0), rows_to_cols(i["L0_ffn_w_up"], NC0)
    w["f0_down"] = i["L0_ffn_w_down"]
    w["a1_wq"], w["a1_wk"], w["a1_wv"], w["a1_wo"] = (i["L1_xattn_W" + k] for k in "qkvo")
    w["f1_sel"] = i["L1_ffn_expert_sel"].T
    w["f1_keys"] = i["L1_ffn_keys"].transpose(1, 0, 2).reshape(D, -1)
    w["f1_values"] = rows_to_cols(i["L1_ffn_values"].reshape(-1, D), 4)
    w["a2_wq"], w["a2_wk"], w["a2_wv"] = i["L2_xattn_Wq"], i["L2_xattn_Wkv"][:, :D], i["L2_xattn_Wkv"][:, D:]
    w["a2_wo"], w["a2_wqs"], w["a2_wks"] = i["L2_xattn_Wo"], swap(w["a2_wq"]), swap(w["a2_wk"])
    w["f2_wg"], w["f2_wu"], w["f2_wd"] = i["L2_ffn_Wg"], i["L2_ffn_Wu"], rows_to_cols(i["L2_ffn_Wd"], 4)
    half = lambda a: np.concatenate([a, a], 0)
    w["f2_wqT"] = half(i["L2_ffn_Wq"].reshape(D, 8, 64).transpose(2, 1, 0).reshape(64, -1))
    w["f2_keysT"] = half(i["L2_ffn_keys"].transpose(3, 2, 0, 1).reshape(64, -1))
    w["f2_downT"], w["f2_upE"] = i["L2_ffn_down_embed"].T, rows_to_cols(i["L2_ffn_up_embed"], 4)
    for k, n in zip("qkv", ("wq_w", "wk_w", "wv_w")):
        w["a3_w" + k] = i["L3_xattn_" + n].T
    w["a3_wo"] = i["L3_xattn_dense_w"].T
    w["f3_gate"] = i["L3_ffn_gate_w"].T
    for n in ("w1", "w3"):
        e = i["L3_ffn_" + n].transpose(2, 0, 1).reshape(D, -1)
        w["f3_" + n] = np.concatenate([e, i["L3_ffn_s" + n].T], 1)
    w["f3_w2"] = np.concatenate([i["L3_ffn_w2"].transpose(2, 0, 1).reshape(P, -1),
                                 rows_to_cols(np.ascontiguousarray(i["L3_ffn_sw2"].T), 2)], 1)
    kv = i["L2_xattn_bkv"]
    c = {"a1_bq": i["L1_xattn_bq"], "a1_bk": i["L1_xattn_bk"], "a1_bv": i["L1_xattn_bv"],
         "a2_bq": i["L2_xattn_bq"], "a2_bk": kv[:D], "a2_bv": kv[D:],
         "a2_bqs": swap(i["L2_xattn_bq"]), "a2_bks": swap(kv[:D]),
         "a3_bq": i["L3_xattn_wq_b"], "a3_bk": i["L3_xattn_wk_b"], "a3_bv": i["L3_xattn_wv_b"]}
    for j in range(4):
        c["f2_bg%d" % j] = i["L2_ffn_bg"][j * P:(j + 1) * P]
        c["f2_bu%d" % j] = i["L2_ffn_bu"][j * P:(j + 1) * P]
    cols = np.zeros((P, 24), np.float32)
    for n, name in enumerate(COLS):
        cols[:, n] = c[name]
    w["cols"] = cols
    out = {"pack_" + k: np.ascontiguousarray(np.concatenate([w[n] for n, _ in parts], 1))
           for k, parts in PACKS.items()}
    for k, parts in PACKS.items():
        assert out["pack_" + k].shape == (P, WIDTH[k]), k
    out["x"] = i["x"].reshape(B * SQ, D)
    cT = i["ctx_1024"].transpose(2, 0, 1)
    out["ctxd"] = np.ascontiguousarray(np.stack([cT, cT], 2).reshape(D, -1))
    m = i["mask_BxSxS2_bf1"].view(np.uint8)
    out["mask"] = np.ascontiguousarray(m.reshape(N_TILES, P, SK).transpose(1, 0, 2).reshape(P, -1))
    km = i["mask_BxS2_bf1"].view(np.uint8)
    out["kmrow"] = np.ascontiguousarray(km.reshape(1, -1))
    out["kmT"] = np.ascontiguousarray(np.concatenate([km.T, km.T], 0))
    out["rows"] = np.concatenate([i["L1_xattn_bo"], i["L2_xattn_bo"], i["L3_xattn_dense_b"], i["L2_ffn_bd"]])[None]
    out["gbias"] = i["L3_ffn_gate_bias"][None]
    out["rscale"] = i["L1_ffn_route_scale"][None]
    return out


def kernel(**inputs):
    import concourse.bacc as bacc
    from concourse.bass_utils import run_bass_kernel_spmd

    arrays = {k: np.ascontiguousarray(v) for k, v in layout(inputs).items()}
    nc = bacc.Bacc("TRN2", target_bir_lowering=False, num_devices=1)
    dram = {k: nc.dram_tensor("in_" + k, v.shape, mybir.dt.from_np(v.dtype), kind="ExternalInput").ap()
            for k, v in arrays.items()}
    dram["out"] = nc.dram_tensor("out", (B * SQ, D), F32, kind="ExternalOutput").ap()
    build(nc, dram)
    r = run_bass_kernel_spmd(nc, [{"in_" + k: v for k, v in arrays.items()}], core_ids=[0])
    return r.results[0]["out"].reshape(B, SQ, D)
```
